# Optimizing a Trainium2 kernel written in Bass

```python
import numpy as np
import jax
import jax.numpy as jnp

def _softmax(x, axis=-1):
    return jax.nn.softmax(x, axis=axis)
def _gelu(x):
    return jax.nn.gelu(x, approximate=True)
def _silu(x):
    return jax.nn.silu(x)
def _sigmoid(x):
    return jax.nn.sigmoid(x)
def _layernorm(x, axis=-1, eps=1e-5):
    m = jnp.mean(x, axis=axis, keepdims=True)
    v = jnp.var(x, axis=axis, keepdims=True)
    return (x - m) / jnp.sqrt(v + eps)
def _scatter_add(tgt, idx, src, axis=0):
    return tgt.at[idx].add(src)
def _segment_sum(src, seg, n):
    return jax.ops.segment_sum(src, seg, n)

kernel_name = 'mk_conv_preact_d4_conv_nchw32_7b1cd0'

def setup_inputs(seed: int = 0):
    np.random.seed(seed)
    _w = jnp.asarray
    def _rec_inputs():
        import jax
        import jax.numpy as jnp
        _gk = jax.random.key(seed)
        x = -0.000125 + 0.9999 * jax.random.normal(jax.random.fold_in(_gk, 1), (16, 32, 256, 256), jnp.float32)
        return x
    x = _rec_inputs()
    def _L0_conv_setup():
        import jax, jax.numpy as jnp
        import numpy as np
        B, IN_CH, OUT_CH, R = (16, 32, 32, 32)
        M1, M2 = (32, 32)
        H, W = (256, 256)
        key = jax.random.key(seed)
        k1, k2, k3, k4 = jax.random.split(key, 4)
        x = jax.random.normal(k1, (B, IN_CH, H, W), jnp.float32)
        coeff_real = jax.random.normal(k2, (R, M1, M2, IN_CH), jnp.float32)
        coeff_imag = jax.random.normal(k3, (R, M1, M2, IN_CH), jnp.float32)
        proj = jax.random.normal(k4, (OUT_CH, R), jnp.float32)
        return {'x': x, 'coeff_real': coeff_real, 'coeff_imag': coeff_imag, 'proj': proj}
    _L0_conv_all = _L0_conv_setup()
    _L0_conv_in = {k: v for k, v in _L0_conv_all.items() if k in ('coeff_real', 'coeff_imag', 'proj', )}
    del _L0_conv_all

    def _L1_conv_setup():
        import jax, jax.numpy as jnp
        import numpy as np
        LEVELS = 3

        def _wavelet_pyramid(x, levels=LEVELS):
            B, C, H, W = x.shape
            k1 = jnp.array([0.25, 0.5, 0.25], dtype=x.dtype)
            K = jnp.outer(k1, k1)[None, None]
            result = x
            for level in range(levels):
                sh, sw = (H // 2 ** level, W // 2 ** level)
                if min(sh, sw) <= 2:
                    break
                temp = result[:, :, :sh, :sw].reshape(B * C, 1, sh, sw)
                approx = jax.lax.conv_general_dilated(temp, K, window_strides=(1, 1), padding='SAME', dimension_numbers=('NCHW', 'OIHW', 'NCHW'))
                down = approx[:, :, ::2, ::2][:, :, :sh // 2, :sw // 2]
                result = result.at[:, :, :sh // 2, :sw // 2].set(down.reshape(B, C, sh // 2, sw // 2))
            return result
        key = jax.random.key(seed)
        x = jax.random.normal(key, (8, 32, 512, 512), dtype=jnp.float32)
        return {'x': x}
    _L1_conv_all = _L1_conv_setup()
    _L1_conv_in = {k: v for k, v in _L1_conv_all.items() if k in ()}
    del _L1_conv_all

    def _L2_conv_setup():
        import jax, jax.numpy as jnp
        import numpy as np
        B, IN_CH, OUT_CH, R = (16, 32, 32, 32)
        M1, M2 = (32, 32)
        H, W = (256, 256)
        key = jax.random.key(seed)
        k1, k2, k3, k4 = jax.random.split(key, 4)
        x = jax.random.normal(k1, (B, IN_CH, H, W), jnp.float32)
        coeff_real = jax.random.normal(k2, (R, M1, M2, IN_CH), jnp.float32)
        coeff_imag = jax.random.normal(k3, (R, M1, M2, IN_CH), jnp.float32)
        proj = jax.random.normal(k4, (OUT_CH, R), jnp.float32)
        return {'x': x, 'coeff_real': coeff_real, 'coeff_imag': coeff_imag, 'proj': proj}
    _L2_conv_all = _L2_conv_setup()
    _L2_conv_in = {k: v for k, v in _L2_conv_all.items() if k in ('coeff_real', 'coeff_imag', 'proj', )}
    del _L2_conv_all

    def _L3_conv_setup():
        import jax, jax.numpy as jnp
        import numpy as np
        B, C, H, W = (16, 32, 256, 256)

        def _dir_scan(xT, w_seq):

            def step(prev, xs):
                xr, wr = xs
                new = jnp.maximum(wr * prev + xr, 0.0)
                return (new, new)
            _, outs = jax.lax.scan(step, xT[0], (xT[1:], w_seq))
            return jnp.concatenate([xT[:1], outs], axis=0)

        def _forward(inp, weights, conv_w, conv_b):
            w_up, w_down, w_left, w_right = jax.nn.sigmoid(weights)
            xH = jnp.moveaxis(inp, 2, 0)
            uc = jnp.moveaxis(_dir_scan(xH, w_up[:-1]), 0, 2)
            dc = jnp.moveaxis(_dir_scan(xH[::-1], w_down[::-1][:-1])[::-1], 0, 2)
            xW = jnp.moveaxis(inp, 3, 0)
            lc = jnp.moveaxis(_dir_scan(xW, w_left.T[:-1]), 0, 3)
            rc = jnp.moveaxis(_dir_scan(xW[::-1], w_right.T[::-1][:-1])[::-1], 0, 3)
            ctx = jnp.concatenate([lc, rc, uc, dc], axis=1)
            out = jnp.einsum('bkhw,ck->bchw', ctx, conv_w) + conv_b[None, :, None, None]
            return jnp.maximum(out, 0.0)
        key = jax.random.key(seed)
        k1, k2, k3, k4 = jax.random.split(key, 4)
        inp = jax.random.normal(k1, (B, C, H, W), dtype=jnp.float32)
        weights = jax.random.normal(k2, (4, H, W), dtype=jnp.float32) * 0.1
        conv_w = jax.random.normal(k3, (C, 4 * C), dtype=jnp.float32) / np.sqrt(4 * C)
        conv_b = jax.random.normal(k4, (C,), dtype=jnp.float32) * 0.01
        return {'inp': inp, 'weights': weights, 'conv_w': conv_w, 'conv_b': conv_b}
    _L3_conv_all = _L3_conv_setup()
    _L3_conv_in = {k: v for k, v in _L3_conv_all.items() if k in ('weights', 'conv_w', 'conv_b', )}
    del _L3_conv_all

    return {
        "x": x,
        "L0_conv_coeff_real": _L0_conv_in["coeff_real"],
        "L0_conv_coeff_imag": _L0_conv_in["coeff_imag"],
        "L0_conv_proj": _L0_conv_in["proj"],
        "L2_conv_coeff_real": _L2_conv_in["coeff_real"],
        "L2_conv_coeff_imag": _L2_conv_in["coeff_imag"],
        "L2_conv_proj": _L2_conv_in["proj"],
        "L3_conv_weights": _L3_conv_in["weights"],
        "L3_conv_conv_w": _L3_conv_in["conv_w"],
        "L3_conv_conv_b": _L3_conv_in["conv_b"],
    }

def reference(x, L0_conv_coeff_real, L0_conv_coeff_imag, L0_conv_proj, L2_conv_coeff_real, L2_conv_coeff_imag, L2_conv_proj, L3_conv_weights, L3_conv_conv_w, L3_conv_conv_b):
    import jax
    import jax.numpy as jnp
    def _L0_conv_ref(x, coeff_real, coeff_imag, proj):
        import jax, jax.numpy as jnp
        import numpy as np
        B, IN_CH, OUT_CH, R = (16, 32, 32, 32)
        M1, M2 = (32, 32)
        H, W = (256, 256)
        x_ft = jnp.fft.rfftn(x, axes=(-2, -1))
        coeff = (coeff_real + 1j * coeff_imag).astype(jnp.complex64)
        Wt = jnp.einsum('or,rabi->oabi', proj.astype(jnp.complex64), coeff)
        Hf, Wf = (x_ft.shape[-2], x_ft.shape[-1])
        m1 = min(M1, Hf)
        m2 = min(M2, Wf)
        sub = jnp.einsum('bcij,ocij->boij', x_ft[..., :m1, :m2], Wt[:, :, :m1, :m2])
        out_ft = jnp.zeros((x.shape[0], OUT_CH, Hf, Wf), jnp.complex64)
        out_ft = out_ft.at[..., :m1, :m2].set(sub.astype(jnp.complex64))
        return jnp.fft.irfftn(out_ft, s=(x.shape[-2], x.shape[-1]), axes=(-2, -1))

    def _L1_conv_ref(x):
        import jax, jax.numpy as jnp
        import numpy as np
        LEVELS = 3

        def _wavelet_pyramid(x, levels=LEVELS):
            B, C, H, W = x.shape
            k1 = jnp.array([0.25, 0.5, 0.25], dtype=x.dtype)
            K = jnp.outer(k1, k1)[None, None]
            result = x
            for level in range(levels):
                sh, sw = (H // 2 ** level, W // 2 ** level)
                if min(sh, sw) <= 2:
                    break
                temp = result[:, :, :sh, :sw].reshape(B * C, 1, sh, sw)
                approx = jax.lax.conv_general_dilated(temp, K, window_strides=(1, 1), padding='SAME', dimension_numbers=('NCHW', 'OIHW', 'NCHW'))
                down = approx[:, :, ::2, ::2][:, :, :sh // 2, :sw // 2]
                result = result.at[:, :, :sh // 2, :sw // 2].set(down.reshape(B, C, sh // 2, sw // 2))
            return result
        return _wavelet_pyramid(x, LEVELS)

    def _L2_conv_ref(x, coeff_real, coeff_imag, proj):
        import jax, jax.numpy as jnp
        import numpy as np
        B, IN_CH, OUT_CH, R = (16, 32, 32, 32)
        M1, M2 = (32, 32)
        H, W = (256, 256)
        x_ft = jnp.fft.rfftn(x, axes=(-2, -1))
        coeff = (coeff_real + 1j * coeff_imag).astype(jnp.complex64)
        Wt = jnp.einsum('or,rabi->oabi', proj.astype(jnp.complex64), coeff)
        Hf, Wf = (x_ft.shape[-2], x_ft.shape[-1])
        m1 = min(M1, Hf)
        m2 = min(M2, Wf)
        sub = jnp.einsum('bcij,ocij->boij', x_ft[..., :m1, :m2], Wt[:, :, :m1, :m2])
        out_ft = jnp.zeros((x.shape[0], OUT_CH, Hf, Wf), jnp.complex64)
        out_ft = out_ft.at[..., :m1, :m2].set(sub.astype(jnp.complex64))
        return jnp.fft.irfftn(out_ft, s=(x.shape[-2], x.shape[-1]), axes=(-2, -1))

    def _L3_conv_ref(inp, weights, conv_w, conv_b):
        import jax, jax.numpy as jnp
        import numpy as np
        B, C, H, W = (16, 32, 256, 256)

        def _dir_scan(xT, w_seq):

            def step(prev, xs):
                xr, wr = xs
                new = jnp.maximum(wr * prev + xr, 0.0)
                return (new, new)
            _, outs = jax.lax.scan(step, xT[0], (xT[1:], w_seq))
            return jnp.concatenate([xT[:1], outs], axis=0)

        def _forward(inp, weights, conv_w, conv_b):
            w_up, w_down, w_left, w_right = jax.nn.sigmoid(weights)
            xH = jnp.moveaxis(inp, 2, 0)
            uc = jnp.moveaxis(_dir_scan(xH, w_up[:-1]), 0, 2)
            dc = jnp.moveaxis(_dir_scan(xH[::-1], w_down[::-1][:-1])[::-1], 0, 2)
            xW = jnp.moveaxis(inp, 3, 0)
            lc = jnp.moveaxis(_dir_scan(xW, w_left.T[:-1]), 0, 3)
            rc = jnp.moveaxis(_dir_scan(xW[::-1], w_right.T[::-1][:-1])[::-1], 0, 3)
            ctx = jnp.concatenate([lc, rc, uc, dc], axis=1)
            out = jnp.einsum('bkhw,ck->bchw', ctx, conv_w) + conv_b[None, :, None, None]
            return jnp.maximum(out, 0.0)
        return _forward(inp, weights, conv_w, conv_b)

    def _gn(v, G=16, eps=1e-5):
        B_, C_, H_, W_ = v.shape
        g = v.reshape(B_, G, C_ // G, H_, W_)
        m = jnp.mean(g, axis=(2, 3, 4), keepdims=True)
        s = jnp.var(g, axis=(2, 3, 4), keepdims=True)
        return ((g - m) / jnp.sqrt(s + eps)).reshape(v.shape)

    def _ln_c(v, eps=1e-6):
        m = jnp.mean(v, axis=1, keepdims=True)
        s = jnp.var(v, axis=1, keepdims=True)
        return (v - m) / jnp.sqrt(s + eps)

    def _ln_t(v, eps=1e-5):
        m = jnp.mean(v, axis=-1, keepdims=True)
        s = jnp.var(v, axis=-1, keepdims=True)
        return (v - m) / jnp.sqrt(s + eps)

    def _to_tokens(v):
        B_, C_, H_, W_ = v.shape
        return v.reshape(B_, C_, H_ * W_).transpose(0, 2, 1)
    def _from_tokens(t, like):
        B_, C_, H_, W_ = like.shape
        return t.transpose(0, 2, 1).reshape(B_, C_, H_, W_)

    x = x + _L0_conv_ref(_gn(x), L0_conv_coeff_real, L0_conv_coeff_imag, L0_conv_proj)
    x = x + _L1_conv_ref(_gn(x))
    x = x + _L2_conv_ref(_gn(x), L2_conv_coeff_real, L2_conv_coeff_imag, L2_conv_proj)
    x = x + _L3_conv_ref(_gn(x), L3_conv_weights, L3_conv_conv_w, L3_conv_conv_b)
    return x


_drawn_inputs = setup_inputs


def setup_inputs(seed=0):
    import zlib

    import numpy as np

    out = dict(_drawn_inputs(seed))
    spreads = {}
    factors = {'L3_conv_weights': 32.019, 'L3_conv_conv_w': 3.482, 'L3_conv_conv_b': 200.0}
    for name, (base, spread) in spreads.items():
        noise = np.random.default_rng([zlib.crc32(name.encode()), seed]).standard_normal(out[name].shape)
        drawn = base * np.exp(spread * noise) if base else spread * noise
        out[name] = jnp.asarray(drawn.astype(out[name].dtype))
    for name, factor in factors.items():
        out[name] = (out[name] * factor).astype(out[name].dtype)
    return out
```

```python
from contextlib import ExitStack

import numpy as np
import concourse.bass as bass
from concourse import mybir

F32 = mybir.dt.float32
ALU = mybir.AluOpType
ACT = mybir.ActivationFunctionType
AX_X = mybir.AxisListType.X

B, C, H, W = 16, 32, 256, 256
P = 128
HB = H // P
M = 32
HW = H * W
GROUP = 2
CU = 8
KU = C // CU
MQ = M // 4
XF = MQ * 3 * M
EPS = 1e-5
GB = B * C // P
RR = 4
RF = 2

_widths = [("FR", HB * 2 * M), ("FI", HB * 2 * M), ("EW", W), ("EH", H), ("EN", H),
           ("D1", HB * 128), ("D2", HB * 64), ("D3", HB * 32), ("GM", P), ("ID", P)]
COL = {}
_at = 0
for _n, _w in _widths:
    COL[_n] = (_at, _at + _w)
    _at += _w
NCOL = _at


def constant_table():
    t = np.zeros((P, NCOL), np.float64)
    ang = 2 * np.pi * ((np.arange(H)[:, None] * np.arange(M)[None, :]) % H) / H
    c, s = np.cos(ang), np.sin(ang)

    def rows(a):
        return a.reshape(HB, P, -1).transpose(1, 0, 2).reshape(P, -1)

    def put(name, a):
        lo, hi = COL[name]
        t[:a.shape[0], lo:lo + a.shape[1]] = a

    put("FR", rows(np.concatenate([c, -s], 1)))
    put("FI", rows(np.concatenate([s, c], 1)))
    wj = np.where(np.arange(M) == 0, 1.0, 2.0)[:, None] / HW
    put("EW", np.concatenate([c.T * wj, -s.T * wj], 0))
    eh = np.concatenate([c.T, -s.T], 0)
    put("EH", eh)
    put("EN", -eh)

    def down(n):
        a = np.zeros((n // 2, n))
        for i in range(n // 2):
            for d, v in ((-1, 0.25), (0, 0.5), (1, 0.25)):
                if 0 <= 2 * i + d < n:
                    a[i, 2 * i + d] = v
        return a
    a1 = down(H)
    a2 = down(H // 2) @ a1
    a3 = down(H // 4) @ a2
    put("D1", rows(a1.T / 4))
    put("D2", rows(a2.T / 16))
    put("D3", rows(a3.T / 64))
    grp = (np.arange(P) % C) // GROUP
    put("GM", (grp[:, None] == grp[None, :]).astype(np.float64))
    put("ID", np.eye(P))
    return t.astype(np.float32)


class Prog:

    def __init__(self, nc, ctx):
        self.nc, self.ctx = nc, ctx
        self.tab = ctx.enter_context(nc.sbuf_tensor("tab", [P, NCOL], F32))
        self.ones = ctx.enter_context(nc.sbuf_tensor("ones", [P, 1], F32))
        self.ps = ctx.enter_context(nc.psum_tensor("ps", [P, 8, 512], F32))

        self.consts_in = self.sem("consts_in")
        self.passed = {}

    def hold(self, eng, sem, value):
        if eng not in self.passed:
            self.passed[eng] = self.sem(f"passed{len(self.passed)}")
        eng.wait_ge(sem, value)
        eng.sem_inc(self.passed[eng], 1)

    def sem(self, name):
        return self.ctx.enter_context(self.nc.semaphore(name))

    def t(self, name, rows=P):
        lo, hi = COL[name]
        return self.tab[0:rows, lo:hi]


def phase_gates(pg, consts, weights, gate_rows, gate_cols):
    nc = pg.nc
    with ExitStack() as mem:
        raw = mem.enter_context(nc.sbuf_tensor("g_raw", [P, 4, HB, W], F32))
        sg = mem.enter_context(nc.sbuf_tensor("g_sig", [P, 4, HB, W], F32))
        zero = mem.enter_context(nc.sbuf_tensor("g_zero", [1, W], F32))
        raw_in = pg.sem("g_raw_in")
        zeroed = pg.sem("g_zeroed")
        sig_done = pg.sem("g_sig_done")
        gates_out = pg.sem("g_gates_out")
        with nc.Block(name="gates") as block:
            @block.sync
            def _(sp):
                sp.dma_start(pg.tab[:, :], consts).then_inc(pg.consts_in, 16)
                for d in range(4):
                    sp.dma_start(raw[:, d], weights[d].rearrange("(n p) w -> p n w", p=P)).then_inc(raw_in, 16)
                pg.hold(sp, zeroed, 1)
                sp.dma_start(gate_rows[0, 0:1, :], zero[:, :]).then_inc(gates_out, 16)
                sp.dma_start(gate_rows[1, H:H + 1, :], zero[:, :]).then_inc(gates_out, 16)
                pg.hold(sp, sig_done, 1)
                sp.dma_start(gate_rows[0, 1:H + 1, :].rearrange("(n p) w -> p n w", p=P), sg[:, 0]).then_inc(gates_out, 16)
                sp.dma_start(gate_rows[1, 0:H, :].rearrange("(n p) w -> p n w", p=P), sg[:, 1]).then_inc(gates_out, 16)
                for d in range(2):
                    sp.dma_start(gate_cols[d].rearrange("(n p) w -> p n w", p=P), sg[:, 2 + d]).then_inc(gates_out, 16)
                pg.hold(sp, gates_out, 6 * 16)
                pg.hold(sp, pg.consts_in, 16)

            @block.vector
            def _(dve):
                nc.vector.memset(pg.ones[:, :], 1.0)
                nc.vector.memset(sg[:, 2, :, 0:1], 0.0)
                nc.vector.memset(sg[:, 3, :, W - 1:W], 0.0)
                nc.vector.memset(zero[:, :], 0.0).then_inc(zeroed, 1)

            @block.scalar
            def _(act):
                act.wait_ge(raw_in, 4 * 16)
                nc.scalar.activation(sg[:, 0:2], raw[:, 0:2], ACT.Sigmoid)
                nc.scalar.activation(sg[:, 2, :, 1:W], raw[:, 2, :, 0:W - 1], ACT.Sigmoid)
                nc.scalar.activation(sg[:, 3, :, 0:W - 1], raw[:, 3, :, 1:W], ACT.Sigmoid).then_inc(sig_done, 1)


class Forward:
    BANKS = 2

    def __init__(self, pg, mem, name, first_bank):
        nc = pg.nc
        self.pg, self.bank0 = pg, first_bank
        self.a1 = mem.enter_context(nc.sbuf_tensor(name + "_a1", [P, 2, 2 * M, C], F32))
        self.xf = mem.enter_context(nc.sbuf_tensor(name + "_xf", [P, MQ, 3, M], F32))
        self.sq = mem.enter_context(nc.sbuf_tensor(name + "_sq", [P, C // GROUP], F32))
        self.junk = [mem.enter_context(nc.sbuf_tensor(f"{name}_junk{i}", [P, HB, GROUP * W], F32)) for i in range(2)]
        self.sqrow = mem.enter_context(nc.sbuf_tensor(name + "_sqrow", [1, C // GROUP, GROUP], F32))
        self.cols_done = pg.sem(name + "_cols_done")
        self.cols_out = pg.sem(name + "_cols_out")
        self.sq_done = pg.sem(name + "_sq_done")
        self.modes_done = pg.sem(name + "_modes_done")
        self.modes_out = pg.sem(name + "_modes_out")
        self.xf_free = pg.sem(name + "_xf_free")
        self.stored = pg.sem(name + "_modes_stored")

    def sq_count(self, s, k):
        return s * (C // GROUP) + ((k + 1) * (CU // GROUP) + 2)

    def start(self, act):
        act.sem_inc(self.sq_done, 2)
        act.sem_inc(self.cols_out, self.BANKS)

    def bank(self, i):
        return self.pg.ps[:, self.bank0 + i]

    def pe_unit(self, pe, s, k, x):
        nc = self.pg.nc
        fr = self.pg.t("FR").rearrange("p (n m) -> p n m", n=HB)
        for wb in range(2):
            pe.wait_ge(self.cols_out, s * (2 * KU) + (2 * k + wb + 1))
            bank = self.bank((2 * k + wb) % self.BANKS).rearrange("p (c m) -> p c m", c=CU)
            for c in range(CU):
                for hb in range(HB):
                    mm = nc.tensor.matmul(bank[:, c, :], x[:, hb, c, wb * P:(wb + 1) * P], fr[:, hb, :],
                                          start=(hb == 0), stop=(hb == HB - 1))
            mm.then_inc(self.cols_done, 1)

    def pe_sample(self, pe, s):
        nc = self.pg.nc
        fr = self.pg.t("FR").rearrange("p (n m) -> p n m", n=HB)
        fi = self.pg.t("FI").rearrange("p (n m) -> p n m", n=HB)
        pe.wait_ge(self.cols_out, s * (2 * KU) + (2 * KU + self.BANKS))
        pe.wait_ge(self.sq_done, self.sq_count(s, KU - 1))
        pe.wait_ge(self.modes_out, s + 1)
        bank = self.bank(2).rearrange("p (q m) -> p q m", q=MQ)
        for iq in range(MQ):
            n = 0
            for wb in range(2):
                for ri, f in ((0, fr), (1, fi)):
                    i0 = ri * M + 4 * iq
                    nc.tensor.matmul(bank[:, iq, :], self.a1[:, wb, i0:i0 + 4, :], f[:, wb, :],
                                     start=(n == 0), stop=(n == 3))
                    n += 1
        sq_ps = self.bank(3)[0:1, 0:C // GROUP]
        nc.tensor.matmul(sq_ps, self.pg.ones[:, :], self.sq[:, :], start=True, stop=True).then_inc(self.modes_done, 1)

    def act_cols(self, act, s, k):
        nc = self.pg.nc
        for wb in range(2):
            act.wait_ge(self.cols_done, s * (2 * KU) + (2 * k + wb + 1))
            if k == 0 and wb == 0:
                act.wait_ge(self.modes_done, s + 1)
            bank = self.bank((2 * k + wb) % self.BANKS).rearrange("p (c m) -> p c m", c=CU)
            dst = self.a1[:, wb, :, k * CU:(k + 1) * CU].rearrange("p m c -> p c m")
            nc.scalar.copy(dst, bank).then_inc(self.cols_out, 1)

    def act_squares(self, act, s, k, x):
        nc = self.pg.nc
        if k == 0:
            act.wait_ge(self.modes_done, s + 1)
        for g in range(CU // GROUP):
            src = x[:, :, g * GROUP:(g + 1) * GROUP, :].rearrange("p n c w -> p n (c w)")
            at = k * (CU // GROUP) + g
            act.wait_ge(self.sq_done, s * (C // GROUP) + (at + 1))
            nc.scalar.activation(self.junk[at % 2][:, :, :], src, ACT.Square, accum_out=self.sq[:, at:at + 1]
                                 ).then_inc(self.sq_done, 1)

    def dve_sample(self, dve, s):
        nc = self.pg.nc
        dve.wait_ge(self.modes_done, s + 2)
        dve.wait_ge(self.xf_free, s + 1)
        bank = self.bank(2).rearrange("p (q r m) -> p q r m", q=MQ, r=2)
        nc.vector.tensor_copy(self.xf[:, :, 1:3, :], bank)
        nc.vector.tensor_scalar(self.xf[:, :, 0, :], bank[:, :, 1, :], -1.0, None, ALU.mult)
        sq_ps = self.bank(3)[0:1, 0:C // GROUP]
        nc.vector.tensor_copy(self.sqrow[:, :, :], sq_ps.unsqueeze(2).to_broadcast([1, C // GROUP, GROUP])
                              ).then_inc(self.modes_out, 1)

    def pool_sample(self, pool, s, modes, sumsq):
        pool.wait_ge(self.modes_out, s + 2)
        pool.dma_start(modes[bass.ds(s, 1)].rearrange("b p f -> p (b f)"),
                       self.xf[:, :, :, :].rearrange("p q r m -> p (q r m)")).then_inc(self.stored, 16)
        pool.dma_start(sumsq[bass.ds(s, 1), :], self.sqrow[:, :, :].rearrange("o g e -> o (g e)")
                       ).then_inc(self.stored, 16)
        pool.wait_ge(self.stored, s * 32 + 32)
        pool.sem_inc(self.xf_free, 1)


def unit_rows(img, s, k, hb):
    return img[bass.ds(s, 1), k * CU:(k + 1) * CU, hb * P:(hb + 1) * P, :].rearrange("b c p w -> p (b c) w")


def phase_forward(pg, x, modes, sumsq):
    nc = pg.nc
    with ExitStack() as mem:
        slot = [mem.enter_context(nc.sbuf_tensor(f"a_x{k}", [P, HB, CU, W], F32)) for k in range(KU)]
        loaded = [pg.sem(f"a_loaded{k}") for k in range(KU)]
        fw = Forward(pg, mem, "a", 0)
        with nc.Block(name="forward") as block:
            @block.sync
            def _(sp):
                def load(s, k):
                    for hb in range(HB):
                        sp.dma_start(slot[k][:, hb], unit_rows(x, s, k, hb)).then_inc(loaded[k], 16)
                for k in range(KU):
                    load(0, k)
                with sp.Fori(1, B) as s:
                    for k in range(KU):
                        pg.hold(sp, fw.cols_done, s * (2 * KU) + (2 * k + 2 - 2 * KU))
                        pg.hold(sp, fw.sq_done, s * (C // GROUP) + ((k + 1 - KU) * (CU // GROUP) + 2))
                        load(s, k)

            @block.tensor
            def _(pe):
                pe.sem_inc(fw.modes_done, 1)
                with pe.Fori(0, B) as s:
                    for k in range(KU):
                        pe.wait_ge(loaded[k], s * 32 + 32)
                        fw.pe_unit(pe, s, k, slot[k])
                    fw.pe_sample(pe, s)

            @block.scalar
            def _(act):
                fw.start(act)
                with act.Fori(0, B) as s:
                    for k in range(KU):
                        act.wait_ge(loaded[k], s * 32 + 32)
                        fw.act_squares(act, s, k, slot[k])
                        fw.act_cols(act, s, k)

            @block.vector
            def _(dve):
                dve.sem_inc(fw.modes_out, 1)
                with dve.Fori(0, B) as s:
                    fw.dve_sample(dve, s)

            @block.gpsimd
            def _(pool):
                pool.sem_inc(fw.xf_free, 1)
                with pool.Fori(0, B) as s:
                    fw.pool_sample(pool, s, modes, sumsq)
                pool.wait_ge(fw.stored, B * 32)


def phase_mix(pg, name, modes, sumsq, coef, projT, sx, stats):
    nc = pg.nc
    NF = HW * GROUP
    with ExitStack() as mem:
        def sb(n, shape):
            return mem.enter_context(nc.sbuf_tensor(name + n, shape, F32))
        X = sb("_x", [P, B, MQ, 3, M])
        S = sb("_s", [P, B, MQ, 3, M])
        cf = [sb(f"_cf{i}", [M, 4 * C, M]) for i in range(2)]
        BD = [sb(f"_bd{i}", [P, 2, M, P]) for i in range(2)]
        pj = sb("_pj", [M, C])
        v = sb("_v", [P, 16, B])
        st = sb("_st", [P, B, 4])
        tot, mean, var, rs, t0, t1, t2, qs, qc, cs, cc, em, m1, v1, t3, t4 = [v[:, n, :] for n in range(16)]

        x_in, sq_in, pj_in = pg.sem(name + "_x_in"), pg.sem(name + "_sq_in"), pg.sem(name + "_pj_in")
        cf_in = [pg.sem(f"{name}_cf_in{i}") for i in range(2)]
        dc_done = pg.sem(name + "_dc_done")
        chain = pg.sem(name + "_dve_chain")
        var_ready = pg.sem(name + "_var_ready")
        sums_ready = pg.sem(name + "_sums_ready")
        root_done = pg.sem(name + "_root_done")
        normed = pg.sem(name + "_normed")
        zeroed = pg.sem(name + "_zeroed")
        w_done = pg.sem(name + "_w_done")
        w_out_act, w_out_dve = pg.sem(name + "_w_out_act"), pg.sem(name + "_w_out_dve")
        mix_done = pg.sem(name + "_mix_done")
        mix_out = pg.sem(name + "_mix_out")
        sums_done = pg.sem(name + "_sums_done")
        s_final = pg.sem(name + "_s_final")
        tr_done = pg.sem(name + "_tr_done")
        tr_out_act, tr_out_dve = pg.sem(name + "_tr_out_act"), pg.sem(name + "_tr_out_dve")
        sx_out = pg.sem(name + "_sx_out")
        st_out = pg.sem(name + "_st_out")
        ident = pg.t("ID")
        gm = pg.t("GM")
        chunks = [(iq, ri) for iq in range(MQ) for ri in range(2)]
        SX = [BD[i][0:2 * M, 0, 0:16, :].rearrange("p a b -> p (a b)").rearrange(
            "p (c r m) -> p c r m", c=C, r=2) for i in range(2)]
        prod = BD[0][:, :, :, :].rearrange("p r m c -> p (r m c)").rearrange(
            "p (b q r m) -> p b q r m", b=B, q=MQ, r=2)

        with nc.Block(name=name) as block:
            @block.sync
            def _(sp):
                sp.dma_start(pj[:, :], projT).then_inc(pj_in, 16)
                for i4 in range(4):
                    with nc.allow_non_contiguous_dma(reason="512 words"):
                        sp.dma_start(tot[i4 * C:(i4 + 1) * C, :], sumsq.rearrange("b c -> c b")).then_inc(sq_in, 16)
                sp.dma_start(X[:].rearrange("p b q r m -> p b (q r m)"),
                             modes.rearrange("b p f -> p b f")).then_inc(x_in, 16)
                for n, (iq, ri) in enumerate(chunks):
                    if n >= 2:
                        pg.hold(sp, w_done, 2 * (n - 1))
                    sp.dma_start(cf[n % 2][:, :, :].rearrange("p m j -> p (m j)"), coef[ri][iq]).then_inc(cf_in[n % 2], 16)
                pg.hold(sp, s_final, 1)
                with nc.allow_non_contiguous_dma(reason="a few words per channel"):
                    sp.dma_start(stats.rearrange("b k c -> c (b k)"),
                                 st[0:C].rearrange("p b k -> p (b k)")).then_inc(st_out, 16)
                for b in range(B):
                    pg.hold(sp, tr_out_act, 2 * (b + 1))
                    pg.hold(sp, tr_out_dve, 2 * (b + 1))
                    sp.dma_start(sx[b], SX[b % 2].rearrange("p c r m -> p (c r m)")).then_inc(sx_out, 16)
                    pg.hold(sp, sx_out, 16 * (b + 1))
                pg.hold(sp, st_out, 16)

            @block.tensor
            def _(pe):
                pe.wait_ge(x_in, 16)
                dc = pg.ps[:, 7, 0:B]
                nc.tensor.matmul(dc, gm[0:C, :], X[0:C, :, 0, 1, 0], start=True, stop=True).then_inc(dc_done, 1)
                pe.wait_ge(pj_in, 16)

                def weights(n):
                    pe.wait_ge(cf_in[n % 2], 16 * (n // 2 + 1))
                    for jh in range(2):
                        if n >= 2:
                            pe.wait_ge(w_out_act, 2 * (n - 2) + jh + 1)
                            pe.wait_ge(w_out_dve, 2 * (n - 2) + jh + 1)
                        bank = pg.ps[:, 2 * (n % 2) + jh].rearrange("p (j o) -> p j o", j=M // 2)
                        for j in range(M // 2):
                            mm = nc.tensor.matmul(bank[:, j, :], cf[n % 2][:, :, jh * 16 + j], pj[:, :],
                                                  start=True, stop=True)
                        mm.then_inc(w_done, 1)

                def mix(iq):
                    pe.wait_ge(w_out_act, 4 * (iq + 1))
                    pe.wait_ge(w_out_dve, 4 * (iq + 1))
                    if iq == 0:
                        pe.wait_ge(normed, 1)
                    for jh in range(2):
                        if iq >= 1:
                            pe.wait_ge(mix_out, 2 * (iq - 1) + jh + 1)
                        bank = pg.ps[:, 4 + jh].rearrange("p (j n) -> p j n", j=M // 2)
                        for j in range(M // 2):
                            jj = jh * 16 + j
                            for ri in range(2):
                                rhs = X[:, :, iq, 1 - ri:3 - ri, jj].rearrange("p b r -> p r b")
                                mm = nc.tensor.matmul(bank[:, j, :], BD[iq % 2][:, ri, jj, :], rhs,
                                                      start=(ri == 0), stop=(ri == 1))
                        mm.then_inc(mix_done, 1)
                weights(0)
                weights(1)
                for iq in range(MQ):
                    if iq + 1 < MQ:
                        weights(2 * iq + 2)
                        weights(2 * iq + 3)
                    mix(iq)
                pe.wait_ge(sums_ready, 1)
                for n, a in enumerate((qs, cs)):
                    mm = nc.tensor.matmul(pg.ps[:, 7, (n + 1) * B:(n + 2) * B], gm, a, start=True, stop=True)
                mm = nc.tensor.matmul(pg.ps[:, 7, 3 * B:4 * B], gm[0:C, :], S[0:C, :, 0, 0, 0], start=True, stop=True)
                mm.then_inc(sums_done, 1)
                pe.wait_ge(s_final, 1)
                for b in range(B):
                    for half in range(2):
                        if b >= 1:
                            pe.wait_ge(tr_out_act, 2 * (b - 1) + half + 1)
                            pe.wait_ge(tr_out_dve, 2 * (b - 1) + half + 1)
                        for r in range(2):
                            for q in range(4):
                                iq = half * 4 + q
                                mm = nc.tensor.transpose(
                                    pg.ps[0:2 * M, 2 * half + r, q * P:(q + 1) * P],
                                    S[:, b, iq, r:r + 2, :].rearrange("p r m -> p (r m)"), ident)
                        mm.then_inc(tr_done, 1)

            def evacuate_weights(eng, copy, out_sem, quads, with_mix):
                for n, (iq, ri) in enumerate(chunks):
                    for jh in range(2):
                        eng.wait_ge(w_done, 2 * n + jh + 1)
                        if n == 0 and jh == 0:
                            eng.wait_ge(zeroed, 1)
                        if iq >= 2 and ri == 0 and jh == 0:
                            eng.wait_ge(mix_done, 2 * (iq - 1))
                        bank = pg.ps[:, 2 * (n % 2) + jh].rearrange("p (j o) -> p j o", j=M // 2)
                        for i4 in quads:
                            r0 = i4 * C
                            op = copy(BD[iq % 2][r0:r0 + C, ri, jh * 16:(jh + 1) * 16, r0:r0 + C],
                                      bank[r0:r0 + C])
                        op.then_inc(out_sem, 1)
                    if with_mix and iq >= 1 and ri == 1:
                        evacuate_mix(eng, iq - 1)
                if with_mix:
                    evacuate_mix(eng, MQ - 1)

            def evacuate_mix(dve, iq):
                for jh in range(2):
                    dve.wait_ge(mix_done, 2 * iq + jh + 1)
                    bank = pg.ps[:, 4 + jh].rearrange("p (j r b) -> p r b j", j=M // 2, r=2)
                    js = slice(jh * 16, (jh + 1) * 16)
                    for r in range(2):
                        nc.vector.tensor_copy(S[:, :, iq, r, js], bank[:, r])
                    nc.vector.tensor_scalar(S[:, :, iq, 2, js], bank[:, 0], -1.0, None, ALU.mult).then_inc(mix_out, 1)

            @block.scalar
            def _(act):
                act.wait_ge(var_ready, 1)
                nc.scalar.activation(t1, var, ACT.Sqrt).then_inc(root_done, 1)
                evacuate_weights(act, nc.scalar.copy, w_out_act, (0, 1), False)
                act.wait_ge(var_ready, 2)
                nc.scalar.activation(t1, v1, ACT.Sqrt).then_inc(root_done, 1)
                for b in range(B):
                    for half in range(2):
                        act.wait_ge(tr_done, 2 * b + half + 1)
                        if half == 0 and b >= 2:
                            act.wait_ge(sx_out, 16 * (b - 1))
                        src = pg.ps[0:2 * M, 2 * half].rearrange("p (i o) -> p i o", i=16)
                        dst = SX[b % 2][:, :, 0, half * 16:(half + 1) * 16].rearrange("p c i -> p i c")
                        nc.scalar.copy(dst, src).then_inc(tr_out_act, 1)

            @block.vector
            def _(dve):
                done = [0]

                def signal(op, sem, value):
                    op.then_inc(sem, 1)
                    dve.wait_ge(sem, value)

                def link(op):
                    done[0] += 1
                    op.then_inc(chain, 1)
                    dve.wait_ge(chain, done[0])

                def inv_root(out, root, variance):
                    link(nc.vector.reciprocal(out, root))
                    link(nc.vector.tensor_tensor(t2, out, out, ALU.mult))
                    link(nc.vector.tensor_tensor(t2, t2, variance, ALU.mult))
                    link(nc.vector.tensor_scalar(t2, t2, -0.5, 1.5, ALU.mult, ALU.add))
                    link(nc.vector.tensor_tensor(out, out, t2, ALU.mult))

                dc = pg.ps[:, 7, 0:B]
                nc.vector.memset(BD[0][:], 0.0)
                nc.vector.memset(BD[1][:], 0.0).then_inc(zeroed, 1)
                link(nc.vector.memset(st[:], 0.0))
                dve.wait_ge(sq_in, 64)
                dve.wait_ge(dc_done, 1)
                link(nc.vector.tensor_scalar(mean, dc, 1.0 / NF, None, ALU.mult))
                link(nc.vector.tensor_tensor(t0, mean, mean, ALU.mult))
                link(nc.vector.tensor_scalar(tot, tot, 1.0 / NF, None, ALU.mult))
                link(nc.vector.tensor_tensor(tot, tot, t0, ALU.subtract))
                signal(nc.vector.tensor_scalar(var, tot, EPS, None, ALU.add), var_ready, 1)
                dve.wait_ge(root_done, 1)
                inv_root(rs, t1, var)
                link(nc.vector.tensor_scalar(t0, mean, float(HW), None, ALU.mult))
                dve.wait_ge(x_in, 16)
                x00 = X[0:C, :, 0, 1, 0]
                link(nc.vector.tensor_tensor(x00, x00, t0[0:C], ALU.subtract))
                for b in range(B):
                    xb = X[:, b].rearrange("p q r m -> p (q r m)")
                    op = nc.vector.tensor_scalar(xb, xb, rs[:, b:b + 1], None, ALU.mult)
                op.then_inc(normed, 1)
                evacuate_weights(dve, nc.vector.tensor_copy, w_out_dve, (2, 3), True)

                dve.wait_ge(mix_out, 2 * MQ)
                dve.wait_ge(mix_done, 2 * MQ)
                link(nc.vector.memset(S[0:C, :, 0, 1, 0], 0.0))
                for a, total, col0 in ((X[:, :, :, 1:3, :], qs, qc), (S[:, :, :, 0:2, :], cs, cc)):
                    for b in range(B):
                        op = nc.vector.tensor_tensor(prod[:, b], a[:, b], S[:, b, :, 0:2, :], ALU.mult)
                    link(op)
                    link(nc.vector.tensor_reduce(total, prod[:].rearrange("p b q r m -> p b (q r m)"), AX_X, ALU.add))
                    link(nc.vector.tensor_reduce(col0, prod[:, :, :, :, 0].rearrange("p b q r -> p b (q r)"), AX_X, ALU.add))
                link(nc.vector.scalar_tensor_tensor(qs, qs, 2.0, qc, ALU.mult, ALU.subtract))
                link(nc.vector.tensor_scalar(cc, cc, 1.5, None, ALU.mult))
                link(nc.vector.scalar_tensor_tensor(cs, cs, 2.0, cc, ALU.mult, ALU.subtract))
                s00 = S[0:C, :, 0, 0, 0]
                link(nc.vector.tensor_tensor(t0[0:C], s00, s00, ALU.mult))
                signal(nc.vector.scalar_tensor_tensor(cs[0:C], t0[0:C], 0.5, cs[0:C], ALU.mult, ALU.add),
                       sums_ready, 1)
                dve.wait_ge(sums_done, 1)
                link(nc.vector.tensor_tensor(t0, var, rs, ALU.mult))
                link(nc.vector.tensor_tensor(t0, t0, pg.ps[:, 7, B:2 * B], ALU.mult))
                link(nc.vector.tensor_scalar(t0, t0, 2.0, None, ALU.mult))
                link(nc.vector.tensor_tensor(t0, t0, pg.ps[:, 7, 2 * B:3 * B], ALU.add))
                link(nc.vector.tensor_scalar(t0, t0, 1.0 / (float(HW) * NF), None, ALU.mult))
                link(nc.vector.tensor_tensor(v1, t0, tot, ALU.add))
                link(nc.vector.tensor_scalar(em, pg.ps[:, 7, 3 * B:4 * B], 1.0 / NF, None, ALU.mult))
                link(nc.vector.tensor_tensor(m1, mean, em, ALU.add))
                link(nc.vector.tensor_tensor(em, em, em, ALU.mult))
                link(nc.vector.tensor_tensor(v1, v1, em, ALU.subtract))
                signal(nc.vector.tensor_scalar(v1, v1, EPS, None, ALU.add), var_ready, 2)
                dve.wait_ge(root_done, 2)
                inv_root(t3, t1, v1)
                nc.vector.tensor_copy(st[:, :, 0], m1)
                nc.vector.tensor_copy(st[:, :, 1], t3)
                nc.vector.tensor_scalar(st[:, :, 2], t3, 1.0, None, ALU.add)
                link(nc.vector.tensor_scalar(t0, m1, float(HW), None, ALU.mult))
                nc.vector.tensor_tensor(s00, s00, t0[0:C], ALU.subtract)
                s00n = S[0:C, :, 0, 2, 0]
                nc.vector.tensor_tensor(s00n, s00n, t0[0:C], ALU.add).then_inc(s_final, 1)
                for b in range(B):
                    for half in range(2):
                        dve.wait_ge(tr_done, 2 * b + half + 1)
                        if half == 0 and b >= 2:
                            dve.wait_ge(sx_out, 16 * (b - 1))
                        src = pg.ps[0:2 * M, 2 * half + 1].rearrange("p (i o) -> p i o", i=16)
                        dst = SX[b % 2][:, :, 1, half * 16:(half + 1) * 16].rearrange("p c i -> p i c")
                        nc.vector.tensor_copy(dst, src).then_inc(tr_out_dve, 1)


class Inverse:
    VB, YB = 2, 2

    def __init__(self, pg, mem, name, first_bank):
        nc = pg.nc
        self.pg, self.bank0 = pg, first_bank
        self.slot = [mem.enter_context(nc.sbuf_tensor(f"{name}_x{k}", [P, HB, CU, W], F32)) for k in range(KU)]
        self.sxs = [mem.enter_context(nc.sbuf_tensor(f"{name}_sx{k}", [2 * M, CU, 2 * M], F32)) for k in range(KU)]
        self.v = [mem.enter_context(nc.sbuf_tensor(f"{name}_v{i}", [2 * M, CU, W], F32)) for i in range(2)]
        self.loaded = [pg.sem(f"{name}_loaded{k}") for k in range(KU)]
        self.v_done = pg.sem(name + "_v_done")
        self.v_out = pg.sem(name + "_v_out")
        self.y_done = pg.sem(name + "_y_done")
        self.y_out = pg.sem(name + "_y_out")

    def load(self, sp, src, sx, s, k):
        for hb in range(HB):
            sp.dma_start(self.slot[k][:, hb], unit_rows(src, s, k, hb)).then_inc(self.loaded[k], 16)
        sp.dma_start(self.sxs[k][:, :, :].rearrange("p c m -> p (c m)"),
                     sx[bass.ds(s, 1), :, k * CU * 2 * M:(k + 1) * CU * 2 * M].rearrange("b p f -> p (b f)")
                     ).then_inc(self.loaded[k], 16)

    def pe_v(self, pe, s, k, loads):
        nc = self.pg.nc
        pe.wait_ge(self.loaded[k], s * (16 * loads) + 16 * loads)
        for n in range(CU // 2):
            self.pg.hold(pe, self.v_out, s * 16 + (4 * k + n + 1))
            bank = self.pg.ps[0:2 * M, self.bank0 + n % 2].rearrange("p (c w) -> p c w", c=2)
            for c in range(2):
                mm = nc.tensor.matmul(bank[:, c, :], self.sxs[k][:, 2 * n + c, :], self.pg.t("EW", 2 * M),
                                      start=True, stop=True)
            mm.then_inc(self.v_done, 1)

    def act_v(self, act, s, k, first):
        nc = self.pg.nc
        if not first:
            act.wait_ge(self.y_done, s * 32 + (8 * k - 8))
        for n in range(CU // 2):
            act.wait_ge(self.v_done, s * 16 + (4 * k + n + 1))
            bank = self.pg.ps[0:2 * M, self.bank0 + n % 2]
            nc.scalar.copy(self.v[k % 2][:, 2 * n:2 * n + 2, :].rearrange("p c w -> p (c w)"), bank
                           ).then_inc(self.v_out, 1)

    def pe_y(self, pe, s, k, table):
        nc = self.pg.nc
        eh = self.pg.t(table, 2 * M)
        for n in range(CU // 2):
            pe.wait_ge(self.v_out, s * 16 + (4 * k + n + 1 + self.VB))
            for hb in range(HB):
                at = 2 * n + hb
                pe.wait_ge(self.y_out, s * 32 + (8 * k + at + 1))
                bank = self.pg.ps[:, self.bank0 + 2 + at % 2]
                nc.tensor.matmul(bank, eh[:, hb * P:(hb + 1) * P],
                                 self.v[k % 2][:, 2 * n:2 * n + 2, :].rearrange("p c w -> p (c w)"),
                                 start=True, stop=True).then_inc(self.y_done, 1)

    def dve_y(self, dve, s, k, op, loads):
        nc = self.pg.nc
        dve.wait_ge(self.loaded[k], s * (16 * loads) + 16 * loads)
        for n in range(CU // 2):
            for hb in range(HB):
                at = 2 * n + hb
                dve.wait_ge(self.y_done, s * 32 + (8 * k + at + 1))
                bank = self.pg.ps[:, self.bank0 + 2 + at % 2]
                xs = self.slot[k][:, hb, 2 * n:2 * n + 2, :].rearrange("p c w -> p (c w)")
                nc.vector.tensor_tensor(xs, bank, xs, op).then_inc(self.y_out, 1)


def phase_wavelet(pg, x, sx, stats, x2, modes, sumsq):
    nc = pg.nc
    LOADS = 4
    Q, Q2, Q3 = W // 2, W // 4, W // 8
    with ExitStack() as mem:
        def sb(n, shape):
            return mem.enter_context(nc.sbuf_tensor("b_" + n, shape, F32))
        iv = Inverse(pg, mem, "b", 0)
        fw = Forward(pg, mem, "bf", 4)
        stt = [sb(f"st{k}", [P, 4, CU]) for k in range(KU)]
        odd = sb("odd", [P, HB, CU, Q])
        f1 = sb("f1", [P, HB * CU, Q + 1])
        f2 = sb("f2", [P, HB * CU, Q2 + 1])
        f3 = sb("f3", [P, HB * CU, Q3])
        down = sb("down", [P, CU, Q])
        zero_cols = pg.sem("b_zero_cols")
        odd1, edge1, odd2, odd3 = (pg.sem("b_" + n) for n in ("odd1", "edge1", "odd2", "odd3"))
        f1_done, f2_done, f3_done = (pg.sem("b_" + n) for n in ("f1_done", "f2_done", "f3_done"))
        d_done = pg.sem("b_d_done")
        d_out = pg.sem("b_d_out")
        scaled = pg.sem("b_scaled")
        d_diff = pg.sem("b_d_diff")
        x2_done = pg.sem("b_x2_done")
        x2_out = [pg.sem(f"b_x2_out{k}") for k in range(KU)]
        R = [iv.slot[k] for k in range(KU)]

        with nc.Block(name="wavelet") as block:
            @block.sync
            def _(sp):
                def load(s, k):
                    iv.load(sp, x, sx, s, k)
                    sp.dma_start(stt[k][:, :, :], stats[bass.ds(s, 1), :, k * CU:(k + 1) * CU].to_broadcast(
                        [P, 4, CU])).then_inc(iv.loaded[k], 16)

                def body(s, first, last):
                    for k in range(KU):
                        pg.hold(sp, x2_done, s * KU + (k + 1))
                        for hb in range(HB):
                            sp.dma_start(unit_rows(x2, s, k, hb), iv.slot[k][:, hb]).then_inc(x2_out[k], 16)
                        if k == 0 and first:
                            continue
                        j = (k - 1) % KU
                        if last and k > 0:
                            continue
                        s_old = s - 1 if k == 0 else s
                        pg.hold(sp, x2_out[j], s_old * 32 + 32)
                        pg.hold(sp, fw.cols_done, s_old * (2 * KU) + (2 * j + 2))
                        pg.hold(sp, fw.sq_done, fw.sq_count(s_old, j))
                        load(s_old + 1, j)
                for k in range(KU):
                    load(0, k)
                body(0, True, False)
                with sp.Fori(1, B - 1) as s:
                    body(s, False, False)
                body(B - 1, False, True)
                for k in range(KU):
                    pg.hold(sp, x2_out[k], B * 32)

            @block.tensor
            def _(pe):
                f1v = f1[:, :, 1:Q + 1].rearrange("p (n c) w -> p n c w", n=HB)
                f2v = f2[:, :, 1:Q2 + 1].rearrange("p (n c) w -> p n c w", n=HB)
                f3v = f3[:, :, :].rearrange("p (n c) w -> p n c w", n=HB)
                d1 = pg.t("D1").rearrange("p (n m) -> p n m", n=HB)
                d2 = pg.t("D2").rearrange("p (n m) -> p n m", n=HB)
                d3 = pg.t("D3").rearrange("p (n m) -> p n m", n=HB)

                def pyramid(s, k):
                    pe.wait_ge(f1_done, s * KU + (k + 1))
                    pe.wait_ge(fw.cols_out, s * (2 * KU) + (2 * k + 2 - 2 + fw.BANKS))
                    for half in range(2):
                        bank = pg.ps[:, 4 + half].rearrange("p (c w) -> p c w", c=4)
                        for hb in range(HB):
                            mm = nc.tensor.matmul(bank, d1[:, hb, :], f1v[:, hb, 4 * half:4 * half + 4, :],
                                                  start=(hb == 0), stop=(hb == HB - 1))
                        mm.then_inc(d_done, 1)
                    pe.wait_ge(f2_done, s * KU + (k + 1))
                    pe.wait_ge(f3_done, s * KU + (k + 1))
                    for bank, dm, f, rows, n in ((pg.ps[0:64, 0], d2, f2v, 64, Q2), (pg.ps[0:32, 1], d3, f3v, 32, Q3)):
                        out = bank[:, 0:CU * n].rearrange("p (c w) -> p c w", c=CU)
                        for hb in range(HB):
                            mm = nc.tensor.matmul(out, dm[:, hb, :], f[:, hb, :, :], start=(hb == 0), stop=(hb == HB - 1))
                        mm.then_inc(d_done, 1)
                    pe.wait_ge(d_out, s * KU + (k + 1))

                def transform(s, k):
                    pe.wait_ge(x2_done, s * KU + (k + 1))
                    fw.pe_unit(pe, s, k, R[k])
                    if k == KU - 1:
                        fw.pe_sample(pe, s)

                def body(s, first=False, last=False):
                    for k in range(KU):
                        more = not (last and k == KU - 1)
                        nxt = (s, k + 1) if k + 1 < KU else (s + 1, 0)
                        if more:
                            iv.pe_v(pe, *nxt, LOADS)
                        if not (first and k == 0):
                            prev = (s, k - 1) if k > 0 else (s - 1, KU - 1)
                            transform(*prev)
                        if more:
                            iv.pe_y(pe, *nxt, "EH")
                        pyramid(s, k)
                pe.sem_inc(fw.modes_done, 1)
                iv.pe_v(pe, 0, 0, LOADS)
                iv.pe_y(pe, 0, 0, "EH")
                body(0, first=True)
                with pe.Fori(1, B - 1) as s:
                    body(s)
                body(B - 1, last=True)
                transform(B - 1, KU - 1)

            @block.scalar
            def _(act):
                act.sem_inc(iv.v_out, iv.VB)
                fw.start(act)

                def copy_down(s, k):
                    act.wait_ge(x2_done, s * KU + k)
                    n = s * 4 * KU + 4 * k
                    act.wait_ge(d_done, n + 2)
                    for half in range(2):
                        bank = pg.ps[:, 4 + half].rearrange("p (c w) -> p c w", c=4)
                        cs = slice(4 * half, 4 * half + 4)
                        nc.scalar.copy(down[64:P, cs, :], bank[64:P])
                        nc.scalar.copy(down[0:64, cs, Q2:Q], bank[0:64, :, Q2:Q])
                    act.wait_ge(d_done, n + 4)
                    b2 = pg.ps[0:64, 0].rearrange("p (c w) -> p c w", c=CU)
                    b3 = pg.ps[0:32, 1, 0:CU * Q3].rearrange("p (c w) -> p c w", c=CU)
                    nc.scalar.copy(down[32:64, :, 0:Q2], b2[32:64])
                    nc.scalar.copy(down[0:32, :, Q3:Q2], b2[0:32, :, Q3:Q2])
                    nc.scalar.copy(down[0:32, :, 0:Q3], b3).then_inc(d_out, 1)

                def scale(s, k):
                    act.wait_ge(d_diff, s * KU + (k + 1))
                    for g in range(CU // GROUP):
                        xg = R[k][:, :, g * GROUP:(g + 1) * GROUP, :].rearrange("p n c w -> p n (c w)")
                        c = g * GROUP
                        op = nc.scalar.activation(xg, xg, ACT.Identity, scale=stt[k][:, 2, c:c + 1],
                                                  bias=stt[k][:, 0, c:c + 1])
                    op.then_inc(scaled, 1)

                def finish(s, k):
                    act.wait_ge(x2_done, s * KU + (k + 1))
                    fw.act_squares(act, s, k, R[k])
                    fw.act_cols(act, s, k)

                def body(s, first=False, last=False):
                    for k in range(KU):
                        if not (last and k == KU - 1):
                            nxt = (s, k + 1) if k + 1 < KU else (s + 1, 0)
                            iv.act_v(act, *nxt, first=(first and k == 0))
                        if not (first and k == 0):
                            finish(*((s, k - 1) if k > 0 else (s - 1, KU - 1)))
                        copy_down(s, k)
                        scale(s, k)
                iv.act_v(act, 0, 0, first=True)
                body(0, first=True)
                with act.Fori(1, B - 1) as s:
                    body(s)
                body(B - 1, last=True)
                finish(B - 1, KU - 1)

            @block.vector
            def _(dve):
                dve.sem_inc(iv.y_out, iv.YB)
                dve.sem_inc(fw.modes_out, 1)
                nc.vector.memset(f1[:, :, 0:1], 0.0)
                nc.vector.memset(f2[:, :, 0:1], 0.0).then_inc(zero_cols, 1)
                dve.wait_ge(zero_cols, 1)

                def filters(s, k):
                    u1 = s * KU + (k + 1)
                    xr = R[k]
                    dve.wait_ge(iv.y_out, s * 32 + (8 * k + 8 + iv.YB))
                    nc.vector.tensor_tensor(odd[:, :, :, 1:Q], xr[:, :, :, 1:W - 2:2], xr[:, :, :, 3:W:2], ALU.add
                                            ).then_inc(odd1, 1)
                    nc.vector.tensor_copy(odd[:, :, :, 0:1], xr[:, :, :, 1:2]).then_inc(edge1, 1)
                    dve.wait_ge(odd1, u1)
                    dve.wait_ge(edge1, u1)
                    dve.wait_ge(d_out, s * KU + k)
                    nc.vector.scalar_tensor_tensor(
                        f1[:, :, 1:Q + 1], xr[:, :, :, 0:W:2].rearrange("p n c w -> p (n c) w"), 2.0,
                        odd[:, :, :, :].rearrange("p n c w -> p (n c) w"), ALU.mult, ALU.add).then_inc(f1_done, 1)
                    dve.wait_ge(f1_done, u1)
                    o2 = odd[:, :, :, 0:Q2].rearrange("p n c w -> p (n c) w")
                    nc.vector.tensor_tensor(o2, f1[:, :, 0:Q - 1:2], f1[:, :, 2:Q + 1:2], ALU.add).then_inc(odd2, 1)
                    dve.wait_ge(odd2, u1)
                    nc.vector.scalar_tensor_tensor(f2[:, :, 1:Q2 + 1], f1[:, :, 1:Q:2], 2.0, o2, ALU.mult, ALU.add
                                                   ).then_inc(f2_done, 1)
                    dve.wait_ge(f2_done, u1)
                    o3 = odd[:, :, :, 0:Q3].rearrange("p n c w -> p (n c) w")
                    nc.vector.tensor_tensor(o3, f2[:, :, 0:Q2 - 1:2], f2[:, :, 2:Q2 + 1:2], ALU.add).then_inc(odd3, 1)
                    dve.wait_ge(odd3, u1)
                    nc.vector.scalar_tensor_tensor(f3[:, :, :], f2[:, :, 1:Q2:2], 2.0, o3, ALU.mult, ALU.add
                                                   ).then_inc(f3_done, 1)

                def finish(s, k):
                    u1 = s * KU + (k + 1)
                    quad = R[k][:, 0, :, 0:Q]
                    dve.wait_ge(d_out, u1)
                    nc.vector.tensor_tensor(down[:, :, :], down[:, :, :], quad, ALU.subtract).then_inc(d_diff, 1)
                    dve.wait_ge(d_diff, u1)
                    dve.wait_ge(scaled, u1)
                    for g in range(CU // GROUP):
                        cs = slice(g * GROUP, (g + 1) * GROUP)
                        op = nc.vector.scalar_tensor_tensor(quad[:, cs], down[:, cs], stt[k][:, 1, g * GROUP:g * GROUP + 1],
                                                            quad[:, cs], ALU.mult, ALU.add)
                    op.then_inc(x2_done, 1)

                def body(s, first=False, last=False):
                    for k in range(KU):
                        if not (last and k == KU - 1):
                            nxt = (s, k + 1) if k + 1 < KU else (s + 1, 0)
                            iv.dve_y(dve, *nxt, ALU.add, LOADS)
                        finish(s, k)
                        if not (last and k == KU - 1):
                            filters(*nxt)
                        if k == 0 and not first:
                            fw.dve_sample(dve, s - 1)
                iv.dve_y(dve, 0, 0, ALU.add, LOADS)
                filters(0, 0)
                body(0, first=True)
                with dve.Fori(1, B - 1) as s:
                    body(s)
                body(B - 1, last=True)
                fw.dve_sample(dve, B - 1)

            @block.gpsimd
            def _(pool):
                pool.sem_inc(fw.xf_free, 1)
                with pool.Fori(0, B) as s:
                    fw.pool_sample(pool, s, modes, sumsq)
                pool.wait_ge(fw.stored, B * 32)


def phase_inverse(pg, x2, sx, nx):
    nc = pg.nc
    LOADS = 3
    with ExitStack() as mem:
        iv = Inverse(pg, mem, "c", 0)
        stored = [pg.sem(f"c_stored{k}") for k in range(KU)]
        with nc.Block(name="inverse") as block:
            @block.sync
            def _(sp):
                def store(s, k):
                    pg.hold(sp, iv.y_out, s * 32 + (8 * k + 8 + iv.YB))
                    for hb in range(HB):
                        sp.dma_start(unit_rows(nx, s, k, hb), iv.slot[k][:, hb]).then_inc(stored[k], 16)

                def reload(s_old, k):
                    pg.hold(sp, stored[k], s_old * 32 + 32)
                    iv.load(sp, x2, sx, s_old + 1, k)
                for k in range(KU):
                    iv.load(sp, x2, sx, 0, k)
                for k in range(KU):
                    store(0, k)
                    if k:
                        reload(0, k - 1)
                with sp.Fori(1, B - 1) as s:
                    for k in range(KU):
                        store(s, k)
                        reload(*((s, k - 1) if k else (s - 1, KU - 1)))
                store(B - 1, 0)
                reload(B - 2, KU - 1)
                for k in range(1, KU):
                    store(B - 1, k)
                for k in range(KU):
                    pg.hold(sp, stored[k], B * 32)

            @block.tensor
            def _(pe):
                iv.pe_v(pe, 0, 0, LOADS)

                def body(s, last=False):
                    for k in range(KU):
                        if not (last and k == KU - 1):
                            iv.pe_v(pe, *((s, k + 1) if k + 1 < KU else (s + 1, 0)), LOADS)
                        iv.pe_y(pe, s, k, "EN")
                with pe.Fori(0, B - 1) as s:
                    body(s)
                body(B - 1, last=True)

            @block.scalar
            def _(act):
                act.sem_inc(iv.v_out, iv.VB)

                def body(s, first=False):
                    for k in range(KU):
                        iv.act_v(act, s, k, first=first and k < 2)
                body(0, first=True)
                with act.Fori(1, B) as s:
                    body(s)

            @block.vector
            def _(dve):
                dve.sem_inc(iv.y_out, iv.YB)
                with dve.Fori(0, B) as s:
                    for k in range(KU):
                        iv.dve_y(dve, s, k, ALU.subtract, LOADS)


def phase_scan_down(pg, nx, gates, ctx_down):
    nc = pg.nc
    NB = H // RR
    nxr = nx.rearrange("b c h w -> (b c) (h w)").rearrange("(g p) f -> p g f", p=P)
    outr = ctx_down.rearrange("b c h w -> (b c) (h w)").rearrange("(g p) f -> p g f", p=P)
    with ExitStack() as mem:
        def sb(n, shape):
            return [mem.enter_context(nc.sbuf_tensor(f"d_{n}{i}", shape, F32)) for i in range(2)]
        xin, u, cx = sb("x", [P, GB, RR, W]), sb("u", [P, GB, RR, W]), sb("c", [P, GB, RR, W])
        gate, carry = sb("g", [P, RR, W]), sb("t", [P, GB, W])
        loaded = [pg.sem(f"d_loaded{i}") for i in range(2)]
        carried = pg.sem("d_carried")
        rows = pg.sem("d_rows")
        clamped = pg.sem("d_clamped")
        stored = [pg.sem(f"d_stored{i}") for i in range(2)]

        def flat(n):
            return bass.ds((n * (-RR) + (H - RR)) * W, RR * W)

        with nc.Block(name="scan_down") as block:
            @block.sync
            def _(sp):
                def load(n, i):
                    sp.dma_start(xin[i][:].rearrange("p g r w -> p g (r w)"), nxr[:, :, flat(n)]).then_inc(loaded[i], 16)
                    sp.dma_start(gate[i][:].rearrange("p r w -> p (r w)"),
                                 gates[1].rearrange("h w -> (h w)").unsqueeze(0)[
                                     :, bass.ds((n * (-RR) + (H - RR + 1)) * W, RR * W)].to_broadcast([P, RR * W])
                                 ).then_inc(loaded[i], 16)

                def store(n, i):
                    pg.hold(sp, clamped, n + 1)
                    sp.dma_start(outr[:, :, flat(n)], cx[i][:].rearrange("p g r w -> p g (r w)")).then_inc(stored[i], 16)
                load(0, 0)
                load(1, 1)
                with sp.Fori(0, NB // 2 - 1) as half:
                    n = half * 2
                    for i in range(2):
                        pg.hold(sp, rows, n * RR + (i + 1) * RR)
                        load(n + (i + 2), i)
                        store(n + i, i)
                for i in range(2):
                    store(NB - 2 + i, i)
                for i in range(2):
                    pg.hold(sp, stored[i], 16 * (NB // 2))

            @block.vector
            def _(dve):
                def block_rows(n, half, i, first=False):
                    dve.wait_ge(loaded[i], half * 32 + 32)
                    if not first:
                        dve.wait_ge(clamped, n - 1)
                    for a in range(RR):
                        r = RR - 1 - a
                        if first and a == 0:
                            nc.vector.tensor_scalar(u[i][:, :, r, :], xin[i][:, :, r, :], -1.0, None, ALU.mult
                                                    ).then_inc(rows, 1)
                            nc.vector.memset(carry[1][:, 0, 0:1], 0.0).then_inc(carried, 1)
                            dve.wait_ge(carried, 1)
                            continue
                        at = n * RR + a
                        dve.wait_ge(rows, at)
                        prev = u[i][:, :, r + 1, :] if a else u[1 - i][:, :, 0, :]
                        g = gate[i][:, r, :].unsqueeze(1).to_broadcast([P, GB, W])
                        if first and a == 1:
                            op = nc.vector.tensor_tensor(carry[a % 2][:], prev, g, ALU.mult)
                        else:
                            op = nc.vector.scalar_tensor_tensor(carry[a % 2][:], prev, 0.0, g, ALU.max, ALU.mult)
                        op.then_inc(carried, 1)
                        dve.wait_ge(carried, at + 1)
                        nc.vector.tensor_tensor(u[i][:, :, r, :], carry[a % 2][:], xin[i][:, :, r, :], ALU.subtract
                                                ).then_inc(rows, 1)
                block_rows(0, 0, 0, first=True)
                block_rows(1, 0, 1)
                with dve.Fori(1, NB // 2) as half:
                    n = half * 2
                    for i in range(2):
                        block_rows(n + i, half, i)

            @block.scalar
            def _(act):
                def clamp(n, i, half, first=False):
                    act.wait_ge(rows, n * RR + RR)
                    act.wait_ge(stored[i], half * 16)
                    if first:
                        nc.scalar.copy(cx[i][:, :, RR - 1, :], u[i][:, :, RR - 1, :])
                        op = nc.scalar.activation(cx[i][:, :, 0:RR - 1, :], u[i][:, :, 0:RR - 1, :], ACT.Relu)
                    else:
                        op = nc.scalar.activation(cx[i][:].rearrange("p g r w -> p (g r w)"),
                                                  u[i][:].rearrange("p g r w -> p (g r w)"), ACT.Relu)
                    op.then_inc(clamped, 1)
                clamp(0, 0, 0, first=True)
                clamp(1, 1, 0)
                with act.Fori(1, NB // 2) as half:
                    n = half * 2
                    for i in range(2):
                        clamp(n + i, i, half)


def phase_scans(pg, nx, ctx_down, gates, gate_cols, conv_w, conv_b, stats, out):
    nc = pg.nc
    NB = H // RF
    F = RF * W

    def grouped(a):
        return a.rearrange("b c h w -> (b c) (h w)").rearrange("(g p) f -> p g f", p=P)
    nxr, cdr, outr = grouped(nx), grouped(ctx_down), grouped(out)
    with ExitStack() as mem:
        def sb(n, shape):
            return mem.enter_context(nc.sbuf_tensor("e_" + n, shape, F32))

        def sb2(n, shape):
            return [sb(f"{n}{i}", shape) for i in range(2)]
        xin, cd, u, cu = (sb2(n, [P, GB, RF, W]) for n in ("x", "cd", "u", "cu"))
        ncl, ncr, dl, dr = (sb2(n, [P, GB, RF, W]) for n in ("ncl", "ncr", "dl", "dr"))
        z = sb2("z", [P, GB, RF, W])
        gate = sb2("g", [P, 3, RF, W])
        carry = sb("carry", [P, GB, W])
        wraw = sb("wraw", [P, 4, P])
        wt = sb("wt", [P, GB, 6, P])
        bias = sb("bias", [P, 1])
        sts = sb("sts", [P, GB, 4])
        set_in = pg.sem("e_set_in")
        sts_in = pg.sem("e_sts_in")
        wt_done = pg.sem("e_wt_done")
        loaded = [pg.sem(f"e_loaded{i}") for i in range(2)]
        carried, rows = pg.sem("e_carried"), pg.sem("e_rows")
        lin_done = pg.sem("e_lin_done")
        gated = pg.sem("e_gated")
        scans_done = pg.sem("e_scans_done")
        up_clamped = pg.sem("e_up_clamped")
        mixed = pg.sem("e_mixed")
        z_done = pg.sem("e_z_done")
        summed = pg.sem("e_summed")
        stored = [pg.sem(f"e_stored{i}") for i in range(2)]

        with nc.Block(name="scans") as block:
            @block.sync
            def _(sp):
                sp.dma_start(wraw[:, :, :], conv_w).then_inc(set_in, 16)
                sp.dma_start(bias[:, :], conv_b).then_inc(set_in, 16)
                def flat(n):
                    return bass.ds(n * F, F)

                def load(n, i):
                    sp.dma_start(xin[i][:].rearrange("p g r w -> p g (r w)"), nxr[:, :, flat(n)]).then_inc(loaded[i], 16)
                    sp.dma_start(cd[i][:].rearrange("p g r w -> p g (r w)"), cdr[:, :, flat(n)]).then_inc(loaded[i], 16)
                    for d, src in enumerate((gates[0], gate_cols[0], gate_cols[1])):
                        sp.dma_start(gate[i][:, d].rearrange("p r w -> p (r w)"),
                                     src.rearrange("h w -> (h w)").unsqueeze(0)[:, flat(n)].to_broadcast([P, F])
                                     ).then_inc(loaded[i], 16)

                def store(n, i):
                    pg.hold(sp, summed, n + 1)
                    sp.dma_start(outr[:, :, flat(n)], z[i][:].rearrange("p g r w -> p g (r w)")).then_inc(stored[i], 16)
                load(0, 0)
                load(1, 1)
                with sp.Fori(0, NB // 2 - 1) as half:
                    n = half * 2
                    for i in range(2):
                        store(n + i, i)
                        pg.hold(sp, mixed, n * GB + (i + 1) * GB)
                        load(n + (i + 2), i)
                for i in range(2):
                    store(NB - 2 + i, i)
                for i in range(2):
                    pg.hold(sp, stored[i], 16 * (NB // 2))

            @block.gpsimd
            def _(pool):
                with nc.allow_non_contiguous_dma(reason="a few words per channel"):
                    for g in range(GB):
                        for b in range(4):
                            pool.dma_start(sts[b * C:(b + 1) * C, g, :],
                                           stats[4 * g + b].rearrange("k c -> c k")).then_inc(sts_in, 16)

            @block.vector
            def _(dve):
                dve.wait_ge(set_in, 2 * 16)
                dve.wait_ge(sts_in, 4 * GB * 16)
                for g in range(GB):
                    r = sts[:, g, 1:2]
                    op = nc.vector.tensor_scalar(wt[:, g, 0:4, :], wraw[:, :, :], r, None, ALU.mult)
                    op = nc.vector.tensor_scalar(wt[:, g, 4:6, :], wraw[:, 0:2, :], r, -1.0, ALU.mult, ALU.mult)
                op.then_inc(wt_done, 1)

                def up_rows(n, i, first=False):
                    for r in range(RF):
                        at = n * RF + r
                        if first and r == 0:
                            nc.vector.tensor_scalar(u[i][:, :, 0, :], xin[i][:, :, 0, :], -1.0, None, ALU.mult
                                                    ).then_inc(rows, 1)
                            nc.vector.memset(carry[:, 0, 0:1], 0.0).then_inc(carried, 1)
                            dve.wait_ge(carried, 1)
                            continue
                        dve.wait_ge(rows, at)
                        prev = u[i][:, :, r - 1, :] if r else u[1 - i][:, :, RF - 1, :]
                        g = gate[i][:, 0, r, :].unsqueeze(1).to_broadcast([P, GB, W])
                        if first and r == 1:
                            op = nc.vector.tensor_tensor(carry[:], prev, g, ALU.mult)
                        else:
                            op = nc.vector.scalar_tensor_tensor(carry[:], prev, 0.0, g, ALU.max, ALU.mult)
                        op.then_inc(carried, 1)
                        dve.wait_ge(carried, at + 1)
                        nc.vector.tensor_tensor(u[i][:, :, r, :], carry[:], xin[i][:, :, r, :], ALU.subtract
                                                ).then_inc(rows, 1)

                def line(t, g=None, d=None, rev=False):
                    a = t[:, d] if g is None else t[:, g]
                    a = a.rearrange("p r w -> p (r w)")
                    return a[:, ::-1] if rev else a

                def scan_block(n, half, i, first=False):
                    dve.wait_ge(loaded[i], half * 80 + 80)
                    if not first:
                        dve.wait_ge(up_clamped, n - 1)
                    up_rows(n, i, first)
                    if not first:
                        dve.wait_ge(mixed, n * GB - GB)
                    for d, nl in ((1, ncl), (2, ncr)):
                        for g in range(GB):
                            rev = d == 2
                            op = nc.vector.tensor_tensor_scan(line(nl[i], g=g, rev=rev), line(gate[i], d=d, rev=rev),
                                                              line(xin[i], g=g, rev=rev), 0.0, ALU.mult, ALU.add)
                        op.then_inc(lin_done, 1)
                    dve.wait_ge(lin_done, n * 2 + 2)
                    nc.vector.memset(gate[i][:, 1, :, 1:2], 0.0)
                    nc.vector.memset(gate[i][:, 2, :, W - 2:W - 1], 0.0).then_inc(gated, 1)

                def clamp_block(n, i):
                    dve.wait_ge(gated, n + 1)
                    for d, nl, dd in ((1, ncl, dl), (2, ncr, dr)):
                        for g in range(GB):
                            rev = d == 2
                            op = nc.vector.tensor_tensor_scan(line(dd[i], g=g, rev=rev), line(gate[i], d=d, rev=rev),
                                                              line(nl[i], g=g, rev=rev), 0.0, ALU.mult, ALU.max)
                    op.then_inc(scans_done, 1)

                def sum_block(n, i):
                    for g in range(GB):
                        dve.wait_ge(z_done, n * GB + (g + 1))
                        zg = z[i][:, g].rearrange("p r w -> p (r w)")
                        op = nc.vector.scalar_tensor_tensor(zg, zg, sts[:, g, 0:1],
                                                            xin[i][:, g].rearrange("p r w -> p (r w)"),
                                                            ALU.add, ALU.subtract)
                    op.then_inc(summed, 1)

                scan_block(0, 0, 0, first=True)
                clamp_block(0, 0)
                scan_block(1, 0, 1)
                sum_block(0, 0)
                clamp_block(1, 1)
                with dve.Fori(1, NB // 2) as half:
                    n = half * 2
                    for i in range(2):
                        scan_block(n + i, half, i)
                        sum_block(n + (i - 1), 1 - i)
                        clamp_block(n + i, i)
                sum_block(NB - 1, 1)

            @block.tensor
            def _(pe):
                pe.wait_ge(wt_done, 1)

                def mix(n, i):
                    pe.wait_ge(scans_done, n + 1)
                    pe.wait_ge(up_clamped, n + 1)
                    for g in range(GB):
                        bank = pg.ps[:, i * GB + g]
                        full = bank
                        for q, (wi, src) in enumerate(((4, ncl), (5, ncr), (2, cu), (3, cd))):
                            nc.tensor.matmul(full, wt[:, g, wi, :], src[i][:, g].rearrange("p r w -> p (r w)"),
                                             start=(q == 0), stop=False)
                        grid = bank.rearrange("p (r w) -> p r w", r=RF)
                        nc.tensor.matmul(grid[:, :, 1:W], wt[:, g, 0, :], dl[i][:, g, :, 1:W], start=False, stop=False)
                        nc.tensor.matmul(grid[:, :, 0:W - 1], wt[:, g, 1, :], dr[i][:, g, :, 0:W - 1],
                                         start=False, stop=True).then_inc(mixed, 1)

                def wait_z(n, i):
                    pe.wait_ge(z_done, n * GB - GB)
                mix(0, 0)
                mix(1, 1)
                with pe.Fori(1, NB // 2) as half:
                    n = half * 2
                    for i in range(2):
                        wait_z(n + i, i)
                        mix(n + i, i)

            @block.scalar
            def _(act):
                act.wait_ge(set_in, 2 * 16)

                def clamp_up(n, i, first=False):
                    act.wait_ge(rows, n * RF + RF)
                    if not first:
                        act.wait_ge(mixed, n * GB - GB)
                    if first:
                        nc.scalar.copy(cu[i][:, :, 0, :], u[i][:, :, 0, :])
                        op = nc.scalar.activation(cu[i][:, :, 1:RF, :], u[i][:, :, 1:RF, :], ACT.Relu)
                    else:
                        op = nc.scalar.activation(cu[i][:].rearrange("p g r w -> p (g r w)"),
                                                  u[i][:].rearrange("p g r w -> p (g r w)"), ACT.Relu)
                    op.then_inc(up_clamped, 1)

                def relu(n, i, half):
                    act.wait_ge(stored[i], half * 16)
                    for g in range(GB):
                        act.wait_ge(mixed, n * GB + (g + 1))
                        nc.scalar.activation(z[i][:, g].rearrange("p r w -> p (r w)"), pg.ps[:, i * GB + g], ACT.Relu,
                                             bias=bias[:, :]).then_inc(z_done, 1)
                clamp_up(0, 0, first=True)
                clamp_up(1, 1)
                relu(0, 0, 0)
                with act.Fori(1, NB // 2) as half:
                    n = half * 2
                    clamp_up(n, 0)
                    relu(n - 1, 1, half - 1)
                    clamp_up(n + 1, 1)
                    relu(n, 0, half)
                relu(NB - 1, 1, NB // 2 - 1)


def build(nc, ins, outs):
    x, cr0, ci0, pj0, cr2, ci2, pj2, weights, conv_w, conv_b, consts = ins
    out, = outs

    def scratch(name, shape):
        return nc.dram_tensor(name, shape, F32, kind="Internal").ap()
    with ExitStack() as ctx:
        pg = Prog(nc, ctx)
        gate_rows = scratch("s_gate_rows", [2, H + 1, W])
        gate_cols = scratch("s_gate_cols", [2, H, W])
        modes = scratch("s_modes", [B, P, XF])
        sumsq = scratch("s_sumsq", [B, C])
        sx = scratch("s_sx", [B, 2 * M, C * 2 * M])
        stats1, stats3 = scratch("s_stats1", [B, 4, C]), scratch("s_stats3", [B, 4, C])
        x2, nx, cdn = (scratch(n, [B, C, H, W]) for n in ("s_x2", "s_nx", "s_ctx_down"))
        phase_gates(pg, consts, weights, gate_rows, gate_cols)
        phase_forward(pg, x, modes, sumsq)
        phase_mix(pg, "m0", modes, sumsq, (cr0, ci0), pj0, sx, stats1)
        phase_wavelet(pg, x, sx, stats1, x2, modes, sumsq)
        phase_mix(pg, "m2", modes, sumsq, (cr2, ci2), pj2, sx, stats3)
        phase_inverse(pg, x2, sx, nx)
        phase_scan_down(pg, nx, gate_rows, cdn)
        phase_scans(pg, nx, cdn, gate_rows, gate_cols, conv_w, conv_b, stats3, out)


def kernel(**inputs):
    import concourse.bacc as bacc
    from concourse.bass_utils import run_bass_kernel_spmd as run

    nc = bacc.Bacc("TRN2", target_bir_lowering=False, num_devices=1)
    names = ["x", "L0_conv_coeff_real", "L0_conv_coeff_imag", "L0_conv_proj", "L2_conv_coeff_real",
             "L2_conv_coeff_imag", "L2_conv_proj", "L3_conv_weights"]
    data = {n: np.ascontiguousarray(inputs[n]) for n in names}
    for n in ("L0_conv_proj", "L2_conv_proj"):
        data[n] = np.ascontiguousarray(data[n].T)
    for n in names:
        if "coeff" in n:
            data[n] = np.ascontiguousarray(data[n].reshape(C, C, MQ, 4, M).transpose(2, 0, 3, 1, 4)
                                           .reshape(MQ, C, 4 * C * M))
    cw = np.asarray(inputs["L3_conv_conv_w"])
    blocks = np.zeros((P, 4, P), cw.dtype)
    for d in range(4):
        for b in range(P // C):
            blocks[b * C:(b + 1) * C, d, b * C:(b + 1) * C] = cw[:, d * C:(d + 1) * C].T
    data["L3_conv_conv_w"] = blocks
    data["L3_conv_conv_b"] = np.tile(np.asarray(inputs["L3_conv_conv_b"]), P // C).reshape(P, 1)
    data["consts"] = constant_table()
    arrays, ins = {}, []
    for n, a in data.items():
        arrays["in_" + n] = a
        ins.append(nc.dram_tensor("in_" + n, a.shape, F32, kind="ExternalInput").ap())
    out = nc.dram_tensor("out_0", (B, C, H, W), F32, kind="ExternalOutput").ap()
    build(nc, ins, [out])
    r = run(nc, [arrays], core_ids=[0])
    return r.results[0]["out_0"]
```

```python
from contextlib import ExitStack

import numpy as np
import concourse.bass as bass
from concourse import mybir

F32 = mybir.dt.float32
ALU = mybir.AluOpType
ACT = mybir.ActivationFunctionType
AX_X = mybir.AxisListType.X

B, C, H, W = 16, 32, 256, 256
P = 128
HB = H // P
M = 32
HW = H * W
GROUP = 2
CU = 8
KU = C // CU
MQ = M // 4
XF = MQ * 3 * M
EPS = 1e-5
GB = B * C // P
RR = 4
RF = 2

_widths = [("FR", HB * 2 * M), ("FI", HB * 2 * M), ("EW", W), ("EH0", H), ("EH1", H), ("EN0", H), ("EN1", H),
           ("D1", HB * 128), ("D2", HB * 64), ("D3", HB * 32), ("GM", P), ("ID", P)]
COL = {}
_at = 0
for _n, _w in _widths:
    COL[_n] = (_at, _at + _w)
    _at += _w
NCOL = _at


def constant_table():
    t = np.zeros((P, NCOL), np.float64)
    ang = 2 * np.pi * ((np.arange(H)[:, None] * np.arange(M)[None, :]) % H) / H
    c, s = np.cos(ang), np.sin(ang)

    def rows(a):
        return a.reshape(HB, P, -1).transpose(1, 0, 2).reshape(P, -1)

    def put(name, a):
        lo, hi = COL[name]
        t[:a.shape[0], lo:lo + a.shape[1]] = a

    put("FR", rows(np.concatenate([c, -s], 1)))
    put("FI", rows(np.concatenate([s, c], 1)))
    wj = np.where(np.arange(M) == 0, 1.0, 2.0)[:, None] / HW
    put("EW", np.concatenate([c.T * wj, -s.T * wj], 0))
    eh = np.concatenate([c.T, -s.T], 0)
    for e in range(2):
        half = np.zeros((P, H))
        half[e * 2 * M:(e + 1) * 2 * M] = eh
        put(f"EH{e}", half)
        put(f"EN{e}", -half)

    def down(n):
        a = np.zeros((n // 2, n))
        for i in range(n // 2):
            for d, v in ((-1, 0.25), (0, 0.5), (1, 0.25)):
                if 0 <= 2 * i + d < n:
                    a[i, 2 * i + d] = v
        return a
    a1 = down(H)
    a2 = down(H // 2) @ a1
    a3 = down(H // 4) @ a2
    put("D1", rows(a1.T / 4))
    put("D2", rows(a2.T / 16))
    put("D3", rows(a3.T / 64))
    grp = (np.arange(P) % C) // GROUP
    put("GM", (grp[:, None] == grp[None, :]).astype(np.float64))
    put("ID", np.eye(P))
    return t.astype(np.float32)


class Prog:

    def __init__(self, nc, ctx):
        self.nc, self.ctx = nc, ctx
        self.tab = ctx.enter_context(nc.sbuf_tensor("tab", [P, NCOL], F32))
        self.ones = ctx.enter_context(nc.sbuf_tensor("ones", [P, 1], F32))
        self.ps = ctx.enter_context(nc.psum_tensor("ps", [P, 8, 512], F32))

        self.consts_in = self.sem("consts_in")
        self.passed = {}

    @staticmethod
    def wait(eng, sem, value):
        if not (isinstance(value, int) and value <= 0):
            eng.wait_ge(sem, value)

    def hold(self, eng, sem, value):
        if eng not in self.passed:
            self.passed[eng] = self.sem(f"passed{len(self.passed)}")
        eng.wait_ge(sem, value)
        eng.sem_inc(self.passed[eng], 1)

    def sem(self, name):
        return self.ctx.enter_context(self.nc.semaphore(name))

    def t(self, name, rows=P):
        lo, hi = COL[name]
        return self.tab[0:rows, lo:hi]


def phase_gates(pg, consts, weights, gate_rows, gate_cols):
    nc = pg.nc
    with ExitStack() as mem:
        raw = mem.enter_context(nc.sbuf_tensor("g_raw", [P, 4, HB, W], F32))
        sg = mem.enter_context(nc.sbuf_tensor("g_sig", [P, 4, HB, W], F32))
        zero = mem.enter_context(nc.sbuf_tensor("g_zero", [1, W], F32))
        raw_in = pg.sem("g_raw_in")
        zeroed = pg.sem("g_zeroed")
        sig_done = pg.sem("g_sig_done")
        gates_out = pg.sem("g_gates_out")
        with nc.Block(name="gates") as block:
            @block.sync
            def _(sp):
                sp.dma_start(pg.tab[:, :], consts).then_inc(pg.consts_in, 16)
                for d in range(4):
                    sp.dma_start(raw[:, d], weights[d].rearrange("(n p) w -> p n w", p=P)).then_inc(raw_in, 16)
                pg.hold(sp, zeroed, 1)
                sp.dma_start(gate_rows[0, 0:1, :], zero[:, :]).then_inc(gates_out, 16)
                sp.dma_start(gate_rows[1, H:H + 1, :], zero[:, :]).then_inc(gates_out, 16)
                pg.hold(sp, sig_done, 1)
                sp.dma_start(gate_rows[0, 1:H + 1, :].rearrange("(n p) w -> p n w", p=P), sg[:, 0]).then_inc(gates_out, 16)
                sp.dma_start(gate_rows[1, 0:H, :].rearrange("(n p) w -> p n w", p=P), sg[:, 1]).then_inc(gates_out, 16)
                for d in range(2):
                    sp.dma_start(gate_cols[d].rearrange("(n p) w -> p n w", p=P), sg[:, 2 + d]).then_inc(gates_out, 16)
                pg.hold(sp, gates_out, 6 * 16)
                pg.hold(sp, pg.consts_in, 16)

            @block.vector
            def _(dve):
                nc.vector.memset(pg.ones[:, :], 1.0)
                nc.vector.memset(sg[:, 2, :, 0:1], 0.0)
                nc.vector.memset(sg[:, 3, :, W - 1:W], 0.0)
                nc.vector.memset(zero[:, :], 0.0).then_inc(zeroed, 1)

            @block.scalar
            def _(act):
                act.wait_ge(raw_in, 4 * 16)
                nc.scalar.activation(sg[:, 0:2], raw[:, 0:2], ACT.Sigmoid)
                nc.scalar.activation(sg[:, 2, :, 1:W], raw[:, 2, :, 0:W - 1], ACT.Sigmoid)
                nc.scalar.activation(sg[:, 3, :, 0:W - 1], raw[:, 3, :, 1:W], ACT.Sigmoid).then_inc(sig_done, 1)


class Forward:

    def __init__(self, pg, mem, name, row_blocks, col_blocks, row_banks, turn_banks, modes_bank, sq_ps):
        nc = pg.nc
        self.pg, self.nh, self.nw = pg, row_blocks, col_blocks
        self.row_banks, self.turn_banks, self.modes_bank, self.sq_ps = row_banks, turn_banks, modes_bank, sq_ps
        self.shared = row_banks == turn_banks
        self.width = col_blocks * P
        self.nb = CU * self.width // 1024
        self.t = [mem.enter_context(nc.sbuf_tensor(f"{name}_t{i}", [P, CU // 2, self.width], F32)) for i in range(2)]
        self.a1 = mem.enter_context(nc.sbuf_tensor(name + "_a1", [P, self.nw, 2 * M, C], F32))
        self.xf = mem.enter_context(nc.sbuf_tensor(name + "_xf", [P, MQ, 3, M], F32))
        self.sq = mem.enter_context(nc.sbuf_tensor(name + "_sq", [P, C // GROUP], F32))
        self.junk = [mem.enter_context(nc.sbuf_tensor(f"{name}_junk{i}", [P, HB, GROUP * W], F32)) for i in range(2)]
        self.sqrow = mem.enter_context(nc.sbuf_tensor(name + "_sqrow", [1, C // GROUP, GROUP], F32))
        self.rows_done = pg.sem(name + "_rows_done")
        self.rows_out = pg.sem(name + "_rows_out")
        self.turn_done = pg.sem(name + "_turn_done")
        self.turn_out = pg.sem(name + "_turn_out")
        self.sq_done = pg.sem(name + "_sq_done")
        self.modes_done = pg.sem(name + "_modes_done")
        self.modes_out = pg.sem(name + "_modes_out")
        self.xf_free = pg.sem(name + "_xf_free")
        self.stored = pg.sem(name + "_modes_stored")

    def rows_count(self, s, k):
        return s * (KU * self.nb) + (k + 1) * self.nb

    def turn_count(self, s, k):
        return s * (KU * self.nw) + (k + 1) * self.nw

    def sq_count(self, s, k):
        return s * (C // GROUP) + ((k + 1) * (CU // GROUP) + 2)

    def start(self, act):
        act.sem_inc(self.sq_done, 2)

    def pe_rows(self, pe, s, k, x):
        nc = self.pg.nc
        fr = self.pg.t("FR").rearrange("p (n m) -> p n m", n=HB)
        if self.shared:
            self.pg.wait(pe, self.turn_out, self.turn_count(s, k - 1))
            if k == 0:
                pe.wait_ge(self.modes_out, s + 1)
        per = 512 // self.width
        for n in range(self.nb):
            if not self.shared:
                self.pg.wait(pe, self.rows_out, self.rows_count(s, k - 1) - self.nb + n + 1)
            bank = self.pg.ps[:, self.row_banks[n]]
            for e in range(2):
                for hb in range(self.nh):
                    c0 = 2 * per * n + e
                    mm = nc.tensor.matmul(bank[e * 2 * M:(e + 1) * 2 * M, :], fr[:, hb, :],
                                          x(hb)[:, c0:c0 + 2 * per - 1:2, :],
                                          start=(hb == 0), stop=(hb == self.nh - 1))
            mm.then_inc(self.rows_done, 1)

    def act_rows(self, act, s, k):
        nc = self.pg.nc
        self.pg.wait(act, self.turn_done, self.turn_count(s, k - 2))
        per = 512 // self.width
        for n in range(self.nb):
            act.wait_ge(self.rows_done, self.rows_count(s, k) - self.nb + n + 1)
            nc.scalar.copy(self.t[k % 2][:, per * n:per * (n + 1), :].rearrange("p q w -> p (q w)"),
                           self.pg.ps[:, self.row_banks[n]]).then_inc(self.rows_out, 1)

    def pe_turn(self, pe, s, k):
        nc = self.pg.nc
        pe.wait_ge(self.rows_out, self.rows_count(s, k))
        for wb in range(self.nw):
            if not self.shared:
                self.pg.wait(pe, self.turn_out, self.turn_count(s, k - 1) - self.nw + wb + 1)
            for q in range(CU // 2):
                mm = nc.tensor.transpose(self.pg.ps[:, self.turn_banks[wb], q * P:(q + 1) * P],
                                         self.t[k % 2][:, q, wb * P:(wb + 1) * P], self.pg.t("ID"))
            mm.then_inc(self.turn_done, 1)

    def act_turn(self, act, s, k):
        nc = self.pg.nc
        if k == 0:
            act.wait_ge(self.modes_done, s + 1)
        for wb in range(self.nw):
            act.wait_ge(self.turn_done, self.turn_count(s, k) - self.nw + wb + 1)
            bank = self.pg.ps[:, self.turn_banks[wb]].rearrange("p (c m) -> p c m", c=CU)
            dst = self.a1[:, wb, :, k * CU:(k + 1) * CU].rearrange("p m c -> p c m")
            nc.scalar.copy(dst, bank).then_inc(self.turn_out, 1)

    def pe_modes(self, pe, s):
        nc = self.pg.nc
        fr = self.pg.t("FR").rearrange("p (n m) -> p n m", n=HB)
        fi = self.pg.t("FI").rearrange("p (n m) -> p n m", n=HB)
        pe.wait_ge(self.turn_out, self.turn_count(s, KU - 1))
        pe.wait_ge(self.sq_done, self.sq_count(s, KU - 1))
        pe.wait_ge(self.modes_out, s + 1)
        bank = self.pg.ps[:, self.modes_bank].rearrange("p (q m) -> p q m", q=MQ)
        for iq in range(MQ):
            n = 0
            for wb in range(self.nw):
                for ri, f in ((0, fr), (1, fi)):
                    i0 = ri * M + 4 * iq
                    nc.tensor.matmul(bank[:, iq, :], self.a1[:, wb, i0:i0 + 4, :], f[:, wb, :],
                                     start=(n == 0), stop=(n == 2 * self.nw - 1))
                    n += 1
        nc.tensor.matmul(self.sq_ps, self.pg.ones[:, :], self.sq[:, :], start=True, stop=True).then_inc(self.modes_done, 1)

    def act_squares(self, act, s, k, x):
        nc = self.pg.nc
        if k == 0:
            act.wait_ge(self.modes_done, s + 1)
        for g in range(CU // GROUP):
            src = x[:, :, g * GROUP:(g + 1) * GROUP, :].rearrange("p n c w -> p n (c w)")
            at = k * (CU // GROUP) + g
            act.wait_ge(self.sq_done, s * (C // GROUP) + (at + 1))
            nc.scalar.activation(self.junk[at % 2][:, :, :], src, ACT.Square, accum_out=self.sq[:, at:at + 1]
                                 ).then_inc(self.sq_done, 1)

    def dve_sample(self, dve, s):
        nc = self.pg.nc
        dve.wait_ge(self.modes_done, s + 2)
        dve.wait_ge(self.xf_free, s + 1)
        bank = self.pg.ps[:, self.modes_bank].rearrange("p (q r m) -> p q r m", q=MQ, r=2)
        nc.vector.tensor_copy(self.xf[:, :, 1:3, :], bank)
        nc.vector.tensor_scalar(self.xf[:, :, 0, :], bank[:, :, 1, :], -1.0, None, ALU.mult)
        nc.vector.tensor_copy(self.sqrow[:, :, :], self.sq_ps.unsqueeze(2).to_broadcast([1, C // GROUP, GROUP])
                              ).then_inc(self.modes_out, 1)

    def pool_sample(self, pool, s, modes, sumsq):
        pool.wait_ge(self.modes_out, s + 2)
        pool.dma_start(modes[bass.ds(s, 1)].rearrange("b p f -> p (b f)"),
                       self.xf[:, :, :, :].rearrange("p q r m -> p (q r m)")).then_inc(self.stored, 16)
        pool.dma_start(sumsq[bass.ds(s, 1), :], self.sqrow[:, :, :].rearrange("o g e -> o (g e)")
                       ).then_inc(self.stored, 16)
        pool.wait_ge(self.stored, s * 32 + 32)
        pool.sem_inc(self.xf_free, 1)


def unit_rows(img, s, k, hb):
    return img[bass.ds(s, 1), k * CU:(k + 1) * CU, hb * P:(hb + 1) * P, :].rearrange("b c p w -> p (b c) w")


def phase_forward(pg, x, modes, sumsq):
    nc = pg.nc
    with ExitStack() as mem:
        slot = [mem.enter_context(nc.sbuf_tensor(f"a_x{k}", [P, HB, CU, W], F32)) for k in range(KU)]
        loaded = [pg.sem(f"a_loaded{k}") for k in range(KU)]
        fw = Forward(pg, mem, "a", HB, 2, (0, 1), (2, 3), 4, pg.ps[96:97, 5, 0:C // GROUP])

        def before(s, k):
            return (s, k - 1) if k else (s - 1, KU - 1)

        with nc.Block(name="forward") as block:
            @block.sync
            def _(sp):
                def load(s, k):
                    for hb in range(HB):
                        sp.dma_start(slot[k][:, hb], unit_rows(x, s, k, hb)).then_inc(loaded[k], 16)
                for k in range(KU):
                    load(0, k)
                with sp.Fori(1, B) as s:
                    for k in range(KU):
                        pg.hold(sp, fw.rows_done, fw.rows_count(s, k - KU))
                        pg.hold(sp, fw.sq_done, fw.sq_count(s, k - KU))
                        load(s, k)

            @block.tensor
            def _(pe):
                def body(s, first=False):
                    for k in range(KU):
                        pe.wait_ge(loaded[k], s * 32 + 32)
                        fw.pe_rows(pe, s, k, lambda hb: slot[k][:, hb])
                        if not (first and k == 0):
                            fw.pe_turn(pe, *before(s, k))
                            if k == 0:
                                fw.pe_modes(pe, s - 1)
                pe.sem_inc(fw.modes_done, 1)
                body(0, first=True)
                with pe.Fori(1, B) as s:
                    body(s)
                fw.pe_turn(pe, B - 1, KU - 1)
                fw.pe_modes(pe, B - 1)

            @block.scalar
            def _(act):
                def body(s, first=False):
                    for k in range(KU):
                        act.wait_ge(loaded[k], s * 32 + 32)
                        fw.act_rows(act, s, k)
                        if not (first and k == 0):
                            fw.act_turn(act, *before(s, k))
                        fw.act_squares(act, s, k, slot[k])
                fw.start(act)
                body(0, first=True)
                with act.Fori(1, B) as s:
                    body(s)
                fw.act_turn(act, B - 1, KU - 1)

            @block.vector
            def _(dve):
                dve.sem_inc(fw.modes_out, 1)
                with dve.Fori(0, B) as s:
                    fw.dve_sample(dve, s)

            @block.gpsimd
            def _(pool):
                pool.sem_inc(fw.xf_free, 1)
                with pool.Fori(0, B) as s:
                    fw.pool_sample(pool, s, modes, sumsq)
                pool.wait_ge(fw.stored, B * 32)


def phase_mix(pg, name, modes, sumsq, coef, projT, sx, stats, base_out=None, prior=None):
    nc = pg.nc
    NF = HW * GROUP
    with ExitStack() as mem:
        def sb(n, shape):
            return mem.enter_context(nc.sbuf_tensor(name + n, shape, F32))
        X = sb("_x", [P, B, MQ, 3, M])
        S = sb("_s", [P, B, MQ, 3, M])
        cf = [sb(f"_cf{i}", [M, 4 * C, M]) for i in range(2)]
        BD = [sb(f"_bd{i}", [P, 2, M, P]) for i in range(2)]
        pj = sb("_pj", [M, C])
        v = sb("_v", [P, 16, B])
        st = sb("_st", [P, B, 4])
        tot, mean, var, rs, t0, t1, t2, qs, qc, cs, cc, em, m1, v1, t3, rel = [v[:, n, :] for n in range(16)]
        pr = sb("_pr", [P, 2, B])

        x_in, sq_in, pj_in = pg.sem(name + "_x_in"), pg.sem(name + "_sq_in"), pg.sem(name + "_pj_in")
        cf_in = [pg.sem(f"{name}_cf_in{i}") for i in range(2)]
        base_in = pg.sem(name + "_base_in")
        joined = pg.sem(name + "_joined")
        base_done, base_stored = pg.sem(name + "_base_done"), pg.sem(name + "_base_stored")
        dc_done = pg.sem(name + "_dc_done")
        chain = pg.sem(name + "_dve_chain")
        var_ready = pg.sem(name + "_var_ready")
        sums_ready = pg.sem(name + "_sums_ready")
        root_done = pg.sem(name + "_root_done")
        normed = pg.sem(name + "_normed")
        zeroed = pg.sem(name + "_zeroed")
        w_done = pg.sem(name + "_w_done")
        w_out_act, w_out_dve = pg.sem(name + "_w_out_act"), pg.sem(name + "_w_out_dve")
        mix_done = pg.sem(name + "_mix_done")
        mix_out = pg.sem(name + "_mix_out")
        sums_done = pg.sem(name + "_sums_done")
        s_final = pg.sem(name + "_s_final")
        tr_done = pg.sem(name + "_tr_done")
        tr_out_act, tr_out_dve = pg.sem(name + "_tr_out_act"), pg.sem(name + "_tr_out_dve")
        sx_out = pg.sem(name + "_sx_out")
        st_out = pg.sem(name + "_st_out")
        ident = pg.t("ID")
        gm = pg.t("GM")
        chunks = [(iq, ri) for iq in range(MQ) for ri in range(2)]
        SX = [BD[i][0:2 * M, 0, 0:16, :].rearrange("p a b -> p (a b)").rearrange(
            "p (c r m) -> p c r m", c=C, r=2) for i in range(2)]
        prod = BD[0][:, :, :, :].rearrange("p r m c -> p (r m c)").rearrange(
            "p (b q r m) -> p b q r m", b=B, q=MQ, r=2)

        with nc.Block(name=name) as block:
            @block.sync
            def _(sp):
                sp.dma_start(pj[:, :], projT).then_inc(pj_in, 16)
                for i4 in range(4):
                    with nc.allow_non_contiguous_dma(reason="512 words"):
                        sp.dma_start(tot[i4 * C:(i4 + 1) * C, :], sumsq.rearrange("b c -> c b")).then_inc(sq_in, 16)
                if prior:
                    sp.dma_start(S[:].rearrange("p b q r m -> p b (q r m)"),
                                 prior[0].rearrange("b p f -> p b f")).then_inc(base_in, 16)
                    for i4 in range(4):
                        for j in range(2):
                            with nc.allow_non_contiguous_dma(reason="512 words"):
                                sp.dma_start(pr[i4 * C:(i4 + 1) * C, j, :],
                                             prior[1][:, j, :].rearrange("b c -> c b")).then_inc(base_in, 16)
                sp.dma_start(X[:].rearrange("p b q r m -> p b (q r m)"),
                             modes.rearrange("b p f -> p b f")).then_inc(x_in, 16)
                for n, (iq, ri) in enumerate(chunks):
                    if n >= 2:
                        pg.hold(sp, w_done, 2 * (n - 1))
                    sp.dma_start(cf[n % 2][:, :, :].rearrange("p m j -> p (m j)"), coef[ri][iq]).then_inc(cf_in[n % 2], 16)
                pg.hold(sp, s_final, 1)
                with nc.allow_non_contiguous_dma(reason="a few words per channel"):
                    sp.dma_start(stats.rearrange("b k c -> c (b k)"),
                                 st[0:C].rearrange("p b k -> p (b k)")).then_inc(st_out, 16)
                for b in range(B):
                    pg.hold(sp, tr_out_act, 2 * (b + 1))
                    pg.hold(sp, tr_out_dve, 2 * (b + 1))
                    sp.dma_start(sx[b], SX[b % 2].rearrange("p c r m -> p (c r m)")).then_inc(sx_out, 16)
                    pg.hold(sp, sx_out, 16 * (b + 1))
                if base_out is not None:
                    pg.hold(sp, base_done, 1)
                    sp.dma_start(base_out.rearrange("b p f -> p b f"), X[:].rearrange("p b q r m -> p b (q r m)")
                                 ).then_inc(base_stored, 16)
                    pg.hold(sp, base_stored, 16)
                pg.hold(sp, st_out, 16)

            @block.tensor
            def _(pe):
                pe.wait_ge(*((joined, 1) if prior else (x_in, 16)))
                dc = pg.ps[:, 7, 0:B]
                nc.tensor.matmul(dc, gm[0:C, :], X[0:C, :, 0, 1, 0], start=True, stop=True).then_inc(dc_done, 1)
                pe.wait_ge(pj_in, 16)

                def weights(n):
                    pe.wait_ge(cf_in[n % 2], 16 * (n // 2 + 1))
                    for jh in range(2):
                        if n >= 2:
                            pe.wait_ge(w_out_act, 2 * (n - 2) + jh + 1)
                            pe.wait_ge(w_out_dve, 2 * (n - 2) + jh + 1)
                        bank = pg.ps[:, 2 * (n % 2) + jh].rearrange("p (j o) -> p j o", j=M // 2)
                        for j in range(M // 2):
                            mm = nc.tensor.matmul(bank[:, j, :], cf[n % 2][:, :, jh * 16 + j], pj[:, :],
                                                  start=True, stop=True)
                        mm.then_inc(w_done, 1)

                def mix(iq):
                    pe.wait_ge(w_out_act, 4 * (iq + 1))
                    pe.wait_ge(w_out_dve, 4 * (iq + 1))
                    if iq == 0:
                        pe.wait_ge(normed, 1)
                    for jh in range(2):
                        if iq >= 1:
                            pe.wait_ge(mix_out, 2 * (iq - 1) + jh + 1)
                        bank = pg.ps[:, 4 + jh].rearrange("p (j n) -> p j n", j=M // 2)
                        for j in range(M // 2):
                            jj = jh * 16 + j
                            for ri in range(2):
                                rhs = X[:, :, iq, 1 - ri:3 - ri, jj].rearrange("p b r -> p r b")
                                mm = nc.tensor.matmul(bank[:, j, :], BD[iq % 2][:, ri, jj, :], rhs,
                                                      start=(ri == 0), stop=(ri == 1))
                        mm.then_inc(mix_done, 1)
                weights(0)
                weights(1)
                for iq in range(MQ):
                    if iq + 1 < MQ:
                        weights(2 * iq + 2)
                        weights(2 * iq + 3)
                    mix(iq)
                pe.wait_ge(sums_ready, 1)
                for n, a in enumerate((qs, cs)):
                    mm = nc.tensor.matmul(pg.ps[:, 7, (n + 1) * B:(n + 2) * B], gm, a, start=True, stop=True)
                mm = nc.tensor.matmul(pg.ps[:, 7, 3 * B:4 * B], gm[0:C, :], S[0:C, :, 0, 0, 0], start=True, stop=True)
                mm.then_inc(sums_done, 1)
                pe.wait_ge(s_final, 1)
                for b in range(B):
                    for half in range(2):
                        if b >= 1:
                            pe.wait_ge(tr_out_act, 2 * (b - 1) + half + 1)
                            pe.wait_ge(tr_out_dve, 2 * (b - 1) + half + 1)
                        for r in range(2):
                            for q in range(4):
                                iq = half * 4 + q
                                mm = nc.tensor.transpose(
                                    pg.ps[0:2 * M, 2 * half + r, q * P:(q + 1) * P],
                                    S[:, b, iq, r:r + 2, :].rearrange("p r m -> p (r m)"), ident)
                        mm.then_inc(tr_done, 1)

            def evacuate_weights(eng, copy, out_sem, quads, with_mix):
                for n, (iq, ri) in enumerate(chunks):
                    for jh in range(2):
                        eng.wait_ge(w_done, 2 * n + jh + 1)
                        if n == 0 and jh == 0:
                            eng.wait_ge(zeroed, 1)
                        if iq >= 2 and ri == 0 and jh == 0:
                            eng.wait_ge(mix_done, 2 * (iq - 1))
                        bank = pg.ps[:, 2 * (n % 2) + jh].rearrange("p (j o) -> p j o", j=M // 2)
                        for i4 in quads:
                            r0 = i4 * C
                            op = copy(BD[iq % 2][r0:r0 + C, ri, jh * 16:(jh + 1) * 16, r0:r0 + C],
                                      bank[r0:r0 + C])
                        op.then_inc(out_sem, 1)
                    if with_mix and iq >= 1 and ri == 1:
                        evacuate_mix(eng, iq - 1)
                if with_mix:
                    evacuate_mix(eng, MQ - 1)

            def evacuate_mix(dve, iq):
                for jh in range(2):
                    dve.wait_ge(mix_done, 2 * iq + jh + 1)
                    bank = pg.ps[:, 4 + jh].rearrange("p (j r b) -> p r b j", j=M // 2, r=2)
                    js = slice(jh * 16, (jh + 1) * 16)
                    for r in range(2):
                        nc.vector.tensor_copy(S[:, :, iq, r, js], bank[:, r])
                    nc.vector.tensor_scalar(S[:, :, iq, 2, js], bank[:, 0], -1.0, None, ALU.mult).then_inc(mix_out, 1)

            @block.scalar
            def _(act):
                act.wait_ge(var_ready, 1)
                nc.scalar.activation(t1, var, ACT.Sqrt).then_inc(root_done, 1)
                evacuate_weights(act, nc.scalar.copy, w_out_act, (0, 1), False)
                act.wait_ge(var_ready, 2)
                nc.scalar.activation(t1, v1, ACT.Sqrt).then_inc(root_done, 1)
                for b in range(B):
                    for half in range(2):
                        act.wait_ge(tr_done, 2 * b + half + 1)
                        if half == 0 and b >= 2:
                            act.wait_ge(sx_out, 16 * (b - 1))
                        src = pg.ps[0:2 * M, 2 * half].rearrange("p (i o) -> p i o", i=16)
                        dst = SX[b % 2][:, :, 0, half * 16:(half + 1) * 16].rearrange("p c i -> p i c")
                        nc.scalar.copy(dst, src).then_inc(tr_out_act, 1)

            @block.vector
            def _(dve):
                done = [0]

                def signal(op, sem, value):
                    op.then_inc(sem, 1)
                    dve.wait_ge(sem, value)

                def link(op):
                    done[0] += 1
                    op.then_inc(chain, 1)
                    dve.wait_ge(chain, done[0])

                def inv_root(out, root, variance):
                    link(nc.vector.reciprocal(out, root))
                    link(nc.vector.tensor_tensor(t2, out, out, ALU.mult))
                    link(nc.vector.tensor_tensor(t2, t2, variance, ALU.mult))
                    link(nc.vector.tensor_scalar(t2, t2, -0.5, 1.5, ALU.mult, ALU.add))
                    link(nc.vector.tensor_tensor(out, out, t2, ALU.mult))

                dc = pg.ps[:, 7, 0:B]
                nc.vector.memset(BD[0][:], 0.0)
                nc.vector.memset(BD[1][:], 0.0).then_inc(zeroed, 1)
                link(nc.vector.memset(st[:], 0.0))
                if prior:
                    dve.wait_ge(x_in, 16)
                    dve.wait_ge(base_in, 16 * 9)
                    for b in range(B):
                        xb, sb_ = (a[:, b].rearrange("p q r m -> p (q r m)") for a in (X, S))
                        op = nc.vector.scalar_tensor_tensor(xb, xb, pr[:, 1, b:b + 1], sb_, ALU.mult, ALU.add)
                    signal(op, joined, 1)
                dve.wait_ge(sq_in, 64)
                dve.wait_ge(dc_done, 1)
                link(nc.vector.tensor_scalar(rel, dc, 1.0 / NF, None, ALU.mult))
                link(nc.vector.tensor_tensor(mean, rel, pr[:, 0, :], ALU.add) if prior
                     else nc.vector.tensor_copy(mean, rel))
                link(nc.vector.tensor_tensor(t0, mean, mean, ALU.mult))
                link(nc.vector.tensor_scalar(tot, tot, 1.0 / NF, None, ALU.mult))
                link(nc.vector.tensor_tensor(tot, tot, t0, ALU.subtract))
                signal(nc.vector.tensor_scalar(var, tot, EPS, None, ALU.add), var_ready, 1)
                dve.wait_ge(root_done, 1)
                inv_root(rs, t1, var)
                link(nc.vector.tensor_scalar(t0, rel, float(HW), None, ALU.mult))
                dve.wait_ge(x_in, 16)
                x00 = X[0:C, :, 0, 1, 0]
                link(nc.vector.tensor_tensor(x00, x00, t0[0:C], ALU.subtract))
                for b in range(B):
                    xb = X[:, b].rearrange("p q r m -> p (q r m)")
                    op = nc.vector.tensor_scalar(xb, xb, rs[:, b:b + 1], None, ALU.mult)
                op.then_inc(normed, 1)
                evacuate_weights(dve, nc.vector.tensor_copy, w_out_dve, (2, 3), True)

                dve.wait_ge(mix_out, 2 * MQ)
                dve.wait_ge(mix_done, 2 * MQ)
                link(nc.vector.memset(S[0:C, :, 0, 1, 0], 0.0))
                for a, total, col0 in ((X[:, :, :, 1:3, :], qs, qc), (S[:, :, :, 0:2, :], cs, cc)):
                    for b in range(B):
                        op = nc.vector.tensor_tensor(prod[:, b], a[:, b], S[:, b, :, 0:2, :], ALU.mult)
                    link(op)
                    link(nc.vector.tensor_reduce(total, prod[:].rearrange("p b q r m -> p b (q r m)"), AX_X, ALU.add))
                    link(nc.vector.tensor_reduce(col0, prod[:, :, :, :, 0].rearrange("p b q r -> p b (q r)"), AX_X, ALU.add))
                link(nc.vector.scalar_tensor_tensor(qs, qs, 2.0, qc, ALU.mult, ALU.subtract))
                link(nc.vector.tensor_scalar(cc, cc, 1.5, None, ALU.mult))
                link(nc.vector.scalar_tensor_tensor(cs, cs, 2.0, cc, ALU.mult, ALU.subtract))
                s00 = S[0:C, :, 0, 0, 0]
                link(nc.vector.tensor_tensor(t0[0:C], s00, s00, ALU.mult))
                signal(nc.vector.scalar_tensor_tensor(cs[0:C], t0[0:C], 0.5, cs[0:C], ALU.mult, ALU.add),
                       sums_ready, 1)
                dve.wait_ge(sums_done, 1)
                link(nc.vector.tensor_tensor(t0, var, rs, ALU.mult))
                link(nc.vector.tensor_tensor(t0, t0, pg.ps[:, 7, B:2 * B], ALU.mult))
                link(nc.vector.tensor_scalar(t0, t0, 2.0, None, ALU.mult))
                link(nc.vector.tensor_tensor(t0, t0, pg.ps[:, 7, 2 * B:3 * B], ALU.add))
                link(nc.vector.tensor_scalar(t0, t0, 1.0 / (float(HW) * NF), None, ALU.mult))
                link(nc.vector.tensor_tensor(v1, t0, tot, ALU.add))
                link(nc.vector.tensor_scalar(em, pg.ps[:, 7, 3 * B:4 * B], 1.0 / NF, None, ALU.mult))
                link(nc.vector.tensor_tensor(m1, mean, em, ALU.add))
                link(nc.vector.tensor_tensor(em, em, em, ALU.mult))
                link(nc.vector.tensor_tensor(v1, v1, em, ALU.subtract))
                signal(nc.vector.tensor_scalar(v1, v1, EPS, None, ALU.add), var_ready, 2)
                dve.wait_ge(root_done, 2)
                inv_root(t3, t1, v1)
                nc.vector.tensor_copy(st[:, :, 0], m1)
                nc.vector.tensor_copy(st[:, :, 1], t3)
                nc.vector.tensor_scalar(st[:, :, 2], t3, 1.0, None, ALU.add)
                if base_out is not None:
                    link(nc.vector.tensor_tensor(t0, var, rs, ALU.mult))
                    for b in range(B):
                        op = nc.vector.scalar_tensor_tensor(X[:, b, :, 1:3, :], X[:, b, :, 1:3, :], t0[:, b:b + 1],
                                                            S[:, b, :, 0:2, :], ALU.mult, ALU.add)
                    link(op)
                    link(nc.vector.scalar_tensor_tensor(
                        X[:, :, :, 1:3, 0].rearrange("p b q r -> p (b q) r"),
                        S[:, :, :, 0:2, 0].rearrange("p b q r -> p (b q) r"), -0.5,
                        X[:, :, :, 1:3, 0].rearrange("p b q r -> p (b q) r"), ALU.mult, ALU.add))
                    link(nc.vector.scalar_tensor_tensor(x00, s00, 0.5, x00, ALU.mult, ALU.add))
                    link(nc.vector.tensor_tensor(t0, m1, mean, ALU.subtract))
                    link(nc.vector.tensor_scalar(t0, t0, float(HW), None, ALU.mult))
                    link(nc.vector.tensor_tensor(x00, x00, t0[0:C], ALU.subtract))
                    link(nc.vector.tensor_scalar(t2, t3, 1.0, None, ALU.add))
                    for b in range(B):
                        op = nc.vector.tensor_scalar(X[:, b, :, 1:3, :], X[:, b, :, 1:3, :], t2[:, b:b + 1], None,
                                                     ALU.mult)
                    link(op)
                    nc.vector.tensor_scalar(X[:, :, :, 0, :].rearrange("p b q m -> p (b q) m"),
                                            X[:, :, :, 2, :].rearrange("p b q m -> p (b q) m"), -1.0, None, ALU.mult
                                            ).then_inc(base_done, 1)
                link(nc.vector.tensor_scalar(t0, m1, float(HW), None, ALU.mult))
                nc.vector.tensor_tensor(s00, s00, t0[0:C], ALU.subtract)
                s00n = S[0:C, :, 0, 2, 0]
                nc.vector.tensor_tensor(s00n, s00n, t0[0:C], ALU.add).then_inc(s_final, 1)
                for b in range(B):
                    for half in range(2):
                        dve.wait_ge(tr_done, 2 * b + half + 1)
                        if half == 0 and b >= 2:
                            dve.wait_ge(sx_out, 16 * (b - 1))
                        src = pg.ps[0:2 * M, 2 * half + 1].rearrange("p (i o) -> p i o", i=16)
                        dst = SX[b % 2][:, :, 1, half * 16:(half + 1) * 16].rearrange("p c i -> p i c")
                        nc.vector.tensor_copy(dst, src).then_inc(tr_out_dve, 1)


class Inverse:
    VB, YB = 2, 2
    NY = CU

    def __init__(self, pg, mem, name):
        nc = pg.nc
        self.pg = pg
        self.slot = [mem.enter_context(nc.sbuf_tensor(f"{name}_x{k}", [P, HB, CU, W], F32)) for k in range(KU)]
        self.sxs = [mem.enter_context(nc.sbuf_tensor(f"{name}_sx{k}", [2 * M, CU, 2 * M], F32)) for k in range(KU)]
        self.v = [mem.enter_context(nc.sbuf_tensor(f"{name}_v{i}", [P, CU // 2, W], F32)) for i in range(2)]
        self.loaded = [pg.sem(f"{name}_loaded{k}") for k in range(KU)]
        self.v_done = pg.sem(name + "_v_done")
        self.v_out = pg.sem(name + "_v_out")
        self.y_done = pg.sem(name + "_y_done")
        self.y_out = pg.sem(name + "_y_out")

    def load(self, sp, src, sx, s, k):
        for hb in range(HB):
            sp.dma_start(self.slot[k][:, hb], unit_rows(src, s, k, hb)).then_inc(self.loaded[k], 16)
        sp.dma_start(self.sxs[k][:, :, :].rearrange("p c m -> p (c m)"),
                     sx[bass.ds(s, 1), :, k * CU * 2 * M:(k + 1) * CU * 2 * M].rearrange("b p f -> p (b f)")
                     ).then_inc(self.loaded[k], 16)

    def pe_v(self, pe, s, k, loads):
        nc = self.pg.nc
        pe.wait_ge(self.loaded[k], s * (16 * loads) + 16 * loads)
        for n in range(2):
            pe.wait_ge(self.v_out, s * 8 + (2 * k + n + 1))
            for q in range(2):
                c = 4 * n + 2 * q
                mm = nc.tensor.matmul(self.pg.ps[:, n, q * W:(q + 1) * W],
                                      self.sxs[k][:, c:c + 2, :].rearrange("p c m -> p (c m)"),
                                      self.pg.t("EW", 2 * M), start=True, stop=True)
            mm.then_inc(self.v_done, 1)

    def act_v(self, act, s, k):
        nc = self.pg.nc
        self.pg.wait(act, self.y_done, s * 32 + (8 * k - 8))
        for n in range(2):
            act.wait_ge(self.v_done, s * 8 + (2 * k + n + 1))
            nc.scalar.copy(self.v[k % 2][:, 2 * n:2 * n + 2, :].rearrange("p q w -> p (q w)"), self.pg.ps[:, n]
                           ).then_inc(self.v_out, 1)

    @staticmethod
    def parts():
        return [(4 * n + 2 * e + hb, n, e, hb) for n in range(2) for e in range(2) for hb in range(HB)]

    def pe_y(self, pe, s, k, table):
        nc = self.pg.nc
        for at, n, e, hb in self.parts():
            if e == 0 and hb == 0:
                pe.wait_ge(self.v_out, s * 8 + (2 * k + n + 1 + self.VB))
            pe.wait_ge(self.y_out, s * 32 + (8 * k + at + 1))
            nc.tensor.matmul(self.pg.ps[:, 2 + at % 2], self.pg.t(f"{table}{e}")[:, hb * P:(hb + 1) * P],
                             self.v[k % 2][:, 2 * n:2 * n + 2, :].rearrange("p q w -> p (q w)"),
                             start=True, stop=True).then_inc(self.y_done, 1)

    def dve_y(self, dve, s, k, op, loads):
        nc = self.pg.nc
        dve.wait_ge(self.loaded[k], s * (16 * loads) + 16 * loads)
        for at, n, e, hb in self.parts():
            dve.wait_ge(self.y_done, s * 32 + (8 * k + at + 1))
            bank = self.pg.ps[:, 2 + at % 2].rearrange("p (q w) -> p q w", q=2)
            xs = self.slot[k][:, hb, 4 * n + e:4 * n + e + 3:2, :]
            nc.vector.tensor_tensor(xs, bank, xs, op).then_inc(self.y_out, 1)


def phase_wavelet(pg, x, sx, stats, x2, modes, sumsq):
    nc = pg.nc
    LOADS = 4
    Q, Q2, Q3 = W // 2, W // 4, W // 8
    with ExitStack() as mem:
        def sb(n, shape):
            return mem.enter_context(nc.sbuf_tensor("b_" + n, shape, F32))
        iv = Inverse(pg, mem, "b")
        fw = Forward(pg, mem, "bf", 1, 1, (7,), (7,), 7, pg.ps[96:97, 6, 0:C // GROUP])
        stt = [sb(f"st{k}", [P, 4, CU]) for k in range(KU)]
        odd = sb("odd", [P, HB, CU, Q])
        f1 = sb("f1", [P, HB * CU, Q + 1])
        f2 = sb("f2", [P, HB * CU, Q2 + 1])
        f3 = sb("f3", [P, HB * CU, Q3])
        down = [sb(f"down{i}", [P, CU, Q]) for i in range(2)]
        zero_cols = pg.sem("b_zero_cols")
        odd1, edge1, odd2, odd3 = (pg.sem("b_" + n) for n in ("odd1", "edge1", "odd2", "odd3"))
        f1_done, f2_done, f3_done = (pg.sem("b_" + n) for n in ("f1_done", "f2_done", "f3_done"))
        d_done = pg.sem("b_d_done")
        d_out = pg.sem("b_d_out")
        scaled = pg.sem("b_scaled")
        d_diff = pg.sem("b_d_diff")
        x2_done = pg.sem("b_x2_done")
        x2_out = [pg.sem(f"b_x2_out{k}") for k in range(KU)]
        R = [iv.slot[k] for k in range(KU)]

        with nc.Block(name="wavelet") as block:
            @block.sync
            def _(sp):
                def load(s, k):
                    iv.load(sp, x, sx, s, k)
                    sp.dma_start(stt[k][:, :, :], stats[bass.ds(s, 1), :, k * CU:(k + 1) * CU].to_broadcast(
                        [P, 4, CU])).then_inc(iv.loaded[k], 16)

                def body(s, first, last):
                    for k in range(KU):
                        pg.hold(sp, x2_done, s * KU + (k + 1))
                        for hb in range(HB):
                            sp.dma_start(unit_rows(x2, s, k, hb), iv.slot[k][:, hb]).then_inc(x2_out[k], 16)
                        if k == 0 and first:
                            continue
                        j = (k - 1) % KU
                        if last and k > 0:
                            continue
                        s_old = s - 1 if k == 0 else s
                        pg.hold(sp, x2_out[j], s_old * 32 + 32)
                        pg.hold(sp, fw.sq_done, fw.sq_count(s_old, j))
                        load(s_old + 1, j)
                for k in range(KU):
                    load(0, k)
                body(0, True, False)
                with sp.Fori(1, B - 1) as s:
                    body(s, False, False)
                body(B - 1, False, True)
                for k in range(KU):
                    pg.hold(sp, x2_out[k], B * 32)

            @block.tensor
            def _(pe):
                f1v = f1[:, :, 1:Q + 1].rearrange("p (n c) w -> p n c w", n=HB)
                f2v = f2[:, :, 1:Q2 + 1].rearrange("p (n c) w -> p n c w", n=HB)
                f3v = f3[:, :, :].rearrange("p (n c) w -> p n c w", n=HB)
                d1 = pg.t("D1").rearrange("p (n m) -> p n m", n=HB)
                d2 = pg.t("D2").rearrange("p (n m) -> p n m", n=HB)
                d3 = pg.t("D3").rearrange("p (n m) -> p n m", n=HB)

                def pyramid(s, k):
                    pe.wait_ge(f1_done, s * KU + (k + 1))
                    pg.wait(pe, d_out, s * KU + k)
                    for half in range(2):
                        bank = pg.ps[:, 4 + half].rearrange("p (c w) -> p c w", c=4)
                        for hb in range(HB):
                            mm = nc.tensor.matmul(bank, d1[:, hb, :], f1v[:, hb, 4 * half:4 * half + 4, :],
                                                  start=(hb == 0), stop=(hb == HB - 1))
                        mm.then_inc(d_done, 1)
                    pe.wait_ge(f2_done, s * KU + (k + 1))
                    pe.wait_ge(f3_done, s * KU + (k + 1))
                    for bank, dm, f, n in ((pg.ps[0:64, 6], d2, f2v, Q2), (pg.ps[64:96, 6], d3, f3v, Q3)):
                        out = bank[:, 0:CU * n].rearrange("p (c w) -> p c w", c=CU)
                        for hb in range(HB):
                            mm = nc.tensor.matmul(out, dm[:, hb, :], f[:, hb, :, :], start=(hb == 0), stop=(hb == HB - 1))
                        mm.then_inc(d_done, 1)

                def body(s, first=False, last=False):
                    for k in range(KU):
                        prev = (s, k - 1) if k > 0 else (s - 1, KU - 1)
                        nxt = (s, k + 1) if k + 1 < KU else (s + 1, 0)
                        more = not (last and k == KU - 1)
                        if more:
                            iv.pe_v(pe, *nxt, LOADS)
                            iv.pe_y(pe, *nxt, "EH")
                        if not (first and k == 0):
                            pe.wait_ge(d_diff, s * KU + k)
                            fw.pe_rows(pe, *prev, lambda hb: down[(k + 1) % 2][:, :, :])
                        pyramid(s, k)
                        if not (first and k == 0):
                            fw.pe_turn(pe, *prev)
                            if k == 0:
                                fw.pe_modes(pe, s - 1)
                pe.sem_inc(fw.modes_done, 1)
                iv.pe_v(pe, 0, 0, LOADS)
                iv.pe_y(pe, 0, 0, "EH")
                body(0, first=True)
                with pe.Fori(1, B - 1) as s:
                    body(s)
                body(B - 1, last=True)
                pe.wait_ge(d_diff, B * KU)
                fw.pe_rows(pe, B - 1, KU - 1, lambda hb: down[(KU - 1) % 2][:, :, :])
                fw.pe_turn(pe, B - 1, KU - 1)
                fw.pe_modes(pe, B - 1)

            @block.scalar
            def _(act):
                act.sem_inc(iv.v_out, iv.VB)
                fw.start(act)

                def copy_down(s, k):
                    dn = down[k % 2]
                    pg.wait(act, x2_done, s * KU + (k - 1))
                    pg.wait(act, fw.rows_done, s * KU + (k - 1))
                    n = s * (4 * KU) + 4 * k
                    act.wait_ge(d_done, n + 2)
                    for half in range(2):
                        bank = pg.ps[:, 4 + half].rearrange("p (c w) -> p c w", c=4)
                        cs = slice(4 * half, 4 * half + 4)
                        nc.scalar.copy(dn[64:P, cs, :], bank[64:P])
                        nc.scalar.copy(dn[0:64, cs, Q2:Q], bank[0:64, :, Q2:Q])
                    act.wait_ge(d_done, n + 4)
                    b2 = pg.ps[0:64, 6].rearrange("p (c w) -> p c w", c=CU)
                    b3 = pg.ps[64:96, 6, 0:CU * Q3].rearrange("p (c w) -> p c w", c=CU)
                    nc.scalar.copy(dn[32:64, :, 0:Q2], b2[32:64])
                    nc.scalar.copy(dn[0:32, :, Q3:Q2], b2[0:32, :, Q3:Q2])
                    nc.scalar.copy(dn[0:32, :, 0:Q3], b3).then_inc(d_out, 1)

                def scale(s, k):
                    act.wait_ge(d_diff, s * KU + (k + 1))
                    for g in range(CU // GROUP):
                        xg = R[k][:, :, g * GROUP:(g + 1) * GROUP, :].rearrange("p n c w -> p n (c w)")
                        c = g * GROUP
                        op = nc.scalar.activation(xg, xg, ACT.Identity, scale=stt[k][:, 2, c:c + 1],
                                                  bias=stt[k][:, 0, c:c + 1])
                    op.then_inc(scaled, 1)

                def squares(s, k):
                    act.wait_ge(x2_done, s * KU + (k + 1))
                    fw.act_squares(act, s, k, R[k])

                def body(s, first=False, last=False):
                    for k in range(KU):
                        prev = (s, k - 1) if k > 0 else (s - 1, KU - 1)
                        nxt = (s, k + 1) if k + 1 < KU else (s + 1, 0)
                        if not (last and k == KU - 1):
                            iv.act_v(act, *nxt)
                        if not (first and k == 0):
                            squares(*prev)
                            fw.act_rows(act, *prev)
                        copy_down(s, k)
                        if not (first and k == 0):
                            fw.act_turn(act, *prev)
                        scale(s, k)
                iv.act_v(act, 0, 0)
                body(0, first=True)
                with act.Fori(1, B - 1) as s:
                    body(s)
                body(B - 1, last=True)
                squares(B - 1, KU - 1)
                fw.act_rows(act, B - 1, KU - 1)
                fw.act_turn(act, B - 1, KU - 1)

            @block.vector
            def _(dve):
                dve.sem_inc(iv.y_out, iv.YB)
                dve.sem_inc(fw.modes_out, 1)
                nc.vector.memset(f1[:, :, 0:1], 0.0)
                nc.vector.memset(f2[:, :, 0:1], 0.0).then_inc(zero_cols, 1)
                dve.wait_ge(zero_cols, 1)

                def filters(s, k):
                    u1 = s * KU + (k + 1)
                    xr = R[k]
                    dve.wait_ge(iv.y_out, s * 32 + (8 * k + 8 + iv.YB))
                    nc.vector.tensor_tensor(odd[:, :, :, 1:Q], xr[:, :, :, 1:W - 2:2], xr[:, :, :, 3:W:2], ALU.add
                                            ).then_inc(odd1, 1)
                    nc.vector.tensor_copy(odd[:, :, :, 0:1], xr[:, :, :, 1:2]).then_inc(edge1, 1)
                    dve.wait_ge(odd1, u1)
                    dve.wait_ge(edge1, u1)
                    dn = s * (4 * KU) + 4 * k
                    pg.wait(dve, d_done, dn - 2)
                    nc.vector.scalar_tensor_tensor(
                        f1[:, :, 1:Q + 1], xr[:, :, :, 0:W:2].rearrange("p n c w -> p (n c) w"), 2.0,
                        odd[:, :, :, :].rearrange("p n c w -> p (n c) w"), ALU.mult, ALU.add).then_inc(f1_done, 1)
                    dve.wait_ge(f1_done, u1)
                    o2 = odd[:, :, :, 0:Q2].rearrange("p n c w -> p (n c) w")
                    nc.vector.tensor_tensor(o2, f1[:, :, 0:Q - 1:2], f1[:, :, 2:Q + 1:2], ALU.add).then_inc(odd2, 1)
                    dve.wait_ge(odd2, u1)
                    pg.wait(dve, d_done, dn - 1)
                    nc.vector.scalar_tensor_tensor(f2[:, :, 1:Q2 + 1], f1[:, :, 1:Q:2], 2.0, o2, ALU.mult, ALU.add
                                                   ).then_inc(f2_done, 1)
                    dve.wait_ge(f2_done, u1)
                    o3 = odd[:, :, :, 0:Q3].rearrange("p n c w -> p (n c) w")
                    nc.vector.tensor_tensor(o3, f2[:, :, 0:Q2 - 1:2], f2[:, :, 2:Q2 + 1:2], ALU.add).then_inc(odd3, 1)
                    dve.wait_ge(odd3, u1)
                    pg.wait(dve, d_done, dn)
                    nc.vector.scalar_tensor_tensor(f3[:, :, :], f2[:, :, 1:Q2:2], 2.0, o3, ALU.mult, ALU.add
                                                   ).then_inc(f3_done, 1)

                def finish(s, k):
                    u1 = s * KU + (k + 1)
                    quad = R[k][:, 0, :, 0:Q]
                    dve.wait_ge(d_out, u1)
                    dn = down[k % 2]
                    nc.vector.tensor_tensor(dn[:, :, :], dn[:, :, :], quad, ALU.subtract).then_inc(d_diff, 1)
                    dve.wait_ge(d_diff, u1)
                    dve.wait_ge(scaled, u1)
                    for g in range(CU // GROUP):
                        cs = slice(g * GROUP, (g + 1) * GROUP)
                        op = nc.vector.scalar_tensor_tensor(quad[:, cs], dn[:, cs], stt[k][:, 1, g * GROUP:g * GROUP + 1],
                                                            quad[:, cs], ALU.mult, ALU.add)
                    op.then_inc(x2_done, 1)

                def body(s, first=False, last=False):
                    for k in range(KU):
                        if not (last and k == KU - 1):
                            nxt = (s, k + 1) if k + 1 < KU else (s + 1, 0)
                            iv.dve_y(dve, *nxt, ALU.add, LOADS)
                            filters(*nxt)
                        finish(s, k)
                        if k == 0 and not first:
                            fw.dve_sample(dve, s - 1)
                iv.dve_y(dve, 0, 0, ALU.add, LOADS)
                filters(0, 0)
                body(0, first=True)
                with dve.Fori(1, B - 1) as s:
                    body(s)
                body(B - 1, last=True)
                fw.dve_sample(dve, B - 1)

            @block.gpsimd
            def _(pool):
                pool.sem_inc(fw.xf_free, 1)
                with pool.Fori(0, B) as s:
                    fw.pool_sample(pool, s, modes, sumsq)
                pool.wait_ge(fw.stored, B * 32)


def phase_inverse(pg, x2, sx, nx):
    nc = pg.nc
    LOADS = 3
    with ExitStack() as mem:
        iv = Inverse(pg, mem, "c")
        stored = [pg.sem(f"c_stored{k}") for k in range(KU)]
        with nc.Block(name="inverse") as block:
            @block.sync
            def _(sp):
                def store(s, k):
                    pg.hold(sp, iv.y_out, s * 32 + (8 * k + 8 + iv.YB))
                    for hb in range(HB):
                        sp.dma_start(unit_rows(nx, s, k, hb), iv.slot[k][:, hb]).then_inc(stored[k], 16)

                def reload(s_old, k):
                    pg.hold(sp, stored[k], s_old * 32 + 32)
                    iv.load(sp, x2, sx, s_old + 1, k)
                for k in range(KU):
                    iv.load(sp, x2, sx, 0, k)
                for k in range(KU):
                    store(0, k)
                    if k:
                        reload(0, k - 1)
                with sp.Fori(1, B - 1) as s:
                    for k in range(KU):
                        store(s, k)
                        reload(*((s, k - 1) if k else (s - 1, KU - 1)))
                store(B - 1, 0)
                reload(B - 2, KU - 1)
                for k in range(1, KU):
                    store(B - 1, k)
                for k in range(KU):
                    pg.hold(sp, stored[k], B * 32)

            @block.tensor
            def _(pe):
                iv.pe_v(pe, 0, 0, LOADS)

                def body(s, last=False):
                    for k in range(KU):
                        if not (last and k == KU - 1):
                            iv.pe_v(pe, *((s, k + 1) if k + 1 < KU else (s + 1, 0)), LOADS)
                        iv.pe_y(pe, s, k, "EN")
                with pe.Fori(0, B - 1) as s:
                    body(s)
                body(B - 1, last=True)

            @block.scalar
            def _(act):
                act.sem_inc(iv.v_out, iv.VB)

                def body(s):
                    for k in range(KU):
                        iv.act_v(act, s, k)
                body(0)
                with act.Fori(1, B) as s:
                    body(s)

            @block.vector
            def _(dve):
                dve.sem_inc(iv.y_out, iv.YB)
                with dve.Fori(0, B) as s:
                    for k in range(KU):
                        iv.dve_y(dve, s, k, ALU.subtract, LOADS)


def phase_scan_down(pg, nx, gates, ctx_down):
    nc = pg.nc
    NB = H // RR
    nxr = nx.rearrange("b c h w -> (b c) (h w)").rearrange("(g p) f -> p g f", p=P)
    outr = ctx_down.rearrange("b c h w -> (b c) (h w)").rearrange("(g p) f -> p g f", p=P)
    with ExitStack() as mem:
        def sb(n, shape):
            return [mem.enter_context(nc.sbuf_tensor(f"d_{n}{i}", shape, F32)) for i in range(2)]
        xin, u, cx = sb("x", [P, GB, RR, W]), sb("u", [P, GB, RR, W]), sb("c", [P, GB, RR, W])
        gate, carry = sb("g", [P, RR, W]), sb("t", [P, GB, W])
        loaded = [pg.sem(f"d_loaded{i}") for i in range(2)]
        carried = pg.sem("d_carried")
        rows = pg.sem("d_rows")
        clamped = pg.sem("d_clamped")
        stored = [pg.sem(f"d_stored{i}") for i in range(2)]

        def flat(n):
            return bass.ds((n * (-RR) + (H - RR)) * W, RR * W)

        with nc.Block(name="scan_down") as block:
            @block.sync
            def _(sp):
                def load(n, i):
                    sp.dma_start(xin[i][:].rearrange("p g r w -> p g (r w)"), nxr[:, :, flat(n)]).then_inc(loaded[i], 16)
                    sp.dma_start(gate[i][:].rearrange("p r w -> p (r w)"),
                                 gates[1].rearrange("h w -> (h w)").unsqueeze(0)[
                                     :, bass.ds((n * (-RR) + (H - RR + 1)) * W, RR * W)].to_broadcast([P, RR * W])
                                 ).then_inc(loaded[i], 16)

                def store(n, i):
                    pg.hold(sp, clamped, n + 1)
                    sp.dma_start(outr[:, :, flat(n)], cx[i][:].rearrange("p g r w -> p g (r w)")).then_inc(stored[i], 16)
                load(0, 0)
                load(1, 1)
                with sp.Fori(0, NB // 2 - 1) as half:
                    n = half * 2
                    for i in range(2):
                        pg.hold(sp, rows, n * RR + (i + 1) * RR)
                        load(n + (i + 2), i)
                        store(n + i, i)
                for i in range(2):
                    store(NB - 2 + i, i)
                for i in range(2):
                    pg.hold(sp, stored[i], 16 * (NB // 2))

            @block.vector
            def _(dve):
                def block_rows(n, half, i, first=False):
                    dve.wait_ge(loaded[i], half * 32 + 32)
                    if not first:
                        dve.wait_ge(clamped, n - 1)
                    for a in range(RR):
                        r = RR - 1 - a
                        if first and a == 0:
                            nc.vector.tensor_scalar(u[i][:, :, r, :], xin[i][:, :, r, :], -1.0, None, ALU.mult
                                                    ).then_inc(rows, 1)
                            nc.vector.memset(carry[1][:, 0, 0:1], 0.0).then_inc(carried, 1)
                            dve.wait_ge(carried, 1)
                            continue
                        at = n * RR + a
                        dve.wait_ge(rows, at)
                        prev = u[i][:, :, r + 1, :] if a else u[1 - i][:, :, 0, :]
                        g = gate[i][:, r, :].unsqueeze(1).to_broadcast([P, GB, W])
                        if first and a == 1:
                            op = nc.vector.tensor_tensor(carry[a % 2][:], prev, g, ALU.mult)
                        else:
                            op = nc.vector.scalar_tensor_tensor(carry[a % 2][:], prev, 0.0, g, ALU.max, ALU.mult)
                        op.then_inc(carried, 1)
                        dve.wait_ge(carried, at + 1)
                        nc.vector.tensor_tensor(u[i][:, :, r, :], carry[a % 2][:], xin[i][:, :, r, :], ALU.subtract
                                                ).then_inc(rows, 1)
                block_rows(0, 0, 0, first=True)
                block_rows(1, 0, 1)
                with dve.Fori(1, NB // 2) as half:
                    n = half * 2
                    for i in range(2):
                        block_rows(n + i, half, i)

            @block.scalar
            def _(act):
                def clamp(n, i, half, first=False):
                    act.wait_ge(rows, n * RR + RR)
                    act.wait_ge(stored[i], half * 16)
                    if first:
                        nc.scalar.copy(cx[i][:, :, RR - 1, :], u[i][:, :, RR - 1, :])
                        op = nc.scalar.activation(cx[i][:, :, 0:RR - 1, :], u[i][:, :, 0:RR - 1, :], ACT.Relu)
                    else:
                        op = nc.scalar.activation(cx[i][:].rearrange("p g r w -> p (g r w)"),
                                                  u[i][:].rearrange("p g r w -> p (g r w)"), ACT.Relu)
                    op.then_inc(clamped, 1)
                clamp(0, 0, 0, first=True)
                clamp(1, 1, 0)
                with act.Fori(1, NB // 2) as half:
                    n = half * 2
                    for i in range(2):
                        clamp(n + i, i, half)


def phase_scans(pg, nx, ctx_down, gates, gate_cols, conv_w, conv_b, stats, out):
    nc = pg.nc
    NB = H // RF
    F = RF * W
    XR = 4

    def grouped(a):
        return a.rearrange("b c h w -> (b c) (h w)").rearrange("(g p) f -> p g f", p=P)
    nxr, cdr, outr = grouped(nx), grouped(ctx_down), grouped(out)
    with ExitStack() as mem:
        def sb(n, shape):
            return mem.enter_context(nc.sbuf_tensor("e_" + n, shape, F32))

        def sb2(n, shape):
            return [sb(f"{n}{i}", shape) for i in range(2)]
        xin = [sb(f"x{i}", [P, GB, RF, W]) for i in range(XR)]
        cd, u, cu = (sb2(n, [P, GB, RF, W]) for n in ("cd", "u", "cu"))
        ncl, ncr, dl, dr = (sb2(n, [P, GB, RF, W]) for n in ("ncl", "ncr", "dl", "dr"))
        z = sb2("z", [P, GB, RF, W])
        gate = sb2("g", [P, 3, RF, W])
        carry = sb("carry", [P, GB, W])
        wraw = sb("wraw", [P, 4, P])
        wt = sb("wt", [P, GB, 6, P])
        bias = sb("bias", [P, 1])
        sts = sb("sts", [P, GB, 4])
        set_in = pg.sem("e_set_in")
        sts_in = pg.sem("e_sts_in")
        wt_done = pg.sem("e_wt_done")
        x_in = [pg.sem(f"e_x_in{i}") for i in range(XR)]
        g_in = [pg.sem(f"e_g_in{i}") for i in range(2)]
        cd_in = [pg.sem(f"e_cd_in{i}") for i in range(2)]
        carried, rows = pg.sem("e_carried"), pg.sem("e_rows")
        lin_done = pg.sem("e_lin_done")
        gated = pg.sem("e_gated")
        scans_done = pg.sem("e_scans_done")
        up_clamped = pg.sem("e_up_clamped")
        mixed = pg.sem("e_mixed")
        z_done = pg.sem("e_z_done")
        summed = pg.sem("e_summed")
        stored = [pg.sem(f"e_stored{i}") for i in range(2)]

        with nc.Block(name="scans") as block:
            @block.sync
            def _(sp):
                sp.dma_start(wraw[:, :, :], conv_w).then_inc(set_in, 16)
                sp.dma_start(bias[:, :], conv_b).then_inc(set_in, 16)
                def flat(n):
                    return bass.ds(n * F, F)

                def load_x(n, j):
                    sp.dma_start(xin[j][:].rearrange("p g r w -> p g (r w)"), nxr[:, :, flat(n)]).then_inc(x_in[j], 16)

                def load_gates(n, i):
                    for d, src in enumerate((gates[0], gate_cols[0], gate_cols[1])):
                        sp.dma_start(gate[i][:, d].rearrange("p r w -> p (r w)"),
                                     src.rearrange("h w -> (h w)").unsqueeze(0)[:, flat(n)].to_broadcast([P, F])
                                     ).then_inc(g_in[i], 16)

                def load_down(n, i):
                    sp.dma_start(cd[i][:].rearrange("p g r w -> p g (r w)"), cdr[:, :, flat(n)]).then_inc(cd_in[i], 16)

                def store(n, i):
                    sp.dma_start(outr[:, :, flat(n)], z[i][:].rearrange("p g r w -> p g (r w)")).then_inc(stored[i], 16)

                def step(n, j, first=False, last=False):
                    i = j % 2
                    if not last:
                        pg.hold(sp, scans_done, n + 1)
                        load_gates(n + 2, i)
                        pg.hold(sp, mixed, n * GB + GB)
                        load_down(n + 2, i)
                    pg.hold(sp, summed, n + 1)
                    store(n, i)
                    if not (last or n_is_late(n)):
                        load_x(n + XR, j)

                def n_is_late(n):
                    return isinstance(n, int) and n + XR >= NB

                for j in range(XR):
                    load_x(j, j)
                for i in range(2):
                    load_gates(i, i)
                    load_down(i, i)
                with sp.Fori(0, NB // XR - 1) as it:
                    n = it * XR
                    for j in range(XR):
                        step(n + j, j)
                for j in range(XR):
                    step(NB - XR + j, j, last=j >= XR - 2)
                for i in range(2):
                    pg.hold(sp, stored[i], 16 * (NB // 2))

            @block.gpsimd
            def _(pool):
                with nc.allow_non_contiguous_dma(reason="a few words per channel"):
                    for g in range(GB):
                        for b in range(4):
                            pool.dma_start(sts[b * C:(b + 1) * C, g, :],
                                           stats[4 * g + b].rearrange("k c -> c k")).then_inc(sts_in, 16)

            @block.vector
            def _(dve):
                dve.wait_ge(set_in, 2 * 16)
                dve.wait_ge(sts_in, 4 * GB * 16)
                for g in range(GB):
                    r = sts[:, g, 1:2]
                    op = nc.vector.tensor_scalar(wt[:, g, 0:4, :], wraw[:, :, :], r, None, ALU.mult)
                    op = nc.vector.tensor_scalar(wt[:, g, 4:6, :], wraw[:, 0:2, :], r, -1.0, ALU.mult, ALU.mult)
                op.then_inc(wt_done, 1)

                def up_rows(n, j, first):
                    i = j % 2
                    for r in range(RF):
                        at = n * RF + r
                        if first and r == 0:
                            nc.vector.tensor_scalar(u[i][:, :, 0, :], xin[j][:, :, 0, :], -1.0, None, ALU.mult
                                                    ).then_inc(rows, 1)
                            nc.vector.memset(carry[:, 0, 0:1], 0.0).then_inc(carried, 1)
                            dve.wait_ge(carried, 1)
                            continue
                        dve.wait_ge(rows, at)
                        prev = u[i][:, :, r - 1, :] if r else u[1 - i][:, :, RF - 1, :]
                        g = gate[i][:, 0, r, :].unsqueeze(1).to_broadcast([P, GB, W])
                        if first and r == 1:
                            op = nc.vector.tensor_tensor(carry[:], prev, g, ALU.mult)
                        else:
                            op = nc.vector.scalar_tensor_tensor(carry[:], prev, 0.0, g, ALU.max, ALU.mult)
                        op.then_inc(carried, 1)
                        dve.wait_ge(carried, at + 1)
                        nc.vector.tensor_tensor(u[i][:, :, r, :], carry[:], xin[j][:, :, r, :], ALU.subtract
                                                ).then_inc(rows, 1)

                def line(t, n, rev=False):
                    a = t[:, n].rearrange("p r w -> p (r w)")
                    return a[:, ::-1] if rev else a

                def step(n, it, j, first=False):
                    i = j % 2
                    dve.wait_ge(x_in[j], it * 16 + 16)
                    dve.wait_ge(g_in[i], it * 96 + (48 * (j // 2) + 48))
                    pg.wait(dve, up_clamped, n - 1)
                    up_rows(n, j, first)
                    pg.wait(dve, mixed, n * GB - GB)
                    for d, nl in ((1, ncl), (2, ncr)):
                        for g in range(GB):
                            rev = d == 2
                            op = nc.vector.tensor_tensor_scan(line(nl[i], g, rev), line(gate[i], d, rev),
                                                              line(xin[j], g, rev), 0.0, ALU.mult, ALU.add)
                        op.then_inc(lin_done, 1)
                    dve.wait_ge(lin_done, n * 2 + 2)
                    nc.vector.memset(gate[i][:, 1, :, 1:2], 0.0)
                    nc.vector.memset(gate[i][:, 2, :, W - 2:W - 1], 0.0).then_inc(gated, 1)
                    dve.wait_ge(gated, n + 1)
                    for d, nl, dd in ((1, ncl, dl), (2, ncr, dr)):
                        for g in range(GB):
                            rev = d == 2
                            op = nc.vector.tensor_tensor_scan(line(dd[i], g, rev), line(gate[i], d, rev),
                                                              line(nl[i], g, rev), 0.0, ALU.mult, ALU.max)
                    op.then_inc(scans_done, 1)
                    if not first:
                        sums(n - 1, (j - 1) % XR)

                def sums(n, j):
                    for g in range(GB):
                        dve.wait_ge(z_done, n * GB + (g + 1))
                        zg = line(z[j % 2], g)
                        op = nc.vector.scalar_tensor_tensor(zg, zg, sts[:, g, 0:1], line(xin[j], g), ALU.add, ALU.subtract)
                    op.then_inc(summed, 1)

                for j in range(XR):
                    step(j, 0, j, first=(j == 0))
                with dve.Fori(1, NB // XR) as it:
                    n = it * XR
                    for j in range(XR):
                        step(n + j, it, j)
                sums(NB - 1, XR - 1)

            @block.tensor
            def _(pe):
                pe.wait_ge(wt_done, 1)

                def mix(n, i, half):
                    pe.wait_ge(scans_done, n + 1)
                    pe.wait_ge(up_clamped, n + 1)
                    pe.wait_ge(cd_in[i], half * 16 + 16)
                    for g in range(GB):
                        bank = pg.ps[:, i * GB + g]
                        full = bank
                        for q, (wi, src) in enumerate(((4, ncl), (5, ncr), (2, cu), (3, cd))):
                            nc.tensor.matmul(full, wt[:, g, wi, :], src[i][:, g].rearrange("p r w -> p (r w)"),
                                             start=(q == 0), stop=False)
                        grid = bank.rearrange("p (r w) -> p r w", r=RF)
                        nc.tensor.matmul(grid[:, :, 1:W], wt[:, g, 0, :], dl[i][:, g, :, 1:W], start=False, stop=False)
                        nc.tensor.matmul(grid[:, :, 0:W - 1], wt[:, g, 1, :], dr[i][:, g, :, 0:W - 1],
                                         start=False, stop=True).then_inc(mixed, 1)

                def wait_z(n, i):
                    pe.wait_ge(z_done, n * GB - GB)
                mix(0, 0, 0)
                mix(1, 1, 0)
                with pe.Fori(1, NB // 2) as half:
                    n = half * 2
                    for i in range(2):
                        wait_z(n + i, i)
                        mix(n + i, i, half)

            @block.scalar
            def _(act):
                act.wait_ge(set_in, 2 * 16)

                def clamp_up(n, i, first=False):
                    act.wait_ge(rows, n * RF + RF)
                    if not first:
                        act.wait_ge(mixed, n * GB - GB)
                    if first:
                        nc.scalar.copy(cu[i][:, :, 0, :], u[i][:, :, 0, :])
                        op = nc.scalar.activation(cu[i][:, :, 1:RF, :], u[i][:, :, 1:RF, :], ACT.Relu)
                    else:
                        op = nc.scalar.activation(cu[i][:].rearrange("p g r w -> p (g r w)"),
                                                  u[i][:].rearrange("p g r w -> p (g r w)"), ACT.Relu)
                    op.then_inc(up_clamped, 1)

                def relu(n, i, half):
                    act.wait_ge(stored[i], half * 16)
                    for g in range(GB):
                        act.wait_ge(mixed, n * GB + (g + 1))
                        nc.scalar.activation(z[i][:, g].rearrange("p r w -> p (r w)"), pg.ps[:, i * GB + g], ACT.Relu,
                                             bias=bias[:, :]).then_inc(z_done, 1)
                clamp_up(0, 0, first=True)
                clamp_up(1, 1)
                relu(0, 0, 0)
                with act.Fori(1, NB // 2) as half:
                    n = half * 2
                    clamp_up(n, 0)
                    relu(n - 1, 1, half - 1)
                    clamp_up(n + 1, 1)
                    relu(n, 0, half)
                relu(NB - 1, 1, NB // 2 - 1)


def build(nc, ins, outs):
    x, cr0, ci0, pj0, cr2, ci2, pj2, weights, conv_w, conv_b, consts = ins
    out, = outs

    def scratch(name, shape):
        return nc.dram_tensor(name, shape, F32, kind="Internal").ap()
    with ExitStack() as ctx:
        pg = Prog(nc, ctx)
        gate_rows = scratch("s_gate_rows", [2, H + 1, W])
        gate_cols = scratch("s_gate_cols", [2, H, W])
        modes = scratch("s_modes", [B, P, XF])
        base = scratch("s_base", [B, P, XF])
        sumsq = scratch("s_sumsq", [B, C])
        sx = scratch("s_sx", [B, 2 * M, C * 2 * M])
        stats1, stats3 = scratch("s_stats1", [B, 4, C]), scratch("s_stats3", [B, 4, C])
        x2, nx, cdn = (scratch(n, [B, C, H, W]) for n in ("s_x2", "s_nx", "s_ctx_down"))
        phase_gates(pg, consts, weights, gate_rows, gate_cols)
        phase_forward(pg, x, modes, sumsq)
        phase_mix(pg, "m0", modes, sumsq, (cr0, ci0), pj0, sx, stats1, base_out=base)
        phase_wavelet(pg, x, sx, stats1, x2, modes, sumsq)
        phase_mix(pg, "m2", modes, sumsq, (cr2, ci2), pj2, sx, stats3, prior=(base, stats1))
        phase_inverse(pg, x2, sx, nx)
        phase_scan_down(pg, nx, gate_rows, cdn)
        phase_scans(pg, nx, cdn, gate_rows, gate_cols, conv_w, conv_b, stats3, out)


def kernel(**inputs):
    import concourse.bacc as bacc
    from concourse.bass_utils import run_bass_kernel_spmd as run

    nc = bacc.Bacc("TRN2", target_bir_lowering=False, num_devices=1)
    names = ["x", "L0_conv_coeff_real", "L0_conv_coeff_imag", "L0_conv_proj", "L2_conv_coeff_real",
             "L2_conv_coeff_imag", "L2_conv_proj", "L3_conv_weights"]
    data = {n: np.ascontiguousarray(inputs[n]) for n in names}
    for n in ("L0_conv_proj", "L2_conv_proj"):
        data[n] = np.ascontiguousarray(data[n].T)
    for n in names:
        if "coeff" in n:
            data[n] = np.ascontiguousarray(data[n].reshape(C, C, MQ, 4, M).transpose(2, 0, 3, 1, 4)
                                           .reshape(MQ, C, 4 * C * M))
    cw = np.asarray(inputs["L3_conv_conv_w"])
    blocks = np.zeros((P, 4, P), cw.dtype)
    for d in range(4):
        for b in range(P // C):
            blocks[b * C:(b + 1) * C, d, b * C:(b + 1) * C] = cw[:, d * C:(d + 1) * C].T
    data["L3_conv_conv_w"] = blocks
    data["L3_conv_conv_b"] = np.tile(np.asarray(inputs["L3_conv_conv_b"]), P // C).reshape(P, 1)
    data["consts"] = constant_table()
    arrays, ins = {}, []
    for n, a in data.items():
        arrays["in_" + n] = a
        ins.append(nc.dram_tensor("in_" + n, a.shape, F32, kind="ExternalInput").ap())
    out = nc.dram_tensor("out_0", (B, C, H, W), F32, kind="ExternalOutput").ap()
    build(nc, ins, [out])
    r = run(nc, [arrays], core_ids=[0])
    return r.results[0]["out_0"]
```

```python
from contextlib import ExitStack

import numpy as np
import concourse.bass as bass
from concourse import mybir

F32 = mybir.dt.float32
ALU = mybir.AluOpType
ACT = mybir.ActivationFunctionType
AX_X = mybir.AxisListType.X

B, C, H, W = 16, 32, 256, 256
P = 128
HB = H // P
M = 32
HW = H * W
GROUP = 2
CU = 8
KU = C // CU
MQ = M // 4
XF = MQ * 3 * M
EPS = 1e-5
GB = B * C // P
RF = 2

_widths = [("FR", HB * 2 * M), ("FI", HB * 2 * M), ("EW", W), ("EH0", H), ("EH1", H), ("EN0", H), ("EN1", H),
           ("D1", HB * 128), ("D2", HB * 64), ("D3", HB * 32), ("GM", P), ("ID", P)]
COL = {}
_at = 0
for _n, _w in _widths:
    COL[_n] = (_at, _at + _w)
    _at += _w
NCOL = _at


def constant_table():
    t = np.zeros((P, NCOL), np.float64)
    ang = 2 * np.pi * ((np.arange(H)[:, None] * np.arange(M)[None, :]) % H) / H
    c, s = np.cos(ang), np.sin(ang)

    def rows(a):
        return a.reshape(HB, P, -1).transpose(1, 0, 2).reshape(P, -1)

    def put(name, a):
        lo, hi = COL[name]
        t[:a.shape[0], lo:lo + a.shape[1]] = a

    put("FR", rows(np.concatenate([c, -s], 1)))
    put("FI", rows(np.concatenate([s, c], 1)))
    wj = np.where(np.arange(M) == 0, 1.0, 2.0)[:, None] / HW
    put("EW", np.concatenate([c.T * wj, -s.T * wj], 0))
    eh = np.concatenate([c.T, -s.T], 0)
    for e in range(2):
        half = np.zeros((P, H))
        half[e * 2 * M:(e + 1) * 2 * M] = eh
        put(f"EH{e}", half)
        put(f"EN{e}", -half)

    def down(n):
        a = np.zeros((n // 2, n))
        for i in range(n // 2):
            for d, v in ((-1, 0.25), (0, 0.5), (1, 0.25)):
                if 0 <= 2 * i + d < n:
                    a[i, 2 * i + d] = v
        return a
    a1 = down(H)
    a2 = down(H // 2) @ a1
    a3 = down(H // 4) @ a2
    put("D1", rows(a1.T / 4))
    put("D2", rows(a2.T / 16))
    put("D3", rows(a3.T / 64))
    grp = (np.arange(P) % C) // GROUP
    put("GM", (grp[:, None] == grp[None, :]).astype(np.float64))
    put("ID", np.eye(P))
    return t.astype(np.float32)


class Prog:

    def __init__(self, nc, ctx):
        self.nc, self.ctx = nc, ctx
        self.tab = ctx.enter_context(nc.sbuf_tensor("tab", [P, NCOL], F32))
        self.ones = ctx.enter_context(nc.sbuf_tensor("ones", [P, 1], F32))
        self.ps = ctx.enter_context(nc.psum_tensor("ps", [P, 8, 512], F32))

        self.consts_in = self.sem("consts_in")
        self.passed = self.sem("passed")
        self.conv_w = ctx.enter_context(nc.sbuf_tensor("conv_w", [P, 4, P], F32))
        self.conv_b = ctx.enter_context(nc.sbuf_tensor("conv_b", [P, 1], F32))

    @staticmethod
    def wait(eng, sem, value):
        if not (isinstance(value, int) and value <= 0):
            eng.wait_ge(sem, value)

    def hold(self, eng, sem, value):
        eng.wait_ge(sem, value)
        eng.sem_inc(self.passed, 1)

    def sem(self, name):
        return self.ctx.enter_context(self.nc.semaphore(name))

    def t(self, name, rows=P):
        lo, hi = COL[name]
        return self.tab[0:rows, lo:hi]


def phase_gates(pg, consts, conv_w, conv_b, weights, gate_rows, gate_cols):
    nc = pg.nc
    with ExitStack() as mem:
        raw = mem.enter_context(nc.sbuf_tensor("g_raw", [P, 4, HB, W], F32))
        sg = mem.enter_context(nc.sbuf_tensor("g_sig", [P, 4, HB, W], F32))
        zero = mem.enter_context(nc.sbuf_tensor("g_zero", [1, W], F32))
        raw_in = pg.sem("g_raw_in")
        zeroed = pg.sem("g_zeroed")
        sig_done = pg.sem("g_sig_done")
        gates_out = pg.sem("g_gates_out")
        with nc.Block(name="gates") as block:
            @block.sync
            def _(sp):
                sp.dma_start(pg.tab[:, :], consts).then_inc(pg.consts_in, 16)
                sp.dma_start(pg.conv_w[:, :, :], conv_w).then_inc(pg.consts_in, 16)
                sp.dma_start(pg.conv_b[:, :], conv_b).then_inc(pg.consts_in, 16)
                for d in range(4):
                    sp.dma_start(raw[:, d], weights[d].rearrange("(n p) w -> p n w", p=P)).then_inc(raw_in, 16)
                pg.hold(sp, zeroed, 1)
                sp.dma_start(gate_rows[0, 0:1, :], zero[:, :]).then_inc(gates_out, 16)
                sp.dma_start(gate_rows[1, H:H + 1, :], zero[:, :]).then_inc(gates_out, 16)
                pg.hold(sp, sig_done, 1)
                sp.dma_start(gate_rows[0, 1:H + 1, :].rearrange("(n p) w -> p n w", p=P), sg[:, 0]).then_inc(gates_out, 16)
                sp.dma_start(gate_rows[1, 0:H, :].rearrange("(n p) w -> p n w", p=P), sg[:, 1]).then_inc(gates_out, 16)
                for d in range(2):
                    sp.dma_start(gate_cols[d].rearrange("(n p) w -> p n w", p=P), sg[:, 2 + d]).then_inc(gates_out, 16)
                pg.hold(sp, gates_out, 6 * 16)
                pg.hold(sp, pg.consts_in, 3 * 16)

            @block.vector
            def _(dve):
                nc.vector.memset(pg.ones[:, :], 1.0)
                nc.vector.memset(sg[:, 2, :, 0:1], 0.0)
                nc.vector.memset(sg[:, 3, :, W - 1:W], 0.0)
                nc.vector.memset(zero[:, :], 0.0).then_inc(zeroed, 1)

            @block.scalar
            def _(act):
                act.wait_ge(raw_in, 4 * 16)
                nc.scalar.activation(sg[:, 0:2], raw[:, 0:2], ACT.Sigmoid)
                nc.scalar.activation(sg[:, 2, :, 1:W], raw[:, 2, :, 0:W - 1], ACT.Sigmoid)
                nc.scalar.activation(sg[:, 3, :, 0:W - 1], raw[:, 3, :, 1:W], ACT.Sigmoid).then_inc(sig_done, 1)


class Forward:

    def __init__(self, pg, mem, name, row_blocks, col_blocks, row_banks, turn_banks, modes_bank, sq_ps, deep=1):
        nc = pg.nc
        self.deep = deep
        self.pg, self.nh, self.nw = pg, row_blocks, col_blocks
        self.row_banks, self.turn_banks, self.modes_bank, self.sq_ps = row_banks, turn_banks, modes_bank, sq_ps
        self.shared = row_banks == turn_banks
        self.width = col_blocks * P
        self.nb = CU * self.width // 1024
        self.t = [mem.enter_context(nc.sbuf_tensor(f"{name}_t{i}", [P, CU // 2, self.width], F32)) for i in range(2)]
        self.a1 = [mem.enter_context(nc.sbuf_tensor(f"{name}_a1{i}", [P, self.nw, 2 * M, C], F32)) for i in range(deep)]
        self.xf = mem.enter_context(nc.sbuf_tensor(name + "_xf", [P, MQ, 3, M], F32))
        self.sq = mem.enter_context(nc.sbuf_tensor(name + "_sq", [P, C // GROUP], F32))
        self.junk = [mem.enter_context(nc.sbuf_tensor(f"{name}_junk{i}", [P, HB, GROUP * W], F32)) for i in range(2)]
        self.sqrow = mem.enter_context(nc.sbuf_tensor(name + "_sqrow", [1, C // GROUP, GROUP], F32))
        self.rows_done = pg.sem(name + "_rows_done")
        self.rows_out = pg.sem(name + "_rows_out")
        self.turn_done = pg.sem(name + "_turn_done")
        self.turn_out = pg.sem(name + "_turn_out")
        self.sq_done = pg.sem(name + "_sq_done")
        self.sq_used = pg.sem(name + "_sq_used")
        self.modes_done = pg.sem(name + "_modes_done")
        self.modes_out = pg.sem(name + "_modes_out")
        self.xf_free = pg.sem(name + "_xf_free")
        self.stored = pg.sem(name + "_modes_stored")

    def rows_count(self, s, k):
        return s * (KU * self.nb) + (k + 1) * self.nb

    def turn_count(self, s, k):
        return s * (KU * self.nw) + (k + 1) * self.nw

    def sq_count(self, s, k):
        return s * (C // GROUP) + ((k + 1) * (CU // GROUP) + 2)

    def start(self, act):
        act.sem_inc(self.sq_done, 2)

    def pe_rows(self, pe, s, k, x):
        nc = self.pg.nc
        fr = self.pg.t("FR").rearrange("p (n m) -> p n m", n=HB)
        if self.shared:
            self.pg.wait(pe, self.turn_out, self.turn_count(s, k - 1))
            if k == 0:
                pe.wait_ge(self.modes_out, s + 1)
        per = 512 // self.width
        for n in range(self.nb):
            if not self.shared:
                self.pg.wait(pe, self.rows_out, self.rows_count(s, k - 1) - self.nb + n + 1)
            bank = self.pg.ps[:, self.row_banks[n]]
            for e in range(2):
                for hb in range(self.nh):
                    c0 = 2 * per * n + e
                    mm = nc.tensor.matmul(bank[e * 2 * M:(e + 1) * 2 * M, :], fr[:, hb, :],
                                          x(hb)[:, c0:c0 + 2 * per - 1:2, :],
                                          start=(hb == 0), stop=(hb == self.nh - 1))
            mm.then_inc(self.rows_done, 1)

    def act_rows(self, act, s, k):
        nc = self.pg.nc
        self.pg.wait(act, self.turn_done, self.turn_count(s, k - 2))
        per = 512 // self.width
        for n in range(self.nb):
            act.wait_ge(self.rows_done, self.rows_count(s, k) - self.nb + n + 1)
            nc.scalar.copy(self.t[k % 2][:, per * n:per * (n + 1), :].rearrange("p q w -> p (q w)"),
                           self.pg.ps[:, self.row_banks[n]]).then_inc(self.rows_out, 1)

    def pe_turn(self, pe, s, k):
        nc = self.pg.nc
        pe.wait_ge(self.rows_out, self.rows_count(s, k))
        for wb in range(self.nw):
            if not self.shared:
                self.pg.wait(pe, self.turn_out, self.turn_count(s, k - 1) - self.nw + wb + 1)
            for q in range(CU // 2):
                mm = nc.tensor.transpose(self.pg.ps[:, self.turn_banks[wb], q * P:(q + 1) * P],
                                         self.t[k % 2][:, q, wb * P:(wb + 1) * P], self.pg.t("ID"))
            mm.then_inc(self.turn_done, 1)

    def act_turn(self, act, s, k, par=0):
        nc = self.pg.nc
        if k == 0:
            self.pg.wait(act, self.modes_done, s + (2 - self.deep))
        for wb in range(self.nw):
            act.wait_ge(self.turn_done, self.turn_count(s, k) - self.nw + wb + 1)
            bank = self.pg.ps[:, self.turn_banks[wb]].rearrange("p (c m) -> p c m", c=CU)
            dst = self.a1[par][:, wb, :, k * CU:(k + 1) * CU].rearrange("p m c -> p c m")
            nc.scalar.copy(dst, bank).then_inc(self.turn_out, 1)

    def pe_sums(self, pe, s):
        nc = self.pg.nc
        pe.wait_ge(self.sq_done, self.sq_count(s, KU - 1))
        pe.wait_ge(self.modes_out, s + 1)
        nc.tensor.matmul(self.sq_ps, self.pg.ones[:, :], self.sq[:, :], start=True, stop=True).then_inc(self.sq_used, 1)

    def pe_modes(self, pe, s, par=0, quads=range(MQ)):
        nc = self.pg.nc
        fr = self.pg.t("FR").rearrange("p (n m) -> p n m", n=HB)
        fi = self.pg.t("FI").rearrange("p (n m) -> p n m", n=HB)
        if quads[0] == 0:
            pe.wait_ge(self.turn_out, self.turn_count(s, KU - 1))
            pe.wait_ge(self.modes_out, s + 1)
        bank = self.pg.ps[:, self.modes_bank].rearrange("p (q m) -> p q m", q=MQ)
        for iq in quads:
            n = 0
            for wb in range(self.nw):
                for ri, f in ((0, fr), (1, fi)):
                    i0 = ri * M + 4 * iq
                    mm = nc.tensor.matmul(bank[:, iq, :], self.a1[par][:, wb, i0:i0 + 4, :], f[:, wb, :],
                                          start=(n == 0), stop=(n == 2 * self.nw - 1))
                    n += 1
        if quads[-1] == MQ - 1:
            mm.then_inc(self.modes_done, 1)

    def act_squares(self, act, s, k, x):
        nc = self.pg.nc
        if k == 0:
            self.pg.wait(act, self.sq_used, s)
        for g in range(CU // GROUP):
            src = x[:, :, g * GROUP:(g + 1) * GROUP, :].rearrange("p n c w -> p n (c w)")
            at = k * (CU // GROUP) + g
            act.wait_ge(self.sq_done, s * (C // GROUP) + (at + 1))
            nc.scalar.activation(self.junk[at % 2][:, :, :], src, ACT.Square, accum_out=self.sq[:, at:at + 1]
                                 ).then_inc(self.sq_done, 1)

    def dve_sample(self, dve, s):
        nc = self.pg.nc
        dve.wait_ge(self.modes_done, s + 2)
        dve.wait_ge(self.sq_used, s + 1)
        dve.wait_ge(self.xf_free, s + 1)
        bank = self.pg.ps[:, self.modes_bank].rearrange("p (q r m) -> p q r m", q=MQ, r=2)
        nc.vector.tensor_copy(self.xf[:, :, 1:3, :], bank)
        nc.vector.tensor_scalar(self.xf[:, :, 0, :], bank[:, :, 1, :], -1.0, None, ALU.mult)
        nc.vector.tensor_copy(self.sqrow[:, :, :], self.sq_ps.unsqueeze(2).to_broadcast([1, C // GROUP, GROUP])
                              ).then_inc(self.modes_out, 1)

    def pool_sample(self, pool, s, modes, sumsq):
        pool.wait_ge(self.modes_out, s + 2)
        pool.dma_start(modes[bass.ds(s, 1)].rearrange("b p f -> p (b f)"),
                       self.xf[:, :, :, :].rearrange("p q r m -> p (q r m)")).then_inc(self.stored, 16)
        pool.dma_start(sumsq[bass.ds(s, 1), :], self.sqrow[:, :, :].rearrange("o g e -> o (g e)")
                       ).then_inc(self.stored, 16)
        pool.wait_ge(self.stored, s * 32 + 32)
        pool.sem_inc(self.xf_free, 1)


def unit_rows(img, s, k, hb):
    return img[bass.ds(s, 1), k * CU:(k + 1) * CU, hb * P:(hb + 1) * P, :].rearrange("b c p w -> p (b c) w")


def phase_forward(pg, x, modes, sumsq):
    nc = pg.nc
    with ExitStack() as mem:
        slot = [mem.enter_context(nc.sbuf_tensor(f"a_x{k}", [P, HB, CU, W], F32)) for k in range(KU)]
        loaded = [pg.sem(f"a_loaded{k}") for k in range(KU)]
        fw = Forward(pg, mem, "a", HB, 2, (0, 1), (2, 3), 4, pg.ps[96:97, 5, 0:C // GROUP], deep=2)

        def before(s, k):
            return (s, k - 1) if k else (s - 1, KU - 1)

        with nc.Block(name="forward") as block:
            @block.sync
            def _(sp):
                def load(s, k):
                    for hb in range(HB):
                        sp.dma_start(slot[k][:, hb], unit_rows(x, s, k, hb)).then_inc(loaded[k], 16)
                for k in range(KU):
                    load(0, k)
                with sp.Fori(1, B) as s:
                    for k in range(KU):
                        pg.hold(sp, fw.rows_done, fw.rows_count(s, k - KU))
                        pg.hold(sp, fw.sq_done, fw.sq_count(s, k - KU))
                        load(s, k)

            @block.tensor
            def _(pe):
                def body(s, par, first=False, second=False):
                    for k in range(KU):
                        if k == 1 and not first:
                            fw.pe_sums(pe, s - 1)
                        pe.wait_ge(loaded[k], s * 32 + 32)
                        fw.pe_rows(pe, s, k, lambda hb: slot[k][:, hb])
                        if k == 0 and not (first or second):
                            fw.pe_modes(pe, s - 2, par, quarter[3])
                        if not (first and k == 0):
                            fw.pe_turn(pe, *before(s, k))
                        if k and not first:
                            fw.pe_modes(pe, s - 1, 1 - par, quarter[k - 1])
                quarter = [range(q * MQ // 4, (q + 1) * MQ // 4) for q in range(4)]
                pe.sem_inc(fw.modes_done, 1)
                body(0, 0, first=True)
                body(1, 1, second=True)
                with pe.Fori(1, B // 2) as pair:
                    body(pair * 2, 0)
                    body(pair * 2 + 1, 1)
                fw.pe_modes(pe, B - 2, 0, quarter[3])
                fw.pe_turn(pe, B - 1, KU - 1)
                fw.pe_sums(pe, B - 1)
                fw.pe_modes(pe, B - 1, 1)

            @block.scalar
            def _(act):
                def body(s, par, first=False):
                    for k in range(KU):
                        act.wait_ge(loaded[k], s * 32 + 32)
                        fw.act_rows(act, s, k)
                        if not (first and k == 0):
                            fw.act_turn(act, *before(s, k), par if k else 1 - par)
                        fw.act_squares(act, s, k, slot[k])
                fw.start(act)
                body(0, 0, first=True)
                body(1, 1)
                with act.Fori(1, B // 2) as pair:
                    body(pair * 2, 0)
                    body(pair * 2 + 1, 1)
                fw.act_turn(act, B - 1, KU - 1, 1)

            @block.vector
            def _(dve):
                dve.sem_inc(fw.modes_out, 1)
                with dve.Fori(0, B) as s:
                    fw.dve_sample(dve, s)

            @block.gpsimd
            def _(pool):
                pool.sem_inc(fw.xf_free, 1)
                with pool.Fori(0, B) as s:
                    fw.pool_sample(pool, s, modes, sumsq)
                pool.wait_ge(fw.stored, B * 32)


def phase_mix(pg, name, modes, sumsq, coef, projT, sx, stats, base_out=None, prior=None):
    nc = pg.nc
    NF = HW * GROUP
    with ExitStack() as mem:
        def sb(n, shape):
            return mem.enter_context(nc.sbuf_tensor(name + n, shape, F32))
        X = sb("_x", [P, B, MQ, 3, M])
        S = sb("_s", [P, B, MQ, 3, M])
        BD = [sb(f"_bd{i}", [P, 2, P, M]) for i in range(2)]
        T = [sb(f"_t{i}", [P, 2, 512]) for i in range(2)]
        pj = sb("_pj", [P, P])
        prod = [sb(f"_prod{i}", [P, B, 2, M]) for i in range(2)]
        part = sb("_part", [P, 4, B, MQ])
        v = sb("_v", [P, 16, B])
        st = sb("_st", [P, B, 4])
        tot, mean, var, rs, t0, t1, t2, qs, qc, cs, cc, em, m1, v1, t3, rel = [v[:, n, :] for n in range(16)]
        pr = sb("_pr", [P, 2, B])

        x_in, sq_in, pj_in = pg.sem(name + "_x_in"), pg.sem(name + "_sq_in"), pg.sem(name + "_pj_in")
        bd_in = [pg.sem(f"{name}_bd_in{i}") for i in range(2)]
        base_in = pg.sem(name + "_base_in")
        joined = pg.sem(name + "_joined")
        base_done, base_stored = pg.sem(name + "_base_done"), pg.sem(name + "_base_stored")
        dc_done = pg.sem(name + "_dc_done")
        chain = pg.sem(name + "_dve_chain")
        var_ready = pg.sem(name + "_var_ready")
        sums_ready = pg.sem(name + "_sums_ready")
        root_done = pg.sem(name + "_root_done")
        normed = pg.sem(name + "_normed")
        zeroed = pg.sem(name + "_zeroed")
        pj_zeroed = pg.sem(name + "_pj_zeroed")
        mix_done = pg.sem(name + "_mix_done")
        t_out = pg.sem(name + "_t_out")
        proj_done = pg.sem(name + "_proj_done")
        s_out = pg.sem(name + "_s_out")
        sums_done = pg.sem(name + "_sums_done")
        s_final = pg.sem(name + "_s_final")
        tr_done = pg.sem(name + "_tr_done")
        tr_out = pg.sem(name + "_tr_out")
        sx_out = [pg.sem(f"{name}_sx_out{i}") for i in range(2)]
        st_out = pg.sem(name + "_st_out")
        ident = pg.t("ID")
        gm = pg.t("GM")
        SX = [BD[i][0:2 * M, 0, 0:64, :].rearrange("p a b -> p (a b)").rearrange(
            "p (c r m) -> p c r m", c=C, r=2) for i in range(2)]
        TB = 3

        with nc.Block(name=name) as block:
            @block.sync
            def _(sp):
                for i4 in range(4):
                    with nc.allow_non_contiguous_dma(reason="512 words"):
                        sp.dma_start(tot[i4 * C:(i4 + 1) * C, :], sumsq.rearrange("b c -> c b")).then_inc(sq_in, 16)
                if prior:
                    sp.dma_start(S[:].rearrange("p b q r m -> p b (q r m)"),
                                 prior[0].rearrange("b p f -> p b f")).then_inc(base_in, 16)
                    for i4 in range(4):
                        for j in range(2):
                            with nc.allow_non_contiguous_dma(reason="512 words"):
                                sp.dma_start(pr[i4 * C:(i4 + 1) * C, j, :],
                                             prior[1][:, j, :].rearrange("b c -> c b")).then_inc(base_in, 16)
                sp.dma_start(X[:].rearrange("p b q r m -> p b (q r m)"),
                             modes.rearrange("b p f -> p b f")).then_inc(x_in, 16)
                pg.hold(sp, pj_zeroed, 1)
                for i4 in range(4):
                    r0 = i4 * C
                    sp.dma_start(pj[r0:r0 + C, r0:r0 + C], projT).then_inc(pj_in, 16)
                for iq in range(MQ):
                    if iq < 2:
                        pg.hold(sp, zeroed, iq + 1)
                    else:
                        pg.hold(sp, mix_done, 2 * (iq - 1))
                    for i4 in range(4):
                        r0 = i4 * C
                        for ri in range(2):
                            sp.dma_start(BD[iq % 2][r0:r0 + C, ri, r0:r0 + C, :].rearrange("p r j -> p (r j)"),
                                         coef[ri][iq, r0:r0 + C, :]).then_inc(bd_in[iq % 2], 16)
                pg.hold(sp, s_final, 1)
                with nc.allow_non_contiguous_dma(reason="a few words per channel"):
                    sp.dma_start(stats.rearrange("b k c -> c (b k)"),
                                 st[0:C].rearrange("p b k -> p (b k)")).then_inc(st_out, 16)
                for b in range(B):
                    pg.hold(sp, tr_out, 4 * (b + 1))
                    sp.dma_start(sx[b], SX[b % 2].rearrange("p c r m -> p (c r m)")).then_inc(sx_out[b % 2], 16)
                if base_out is not None:
                    pg.hold(sp, base_done, 1)
                    sp.dma_start(base_out.rearrange("b p f -> p b f"), X[:].rearrange("p b q r m -> p b (q r m)")
                                 ).then_inc(base_stored, 16)
                    pg.hold(sp, base_stored, 16)
                pg.hold(sp, st_out, 16)
                for i in range(2):
                    pg.hold(sp, sx_out[i], 16 * (B // 2))

            @block.tensor
            def _(pe):
                pe.wait_ge(*((joined, 1) if prior else (x_in, 16)))
                dc = pg.ps[:, 7, 0:B]
                nc.tensor.matmul(dc, gm[0:C, :], X[0:C, :, 0, 1, 0], start=True, stop=True).then_inc(dc_done, 1)

                def mix(iq):
                    pe.wait_ge(bd_in[iq % 2], 128 * (iq // 2 + 1))
                    if iq == 0:
                        pe.wait_ge(normed, 1)
                    for jh in range(2):
                        if iq >= 2:
                            pe.wait_ge(t_out, 2 * (iq - 2) + jh + 1)
                        bank = pg.ps[:, 2 * (iq % 2) + jh].rearrange("p (j n) -> p j n", j=M // 2)
                        for j in range(M // 2):
                            jj = jh * 16 + j
                            for ri in range(2):
                                rhs = X[:, :, iq, 1 - ri:3 - ri, jj].rearrange("p b r -> p r b")
                                mm = nc.tensor.matmul(bank[:, j, :], BD[iq % 2][:, ri, :, jj], rhs,
                                                      start=(ri == 0), stop=(ri == 1))
                        mm.then_inc(mix_done, 1)

                def project(iq):
                    for jh in range(2):
                        pe.wait_ge(t_out, 2 * iq + jh + 1)
                        if iq >= 1:
                            pe.wait_ge(s_out, 2 * (iq - 1) + jh + 1)
                        nc.tensor.matmul(pg.ps[:, 4 + jh], pj[:, :], T[iq % 2][:, jh, :], start=True, stop=True
                                         ).then_inc(proj_done, 1)
                mix(0)
                pe.wait_ge(pj_in, 4 * 16)
                for iq in range(MQ):
                    if iq + 1 < MQ:
                        mix(iq + 1)
                    project(iq)
                pe.wait_ge(sums_ready, 1)
                for n, a in enumerate((qs, cs)):
                    mm = nc.tensor.matmul(pg.ps[:, 7, (n + 1) * B:(n + 2) * B], gm, a, start=True, stop=True)
                mm = nc.tensor.matmul(pg.ps[:, 7, 3 * B:4 * B], gm[0:C, :], S[0:C, :, 0, 0, 0], start=True, stop=True)
                mm.then_inc(sums_done, 1)
                pe.wait_ge(s_final, 1)
                for b in range(B):
                    for half in range(2):
                        u = 2 * b + half
                        if u >= TB:
                            pe.wait_ge(tr_out, 2 * (u - TB) + 2)
                        for r in range(2):
                            for q in range(4):
                                iq = half * 4 + q
                                mm = nc.tensor.transpose(
                                    pg.ps[0:2 * M, 2 * (u % TB) + r, q * P:(q + 1) * P],
                                    S[:, b, iq, r:r + 2, :].rearrange("p r m -> p (r m)"), ident)
                            mm.then_inc(tr_done, 1)

            @block.gpsimd
            def _(pool):
                for i in range(2):
                    nc.gpsimd.memset(BD[i][:].rearrange("p r m j -> p (r m j)"), 0.0).then_inc(zeroed, 1)

            @block.scalar
            def _(act):
                act.wait_ge(var_ready, 1)
                nc.scalar.activation(t1, var, ACT.Sqrt).then_inc(root_done, 1)
                for iq in range(MQ):
                    for jh in range(2):
                        act.wait_ge(mix_done, 2 * iq + jh + 1)
                        if iq >= 2:
                            act.wait_ge(proj_done, 2 * (iq - 2) + jh + 1)
                        nc.scalar.copy(T[iq % 2][:, jh, :], pg.ps[:, 2 * (iq % 2) + jh]).then_inc(t_out, 1)
                act.wait_ge(var_ready, 2)
                nc.scalar.activation(t1, v1, ACT.Sqrt).then_inc(root_done, 1)
                for b in range(B):
                    if b >= 2:
                        act.wait_ge(sx_out[b % 2], 16 * (b // 2))
                    for half in range(2):
                        u = 2 * b + half
                        for r in range(2):
                            act.wait_ge(tr_done, 2 * u + r + 1)
                            src = pg.ps[0:2 * M, 2 * (u % TB) + r].rearrange("p (i o) -> p i o", i=16)
                            dst = SX[b % 2][:, :, r, half * 16:(half + 1) * 16].rearrange("p c i -> p i c")
                            nc.scalar.copy(dst, src).then_inc(tr_out, 1)

            @block.vector
            def _(dve):
                done = [0]

                def signal(op, sem, value):
                    op.then_inc(sem, 1)
                    dve.wait_ge(sem, value)

                def link(op):
                    done[0] += 1
                    op.then_inc(chain, 1)
                    dve.wait_ge(chain, done[0])

                def inv_root(out, root, variance):
                    link(nc.vector.reciprocal(out, root))
                    link(nc.vector.tensor_tensor(t2, out, out, ALU.mult))
                    link(nc.vector.tensor_tensor(t2, t2, variance, ALU.mult))
                    link(nc.vector.tensor_scalar(t2, t2, -0.5, 1.5, ALU.mult, ALU.add))
                    link(nc.vector.tensor_tensor(out, out, t2, ALU.mult))

                dc = pg.ps[:, 7, 0:B]
                nc.vector.memset(pj[:, :], 0.0).then_inc(pj_zeroed, 1)
                link(nc.vector.memset(st[:], 0.0))
                if prior:
                    dve.wait_ge(x_in, 16)
                    dve.wait_ge(base_in, 16 * 9)
                    for b in range(B):
                        xb, sb_ = (a[:, b].rearrange("p q r m -> p (q r m)") for a in (X, S))
                        op = nc.vector.scalar_tensor_tensor(xb, xb, pr[:, 1, b:b + 1], sb_, ALU.mult, ALU.add)
                    signal(op, joined, 1)
                dve.wait_ge(sq_in, 64)
                dve.wait_ge(dc_done, 1)
                link(nc.vector.tensor_scalar(rel, dc, 1.0 / NF, None, ALU.mult))
                link(nc.vector.tensor_tensor(mean, rel, pr[:, 0, :], ALU.add) if prior
                     else nc.vector.tensor_copy(mean, rel))
                link(nc.vector.tensor_tensor(t0, mean, mean, ALU.mult))
                link(nc.vector.tensor_scalar(tot, tot, 1.0 / NF, None, ALU.mult))
                link(nc.vector.tensor_tensor(tot, tot, t0, ALU.subtract))
                signal(nc.vector.tensor_scalar(var, tot, EPS, None, ALU.add), var_ready, 1)
                dve.wait_ge(root_done, 1)
                inv_root(rs, t1, var)
                link(nc.vector.tensor_scalar(t0, rel, float(HW), None, ALU.mult))
                dve.wait_ge(x_in, 16)
                x00 = X[0:C, :, 0, 1, 0]
                link(nc.vector.tensor_tensor(x00, x00, t0[0:C], ALU.subtract))
                for b in range(B):
                    xb = X[:, b].rearrange("p q r m -> p (q r m)")
                    op = nc.vector.tensor_scalar(xb, xb, rs[:, b:b + 1], None, ALU.mult)
                op.then_inc(normed, 1)

                for iq in range(MQ):
                    for jh in range(2):
                        dve.wait_ge(proj_done, 2 * iq + jh + 1)
                        bank = pg.ps[:, 4 + jh].rearrange("p (j r b) -> p r b j", j=M // 2, r=2)
                        js = slice(jh * 16, (jh + 1) * 16)
                        for r in range(2):
                            nc.vector.tensor_copy(S[:, :, iq, r, js], bank[:, r])
                        nc.vector.tensor_scalar(S[:, :, iq, 2, js], bank[:, 0], -1.0, None, ALU.mult).then_inc(s_out, 1)
                    dve.wait_ge(s_out, 2 * iq + 2)
                    if iq == 0:
                        link(nc.vector.memset(S[0:C, :, 0, 1, 0], 0.0))
                    y = S[:, :, iq, 0:2, :]
                    nc.vector.tensor_tensor(prod[0][:], X[:, :, iq, 1:3, :], y, ALU.mult)
                    link(nc.vector.tensor_tensor(prod[1][:], y, y, ALU.mult))
                    for n in range(2):
                        nc.vector.tensor_reduce(part[:, 2 * n, :, iq], prod[n][:].rearrange("p b r m -> p b (r m)"),
                                                AX_X, ALU.add)
                        op = nc.vector.tensor_reduce(part[:, 2 * n + 1, :, iq], prod[n][:, :, :, 0], AX_X, ALU.add)
                    link(op)
                for n, total in enumerate((qs, qc, cs, cc)):
                    op = nc.vector.tensor_reduce(total, part[:, n], AX_X, ALU.add)
                link(op)
                link(nc.vector.scalar_tensor_tensor(qs, qs, 2.0, qc, ALU.mult, ALU.subtract))
                link(nc.vector.tensor_scalar(cc, cc, 1.5, None, ALU.mult))
                link(nc.vector.scalar_tensor_tensor(cs, cs, 2.0, cc, ALU.mult, ALU.subtract))
                s00 = S[0:C, :, 0, 0, 0]
                link(nc.vector.tensor_tensor(t0[0:C], s00, s00, ALU.mult))
                signal(nc.vector.scalar_tensor_tensor(cs[0:C], t0[0:C], 0.5, cs[0:C], ALU.mult, ALU.add),
                       sums_ready, 1)
                dve.wait_ge(sums_done, 1)
                link(nc.vector.tensor_tensor(t0, var, rs, ALU.mult))
                link(nc.vector.tensor_tensor(t0, t0, pg.ps[:, 7, B:2 * B], ALU.mult))
                link(nc.vector.tensor_scalar(t0, t0, 2.0, None, ALU.mult))
                link(nc.vector.tensor_tensor(t0, t0, pg.ps[:, 7, 2 * B:3 * B], ALU.add))
                link(nc.vector.tensor_scalar(t0, t0, 1.0 / (float(HW) * NF), None, ALU.mult))
                link(nc.vector.tensor_tensor(v1, t0, tot, ALU.add))
                link(nc.vector.tensor_scalar(em, pg.ps[:, 7, 3 * B:4 * B], 1.0 / NF, None, ALU.mult))
                link(nc.vector.tensor_tensor(m1, mean, em, ALU.add))
                link(nc.vector.tensor_tensor(em, em, em, ALU.mult))
                link(nc.vector.tensor_tensor(v1, v1, em, ALU.subtract))
                signal(nc.vector.tensor_scalar(v1, v1, EPS, None, ALU.add), var_ready, 2)
                dve.wait_ge(root_done, 2)
                inv_root(t3, t1, v1)
                nc.vector.tensor_copy(st[:, :, 0], m1)
                nc.vector.tensor_copy(st[:, :, 1], t3)
                nc.vector.tensor_scalar(st[:, :, 2], t3, 1.0, None, ALU.add)
                link(nc.vector.tensor_scalar(t0, m1, float(HW), None, ALU.mult))
                nc.vector.tensor_tensor(s00, s00, t0[0:C], ALU.subtract)
                s00n = S[0:C, :, 0, 2, 0]
                signal(nc.vector.tensor_tensor(s00n, s00n, t0[0:C], ALU.add), s_final, 1)
                if base_out is not None:
                    link(nc.vector.tensor_tensor(t0, var, rs, ALU.mult))
                    for b in range(B):
                        op = nc.vector.scalar_tensor_tensor(X[:, b, :, 1:3, :], X[:, b, :, 1:3, :], t0[:, b:b + 1],
                                                            S[:, b, :, 0:2, :], ALU.mult, ALU.add)
                    link(op)
                    link(nc.vector.scalar_tensor_tensor(
                        X[:, :, :, 1:3, 0].rearrange("p b q r -> p (b q) r"),
                        S[:, :, :, 0:2, 0].rearrange("p b q r -> p (b q) r"), -0.5,
                        X[:, :, :, 1:3, 0].rearrange("p b q r -> p (b q) r"), ALU.mult, ALU.add))
                    link(nc.vector.scalar_tensor_tensor(x00, s00, 0.5, x00, ALU.mult, ALU.add))
                    link(nc.vector.tensor_scalar(t0, mean, float(HW), None, ALU.mult))
                    link(nc.vector.tensor_tensor(x00, x00, t0[0:C], ALU.add))
                    link(nc.vector.tensor_scalar(t2, t3, 1.0, None, ALU.add))
                    for b in range(B):
                        op = nc.vector.tensor_scalar(X[:, b, :, 1:3, :], X[:, b, :, 1:3, :], t2[:, b:b + 1], None,
                                                     ALU.mult)
                    link(op)
                    nc.vector.tensor_scalar(X[:, :, :, 0, :].rearrange("p b q m -> p (b q) m"),
                                            X[:, :, :, 2, :].rearrange("p b q m -> p (b q) m"), -1.0, None, ALU.mult
                                            ).then_inc(base_done, 1)

class Inverse:
    VB, YB = 2, 4
    NY = CU

    def __init__(self, pg, mem, name):
        nc = pg.nc
        self.pg = pg
        self.slot = [mem.enter_context(nc.sbuf_tensor(f"{name}_x{k}", [P, HB, CU, W], F32)) for k in range(KU)]
        self.sxs = [mem.enter_context(nc.sbuf_tensor(f"{name}_sx{k}", [2 * M, CU, 2 * M], F32)) for k in range(KU)]
        self.v = [mem.enter_context(nc.sbuf_tensor(f"{name}_v{i}", [P, CU // 2, W], F32)) for i in range(2)]
        self.loaded = [pg.sem(f"{name}_loaded{k}") for k in range(KU)]
        self.v_done = pg.sem(name + "_v_done")
        self.v_out = pg.sem(name + "_v_out")
        self.y_done = pg.sem(name + "_y_done")
        self.y_out = pg.sem(name + "_y_out")

    def load(self, sp, src, sx, s, k):
        for hb in range(HB):
            sp.dma_start(self.slot[k][:, hb], unit_rows(src, s, k, hb)).then_inc(self.loaded[k], 16)
        sp.dma_start(self.sxs[k][:, :, :].rearrange("p c m -> p (c m)"),
                     sx[bass.ds(s, 1), :, k * CU * 2 * M:(k + 1) * CU * 2 * M].rearrange("b p f -> p (b f)")
                     ).then_inc(self.loaded[k], 16)

    def pe_v(self, pe, s, k, loads):
        nc = self.pg.nc
        pe.wait_ge(self.loaded[k], s * (16 * loads) + 16 * loads)
        for n in range(2):
            pe.wait_ge(self.v_out, s * 8 + (2 * k + n + 1))
            for q in range(2):
                c = 4 * n + 2 * q
                mm = nc.tensor.matmul(self.pg.ps[:, n, q * W:(q + 1) * W],
                                      self.sxs[k][:, c:c + 2, :].rearrange("p c m -> p (c m)"),
                                      self.pg.t("EW", 2 * M), start=True, stop=True)
            mm.then_inc(self.v_done, 1)

    def act_v(self, act, s, k):
        nc = self.pg.nc
        self.pg.wait(act, self.y_done, s * 32 + (8 * k - 8))
        for n in range(2):
            act.wait_ge(self.v_done, s * 8 + (2 * k + n + 1))
            nc.scalar.copy(self.v[k % 2][:, 2 * n:2 * n + 2, :].rearrange("p q w -> p (q w)"), self.pg.ps[:, n]
                           ).then_inc(self.v_out, 1)

    @staticmethod
    def parts():
        return [(4 * n + 2 * e + hb, n, e, hb) for n in range(2) for e in range(2) for hb in range(HB)]

    def pe_y(self, pe, s, k, table, pairs=(0, 1)):
        nc = self.pg.nc
        for at, n, e, hb in self.parts():
            if n not in pairs:
                continue
            if e == 0 and hb == 0:
                pe.wait_ge(self.v_out, s * 8 + (2 * k + n + 1 + self.VB))
            pe.wait_ge(self.y_out, s * 32 + (8 * k + at + 1))
            nc.tensor.matmul(self.pg.ps[:, self.VB + at % self.YB], self.pg.t(f"{table}{e}")[:, hb * P:(hb + 1) * P],
                             self.v[k % 2][:, 2 * n:2 * n + 2, :].rearrange("p q w -> p (q w)"),
                             start=True, stop=True).then_inc(self.y_done, 1)

    def dve_y(self, dve, s, k, op, loads):
        nc = self.pg.nc
        dve.wait_ge(self.loaded[k], s * (16 * loads) + 16 * loads)
        for at, n, e, hb in self.parts():
            dve.wait_ge(self.y_done, s * 32 + (8 * k + at + 1))
            bank = self.pg.ps[:, self.VB + at % self.YB].rearrange("p (q w) -> p q w", q=2)
            xs = self.slot[k][:, hb, 4 * n + e:4 * n + e + 3:2, :]
            nc.vector.tensor_tensor(xs, bank, xs, op).then_inc(self.y_out, 1)


def ahead(s, k, n):
    return (s + (k + n) // KU, (k + n) % KU) if not 0 <= k + n < KU else (s, k + n)


def phase_wavelet(pg, x, sx, stats, x2, modes, sumsq):
    nc = pg.nc
    LOADS = 4
    Q, Q2, Q3 = W // 2, W // 4, W // 8
    with ExitStack() as mem:
        def sb(n, shape):
            return mem.enter_context(nc.sbuf_tensor("b_" + n, shape, F32))
        iv = Inverse(pg, mem, "b")
        fw = Forward(pg, mem, "bf", 1, 1, (7,), (7,), 7, pg.ps[96:97, 6, 0:C // GROUP])
        stt = [sb(f"st{k}", [P, 4, CU]) for k in range(KU)]
        odd = sb("odd", [P, HB, CU, Q])
        f1 = sb("f1", [P, HB * CU, Q + 1])
        f2 = sb("f2", [P, HB * CU, Q2 + 1])
        f3 = sb("f3", [P, HB * CU, Q3])
        down = [sb(f"down{i}", [P, CU, Q]) for i in range(2)]
        zero_cols = pg.sem("b_zero_cols")
        odd_done = pg.sem("b_odd_done")
        f1_done, f2_done, f3_done = (pg.sem("b_" + n) for n in ("f1_done", "f2_done", "f3_done"))
        d_done = pg.sem("b_d_done")
        d_out = pg.sem("b_d_out")
        scaled = pg.sem("b_scaled")
        d_diff = pg.sem("b_d_diff")
        x2_done = pg.sem("b_x2_done")
        x2_out = [pg.sem(f"b_x2_out{k}") for k in range(KU)]
        R = [iv.slot[k] for k in range(KU)]

        with nc.Block(name="wavelet") as block:
            @block.sync
            def _(sp):
                def load(s, k):
                    iv.load(sp, x, sx, s, k)
                    sp.dma_start(stt[k][:, :, :], stats[bass.ds(s, 1), :, k * CU:(k + 1) * CU].to_broadcast(
                        [P, 4, CU])).then_inc(iv.loaded[k], 16)

                def body(s, last=False):
                    for k in range(KU):
                        pg.hold(sp, x2_done, s * KU + (k + 1))
                        for hb in range(HB):
                            sp.dma_start(unit_rows(x2, s, k, hb), iv.slot[k][:, hb]).then_inc(x2_out[k], 16)
                        if last:
                            continue
                        pg.hold(sp, x2_out[k], s * 32 + 32)
                        pg.hold(sp, fw.sq_done, fw.sq_count(s, k))
                        load(s + 1, k)
                for k in range(KU):
                    load(0, k)
                with sp.Fori(0, B - 1) as s:
                    body(s)
                body(B - 1, last=True)
                for k in range(KU):
                    pg.hold(sp, x2_out[k], B * 32)

            @block.tensor
            def _(pe):
                f1v = f1[:, :, 1:Q + 1].rearrange("p (n c) w -> p n c w", n=HB)
                f2v = f2[:, :, 1:Q2 + 1].rearrange("p (n c) w -> p n c w", n=HB)
                f3v = f3[:, :, :].rearrange("p (n c) w -> p n c w", n=HB)
                d1 = pg.t("D1").rearrange("p (n m) -> p n m", n=HB)
                d2 = pg.t("D2").rearrange("p (n m) -> p n m", n=HB)
                d3 = pg.t("D3").rearrange("p (n m) -> p n m", n=HB)

                def pyramid(s, k, more):
                    pe.wait_ge(f1_done, s * KU + (k + 1))
                    if more:
                        pe.wait_ge(iv.y_out, s * 32 + (8 * k + 16 + iv.YB))
                    pg.wait(pe, d_out, s * KU + k)
                    for half in range(2):
                        bank = pg.ps[:, 4 + half].rearrange("p (c w) -> p c w", c=4)
                        for hb in range(HB):
                            mm = nc.tensor.matmul(bank, d1[:, hb, :], f1v[:, hb, 4 * half:4 * half + 4, :],
                                                  start=(hb == 0), stop=(hb == HB - 1))
                        mm.then_inc(d_done, 1)
                    pe.wait_ge(f2_done, s * KU + (k + 1))
                    pe.wait_ge(f3_done, s * KU + (k + 1))
                    for bank, dm, f, n in ((pg.ps[0:64, 6], d2, f2v, Q2), (pg.ps[64:96, 6], d3, f3v, Q3)):
                        out = bank[:, 0:CU * n].rearrange("p (c w) -> p c w", c=CU)
                        for hb in range(HB):
                            mm = nc.tensor.matmul(out, dm[:, hb, :], f[:, hb, :, :], start=(hb == 0), stop=(hb == HB - 1))
                        mm.then_inc(d_done, 1)

                def body(s, first=False, last=False):
                    for k in range(KU):
                        more = not (last and k == KU - 1)
                        if more:
                            pg.wait(pe, d_out, s * KU + k)
                            iv.pe_y(pe, *ahead(s, k, 1), "EH")
                        if not (first and k == 0):
                            pe.wait_ge(d_diff, s * KU + k)
                            fw.pe_rows(pe, *ahead(s, k, -1), lambda hb: down[(k + 1) % 2][:, :, :])
                        pyramid(s, k, more)
                        if not (last and k + 2 >= KU):
                            iv.pe_v(pe, *ahead(s, k, 2), LOADS)
                        if not (first and k == 0):
                            fw.pe_turn(pe, *ahead(s, k, -1))
                        if k == 0 and not first:
                            fw.pe_modes(pe, s - 1)
                            fw.pe_sums(pe, s - 1)
                pe.sem_inc(fw.modes_done, 1)
                iv.pe_v(pe, 0, 0, LOADS)
                iv.pe_y(pe, 0, 0, "EH")
                iv.pe_v(pe, 0, 1, LOADS)
                body(0, first=True)
                with pe.Fori(1, B - 1) as s:
                    body(s)
                body(B - 1, last=True)
                pe.wait_ge(d_diff, B * KU)
                fw.pe_rows(pe, B - 1, KU - 1, lambda hb: down[(KU - 1) % 2][:, :, :])
                fw.pe_turn(pe, B - 1, KU - 1)
                fw.pe_sums(pe, B - 1)
                fw.pe_modes(pe, B - 1)

            @block.scalar
            def _(act):
                act.sem_inc(iv.v_out, iv.VB)
                fw.start(act)

                def copy_down(s, k):
                    dn = down[k % 2]
                    pg.wait(act, x2_done, s * KU + (k - 1))
                    pg.wait(act, fw.rows_done, s * KU + (k - 1))
                    n = s * (4 * KU) + 4 * k
                    act.wait_ge(d_done, n + 2)
                    for half in range(2):
                        bank = pg.ps[:, 4 + half].rearrange("p (c w) -> p c w", c=4)
                        cs = slice(4 * half, 4 * half + 4)
                        nc.scalar.copy(dn[64:P, cs, :], bank[64:P])
                        nc.scalar.copy(dn[0:64, cs, Q2:Q], bank[0:64, :, Q2:Q])
                    act.wait_ge(d_done, n + 4)
                    b2 = pg.ps[0:64, 6].rearrange("p (c w) -> p c w", c=CU)
                    b3 = pg.ps[64:96, 6, 0:CU * Q3].rearrange("p (c w) -> p c w", c=CU)
                    nc.scalar.copy(dn[32:64, :, 0:Q2], b2[32:64])
                    nc.scalar.copy(dn[0:32, :, Q3:Q2], b2[0:32, :, Q3:Q2])
                    nc.scalar.copy(dn[0:32, :, 0:Q3], b3).then_inc(d_out, 1)

                def scale(s, k):
                    act.wait_ge(d_diff, s * KU + (k + 1))
                    for g in range(CU // GROUP):
                        xg = R[k][:, :, g * GROUP:(g + 1) * GROUP, :].rearrange("p n c w -> p n (c w)")
                        c = g * GROUP
                        op = nc.scalar.activation(xg, xg, ACT.Identity, scale=stt[k][:, 2, c:c + 1],
                                                  bias=stt[k][:, 0, c:c + 1])
                    op.then_inc(scaled, 1)

                def squares(s, k):
                    act.wait_ge(x2_done, s * KU + (k + 1))
                    fw.act_squares(act, s, k, R[k])

                def body(s, first=False, last=False):
                    for k in range(KU):
                        prev = ahead(s, k, -1)
                        behind = not (first and k == 0)
                        if behind:
                            scale(*prev)
                            fw.act_rows(act, *prev)
                        copy_down(s, k)
                        if not (last and k + 2 >= KU):
                            iv.act_v(act, *ahead(s, k, 2))
                        if behind:
                            fw.act_turn(act, *prev)
                            squares(*prev)
                iv.act_v(act, 0, 0)
                iv.act_v(act, 0, 1)
                body(0, first=True)
                with act.Fori(1, B - 1) as s:
                    body(s)
                body(B - 1, last=True)
                scale(B - 1, KU - 1)
                fw.act_rows(act, B - 1, KU - 1)
                fw.act_turn(act, B - 1, KU - 1)
                squares(B - 1, KU - 1)

            @block.vector
            def _(dve):
                dve.sem_inc(iv.y_out, iv.YB)
                dve.sem_inc(fw.modes_out, 1)
                nc.vector.memset(f1[:, :, 0:1], 0.0)
                nc.vector.memset(f2[:, :, 0:1], 0.0).then_inc(zero_cols, 1)
                dve.wait_ge(zero_cols, 1)

                def filters(s, k):
                    u1 = s * KU + (k + 1)
                    xr = R[k]
                    dve.wait_ge(iv.y_out, s * 32 + (8 * k + 8 + iv.YB))
                    nc.vector.tensor_tensor(odd[:, :, :, 1:Q], xr[:, :, :, 1:W - 2:2], xr[:, :, :, 3:W:2], ALU.add)
                    nc.vector.tensor_copy(odd[:, :, :, 0:1], xr[:, :, :, 1:2]).then_inc(odd_done, 1)
                    dve.wait_ge(odd_done, s * (3 * KU) + (3 * k + 1))
                    dn = s * (4 * KU) + 4 * k
                    pg.wait(dve, d_done, dn - 2)
                    nc.vector.scalar_tensor_tensor(
                        f1[:, :, 1:Q + 1], xr[:, :, :, 0:W:2].rearrange("p n c w -> p (n c) w"), 2.0,
                        odd[:, :, :, :].rearrange("p n c w -> p (n c) w"), ALU.mult, ALU.add).then_inc(f1_done, 1)
                    dve.wait_ge(f1_done, u1)
                    o2 = odd[:, :, :, 0:Q2].rearrange("p n c w -> p (n c) w")
                    nc.vector.tensor_tensor(o2, f1[:, :, 0:Q - 1:2], f1[:, :, 2:Q + 1:2], ALU.add).then_inc(odd_done, 1)
                    dve.wait_ge(odd_done, s * (3 * KU) + (3 * k + 2))
                    pg.wait(dve, d_done, dn - 1)
                    nc.vector.scalar_tensor_tensor(f2[:, :, 1:Q2 + 1], f1[:, :, 1:Q:2], 2.0, o2, ALU.mult, ALU.add
                                                   ).then_inc(f2_done, 1)
                    dve.wait_ge(f2_done, u1)
                    o3 = odd[:, :, :, 0:Q3].rearrange("p n c w -> p (n c) w")
                    nc.vector.tensor_tensor(o3, f2[:, :, 0:Q2 - 1:2], f2[:, :, 2:Q2 + 1:2], ALU.add).then_inc(odd_done, 1)
                    dve.wait_ge(odd_done, s * (3 * KU) + (3 * k + 3))
                    pg.wait(dve, d_done, dn)
                    nc.vector.scalar_tensor_tensor(f3[:, :, :], f2[:, :, 1:Q2:2], 2.0, o3, ALU.mult, ALU.add
                                                   ).then_inc(f3_done, 1)

                def less_x1(s, k):
                    dve.wait_ge(d_out, s * KU + (k + 1))
                    dn = down[k % 2]
                    nc.vector.tensor_tensor(dn[:, :, :], dn[:, :, :], R[k][:, 0, :, 0:Q], ALU.subtract
                                            ).then_inc(d_diff, 1)

                def finish(s, k):
                    u1 = s * KU + (k + 1)
                    quad = R[k][:, 0, :, 0:Q]
                    dn = down[k % 2]
                    dve.wait_ge(d_diff, u1)
                    dve.wait_ge(scaled, u1)
                    for g in range(CU // GROUP):
                        cs = slice(g * GROUP, (g + 1) * GROUP)
                        op = nc.vector.scalar_tensor_tensor(quad[:, cs], dn[:, cs], stt[k][:, 1, g * GROUP:g * GROUP + 1],
                                                            quad[:, cs], ALU.mult, ALU.add)
                    op.then_inc(x2_done, 1)

                def body(s, first=False, last=False):
                    for k in range(KU):
                        more = not (last and k == KU - 1)
                        if k == 1 and not first:
                            fw.dve_sample(dve, s - 1)
                        if more:
                            iv.dve_y(dve, *ahead(s, k, 1), ALU.add, LOADS)
                        if not (first and k == 0):
                            finish(*ahead(s, k, -1))
                        if more:
                            filters(*ahead(s, k, 1))
                        less_x1(s, k)
                iv.dve_y(dve, 0, 0, ALU.add, LOADS)
                filters(0, 0)
                body(0, first=True)
                with dve.Fori(1, B - 1) as s:
                    body(s)
                body(B - 1, last=True)
                finish(B - 1, KU - 1)
                fw.dve_sample(dve, B - 1)

            @block.gpsimd
            def _(pool):
                pool.sem_inc(fw.xf_free, 1)
                with pool.Fori(0, B) as s:
                    fw.pool_sample(pool, s, modes, sumsq)
                pool.wait_ge(fw.stored, B * 32)


def phase_inverse(pg, x2, sx, nx):
    nc = pg.nc
    LOADS = 3
    with ExitStack() as mem:
        iv = Inverse(pg, mem, "c")
        stored = [pg.sem(f"c_stored{k}") for k in range(KU)]
        with nc.Block(name="inverse") as block:
            @block.sync
            def _(sp):
                for k in range(KU):
                    iv.load(sp, x2, sx, 0, k)
                with sp.Fori(0, B - 1) as s:
                    for k in range(KU):
                        pg.hold(sp, stored[k], s * 32 + 32)
                        iv.load(sp, x2, sx, s + 1, k)
                for k in range(KU):
                    pg.hold(sp, stored[k], B * 32)

            @block.tensor
            def _(pe):
                iv.pe_v(pe, 0, 0, LOADS)

                def body(s, last=False):
                    for k in range(KU):
                        iv.pe_y(pe, s, k, "EN", (0,))
                        if not (last and k == KU - 1):
                            iv.pe_v(pe, *ahead(s, k, 1), LOADS)
                        iv.pe_y(pe, s, k, "EN", (1,))
                with pe.Fori(0, B - 1) as s:
                    body(s)
                body(B - 1, last=True)

            @block.scalar
            def _(act):
                act.sem_inc(iv.v_out, iv.VB)

                def body(s, last=False):
                    for k in range(KU):
                        if not (last and k == KU - 1):
                            iv.act_v(act, *ahead(s, k, 1))
                        pg.hold(act, iv.y_out, s * 32 + (8 * k + 8 + iv.YB))
                        for hb in range(HB):
                            act.dma_start(unit_rows(nx, s, k, hb), iv.slot[k][:, hb]).then_inc(stored[k], 16)
                iv.act_v(act, 0, 0)
                body(0)
                with act.Fori(1, B - 1) as s:
                    body(s)
                body(B - 1, last=True)

            @block.vector
            def _(dve):
                dve.sem_inc(iv.y_out, iv.YB)
                with dve.Fori(0, B) as s:
                    for k in range(KU):
                        iv.dve_y(dve, s, k, ALU.subtract, LOADS)


def phase_scans(pg, name, nx, gates_v, gates_h, stats, out, part=None):
    nc = pg.nc
    final = part is not None
    NB = H // RF
    F = RF * W
    XR = 4 if final else 2

    def grouped(a):
        return a.rearrange("b c h w -> (b c) (h w)").rearrange("(g p) f -> p g f", p=P)
    nxr, outr = grouped(nx), grouped(out)
    partr = grouped(part) if final else None
    wv, wh = (2, 1) if final else (3, 0)
    rev = final
    body = slice(0, W - 1) if rev else slice(1, W)
    start = slice(W - 2, W - 1) if rev else slice(1, 2)
    order = list(range(RF)) if final else list(range(RF))[::-1]

    def flat(n, rows_on=0):
        return bass.ds(n * F + rows_on * W, F) if final else bass.ds(n * (-F) + (H * W - F + rows_on * W), F)
    with ExitStack() as mem:
        def sb(n, shape):
            return mem.enter_context(nc.sbuf_tensor(name + n, shape, F32))

        def sb2(n, shape):
            return [sb(f"{n}{i}", shape) for i in range(2)]
        xin = [sb(f"_x{i}", [P, GB, RF, W]) for i in range(XR)]
        u, cu, ncx, dx, z = (sb2(n, [P, GB, RF, W]) for n in ("_u", "_cu", "_ncx", "_dx", "_z"))
        pt = sb2("_part", [P, GB, RF, W]) if final else None
        gate = sb2("_g", [P, 2, RF, W])
        carry = sb("_carry", [P, GB, W])
        wt = sb("_wt", [P, GB, 3, P])
        sts = sb("_sts", [P, GB, 4])
        sts_in = pg.sem(name + "_sts_in")
        wt_done = pg.sem(name + "_wt_done")
        x_in = [pg.sem(f"{name}_x_in{i}") for i in range(XR)]
        g_in = [pg.sem(f"{name}_g_in{i}") for i in range(2)]
        part_in = [pg.sem(f"{name}_part_in{i}") for i in range(2)] if final else None
        carried, rows = pg.sem(name + "_carried"), pg.sem(name + "_rows")
        lined = pg.sem(name + "_lined")
        scans_done = pg.sem(name + "_scans_done")
        clamped = pg.sem(name + "_clamped")
        mixed = pg.sem(name + "_mixed")
        z_done = pg.sem(name + "_z_done")
        summed = pg.sem(name + "_summed") if final else None
        stored = [pg.sem(f"{name}_stored{i}") for i in range(2)]

        with nc.Block(name=name) as block:
            @block.sync
            def _(sp):
                def load_x(n, j):
                    sp.dma_start(xin[j][:].rearrange("p g r w -> p g (r w)"), nxr[:, :, flat(n)]).then_inc(x_in[j], 16)

                def load_gates(n, i):
                    for d, src, on in ((0, gates_v, 0 if final else 1), (1, gates_h, 0)):
                        sp.dma_start(gate[i][:, d].rearrange("p r w -> p (r w)"),
                                     src.rearrange("h w -> (h w)").unsqueeze(0)[:, flat(n, on)].to_broadcast([P, F])
                                     ).then_inc(g_in[i], 16)

                def load_part(n, i):
                    sp.dma_start(pt[i][:].rearrange("p g r w -> p g (r w)"), partr[:, :, flat(n)]).then_inc(part_in[i], 16)

                def step(n, j, last=False, x_more=True):
                    i = j % 2
                    if not last:
                        pg.hold(sp, scans_done, n + 1)
                        load_gates(n + 2, i)
                        if final:
                            pg.hold(sp, mixed, n * GB + GB)
                            load_part(n + 2, i)
                        elif x_more:
                            load_x(n + XR, j)
                    if final:
                        pg.hold(sp, summed, n + 1)
                    else:
                        pg.hold(sp, z_done, n * GB + GB)
                    sp.dma_start(outr[:, :, flat(n)], z[i][:].rearrange("p g r w -> p g (r w)")).then_inc(stored[i], 16)
                    if final and x_more:
                        load_x(n + XR, j)

                for j in range(XR):
                    load_x(j, j)
                for i in range(2):
                    load_gates(i, i)
                    if final:
                        load_part(i, i)
                with sp.Fori(0, NB // XR - 1) as it:
                    n = it * XR
                    for j in range(XR):
                        step(n + j, j)
                for j in range(XR):
                    step(NB - XR + j, j, last=j >= XR - 2, x_more=False)
                for i in range(2):
                    pg.hold(sp, stored[i], 16 * (NB // 2))

            @block.vector
            def _(dve):
                def vertical(n, j, first):
                    i = j % 2
                    for a, r in enumerate(order):
                        at = n * RF + a
                        if first and a == 0:
                            nc.vector.tensor_scalar(u[i][:, :, r, :], xin[j][:, :, r, :], -1.0, None, ALU.mult
                                                    ).then_inc(rows, 1)
                            nc.vector.memset(carry[:, 0, 0:1], 0.0).then_inc(carried, 1)
                            dve.wait_ge(carried, 1)
                            continue
                        dve.wait_ge(rows, at)
                        prev = u[i][:, :, order[a - 1], :] if a else u[1 - i][:, :, order[-1], :]
                        g = gate[i][:, 0, r, :].unsqueeze(1).to_broadcast([P, GB, W])
                        if first and a == 1:
                            op = nc.vector.tensor_tensor(carry[:], prev, g, ALU.mult)
                        else:
                            op = nc.vector.scalar_tensor_tensor(carry[:], prev, 0.0, g, ALU.max, ALU.mult)
                        op.then_inc(carried, 1)
                        dve.wait_ge(carried, at + 1)
                        nc.vector.tensor_tensor(u[i][:, :, r, :], carry[:], xin[j][:, :, r, :], ALU.subtract
                                                ).then_inc(rows, 1)

                def line(t, g, back=False):
                    a = t[:, g].rearrange("p r w -> p (r w)")
                    return a[:, ::-1] if back else a

                def step(n, it, j, first=False):
                    i = j % 2
                    dve.wait_ge(x_in[j], it * 16 + 16)
                    dve.wait_ge(g_in[i], it * (16 * XR) + (32 * (j // 2) + 32))
                    pg.wait(dve, clamped, n - 1)
                    vertical(n, j, first)
                    pg.wait(dve, mixed, n * GB - GB)
                    for g in range(GB):
                        op = nc.vector.tensor_tensor_scan(line(ncx[i], g, rev), line(gate[i], 1, rev),
                                                          line(xin[j], g, rev), 0.0, ALU.mult, ALU.add)
                    op.then_inc(lined, 1)
                    dve.wait_ge(lined, n * 2 + 1)
                    nc.vector.memset(gate[i][:, 1, :, start], 0.0).then_inc(lined, 1)
                    dve.wait_ge(lined, n * 2 + 2)
                    for g in range(GB):
                        op = nc.vector.tensor_tensor_scan(line(dx[i], g, rev), line(gate[i], 1, rev),
                                                          line(ncx[i], g, rev), 0.0, ALU.mult, ALU.max)
                    op.then_inc(scans_done, 1)
                    if final and not first:
                        sums(n - 1, (j - 1) % XR, first=isinstance(n, int) and n == 1)

                def sums(n, j, first=False):
                    if first:
                        dve.wait_ge(sts_in, 4 * GB * 16)
                    for g in range(GB):
                        dve.wait_ge(z_done, n * GB + (g + 1))
                        zg = line(z[j % 2], g)
                        op = nc.vector.scalar_tensor_tensor(zg, zg, sts[:, g, 0:1], line(xin[j], g), ALU.add, ALU.subtract)
                    op.then_inc(summed, 1)

                for j in range(XR):
                    step(j, 0, j, first=(j == 0))
                with dve.Fori(1, NB // XR) as it:
                    n = it * XR
                    for j in range(XR):
                        step(n + j, it, j)
                if final:
                    sums(NB - 1, XR - 1)

            @block.tensor
            def _(pe):
                pe.wait_ge(wt_done, 2)

                def mix(n, i, half):
                    def flat_of(t, g):
                        return t[i][:, g].rearrange("p r w -> p (r w)")
                    for g in range(GB):
                        bank = pg.ps[:, i * GB + g]
                        if final:
                            if g == 0:
                                pe.wait_ge(part_in[i], half * 16 + 16)
                            nc.tensor.matmul(bank, pg.t("ID"), flat_of(pt, g), start=True, stop=False)
                        if g == 0:
                            pe.wait_ge(clamped, n + 1)
                        nc.tensor.matmul(bank, wt[:, g, 0, :], flat_of(cu, g), start=not final, stop=False)
                        if g == 0:
                            pe.wait_ge(scans_done, n + 1)
                        nc.tensor.matmul(bank, wt[:, g, 2, :], flat_of(ncx, g), start=False, stop=False)
                        grid = bank.rearrange("p (r w) -> p r w", r=RF)
                        nc.tensor.matmul(grid[:, :, body], wt[:, g, 1, :], dx[i][:, g, :, body], start=False, stop=True
                                         ).then_inc(mixed, 1)

                mix(0, 0, 0)
                mix(1, 1, 0)
                with pe.Fori(1, NB // 2) as half:
                    n = half * 2
                    for i in range(2):
                        pe.wait_ge(z_done, (n + i) * GB - GB)
                        mix(n + i, i, half)

            @block.scalar
            def _(act):
                def clamp(n, i, first=False):
                    act.wait_ge(rows, n * RF + RF)
                    if not first:
                        act.wait_ge(mixed, n * GB - GB)
                    if first:
                        r0 = order[0]
                        others = slice(1, RF) if r0 == 0 else slice(0, RF - 1)
                        nc.scalar.copy(cu[i][:, :, r0, :], u[i][:, :, r0, :])
                        op = nc.scalar.activation(cu[i][:, :, others, :], u[i][:, :, others, :], ACT.Relu)
                    else:
                        op = nc.scalar.activation(cu[i][:].rearrange("p g r w -> p (g r w)"),
                                                  u[i][:].rearrange("p g r w -> p (g r w)"), ACT.Relu)
                    op.then_inc(clamped, 1)

                def take(n, i, half):
                    act.wait_ge(stored[i], half * 16)
                    for g in range(GB):
                        act.wait_ge(mixed, n * GB + (g + 1))
                        zg, bank = z[i][:, g].rearrange("p r w -> p (r w)"), pg.ps[:, i * GB + g]
                        if final:
                            op = nc.scalar.activation(zg, bank, ACT.Relu, bias=pg.conv_b[:, :])
                        else:
                            op = nc.scalar.copy(zg, bank)
                        op.then_inc(z_done, 1)
                with nc.allow_non_contiguous_dma(reason="a few words per channel"):
                    for g in range(GB):
                        for b in range(4):
                            act.dma_start(sts[b * C:(b + 1) * C, g, :],
                                          stats[4 * g + b].rearrange("k c -> c k")).then_inc(sts_in, 16)
                act.wait_ge(sts_in, 4 * GB * 16)
                for g in range(GB):
                    for n, w in ((0, wv), (1, wh)):
                        op = nc.scalar.activation(wt[:, g, n, :], pg.conv_w[:, w, :], ACT.Identity, scale=sts[:, g, 1:2])
                op.then_inc(wt_done, 1)
                act.wait_ge(wt_done, 1)
                for g in range(GB):
                    op = nc.scalar.mul(wt[:, g, 2, :], wt[:, g, 1, :], -1.0)
                op.then_inc(wt_done, 1)
                clamp(0, 0, first=True)
                clamp(1, 1)
                take(0, 0, 0)
                with act.Fori(1, NB // 2) as half:
                    n = half * 2
                    clamp(n, 0)
                    take(n - 1, 1, half - 1)
                    clamp(n + 1, 1)
                    take(n, 0, half)
                take(NB - 1, 1, NB // 2 - 1)


def build(nc, ins, outs):
    x, cr0, ci0, pj0, cr2, ci2, pj2, weights, conv_w, conv_b, consts = ins
    out, = outs

    def scratch(name, shape):
        return nc.dram_tensor(name, shape, F32, kind="Internal").ap()
    with ExitStack() as ctx:
        pg = Prog(nc, ctx)
        gate_rows = scratch("s_gate_rows", [2, H + 1, W])
        gate_cols = scratch("s_gate_cols", [2, H, W])
        modes = scratch("s_modes", [B, P, XF])
        base = scratch("s_base", [B, P, XF])
        sumsq = scratch("s_sumsq", [B, C])
        sx = scratch("s_sx", [B, 2 * M, C * 2 * M])
        stats1, stats3 = scratch("s_stats1", [B, 4, C]), scratch("s_stats3", [B, 4, C])
        x2, nx, part = (scratch(n, [B, C, H, W]) for n in ("s_x2", "s_nx", "s_part"))
        phase_gates(pg, consts, conv_w, conv_b, weights, gate_rows, gate_cols)
        phase_forward(pg, x, modes, sumsq)
        phase_mix(pg, "m0", modes, sumsq, (cr0, ci0), pj0, sx, stats1, base_out=base)
        phase_wavelet(pg, x, sx, stats1, x2, modes, sumsq)
        phase_mix(pg, "m2", modes, sumsq, (cr2, ci2), pj2, sx, stats3, prior=(base, stats1))
        phase_inverse(pg, x2, sx, nx)
        phase_scans(pg, "d", nx, gate_rows[1], gate_cols[0], stats3, part)
        phase_scans(pg, "e", nx, gate_rows[0], gate_cols[1], stats3, out, part)


def kernel(**inputs):
    import concourse.bacc as bacc
    from concourse.bass_utils import run_bass_kernel_spmd as run

    nc = bacc.Bacc("TRN2", target_bir_lowering=False, num_devices=1)
    names = ["x", "L0_conv_coeff_real", "L0_conv_coeff_imag", "L0_conv_proj", "L2_conv_coeff_real",
             "L2_conv_coeff_imag", "L2_conv_proj", "L3_conv_weights"]
    data = {n: np.ascontiguousarray(inputs[n]) for n in names}
    for n in ("L0_conv_proj", "L2_conv_proj"):
        data[n] = np.ascontiguousarray(data[n].T)
    for n in names:
        if "coeff" in n:
            data[n] = np.ascontiguousarray(data[n].reshape(C, C, MQ, 4, M).transpose(2, 3, 1, 0, 4)
                                           .reshape(MQ, P, C * M))
    cw = np.asarray(inputs["L3_conv_conv_w"])
    blocks = np.zeros((P, 4, P), cw.dtype)
    for d in range(4):
        for b in range(P // C):
            blocks[b * C:(b + 1) * C, d, b * C:(b + 1) * C] = cw[:, d * C:(d + 1) * C].T
    data["L3_conv_conv_w"] = blocks
    data["L3_conv_conv_b"] = np.tile(np.asarray(inputs["L3_conv_conv_b"]), P // C).reshape(P, 1)
    data["consts"] = constant_table()
    arrays, ins = {}, []
    for n, a in data.items():
        arrays["in_" + n] = a
        ins.append(nc.dram_tensor("in_" + n, a.shape, F32, kind="ExternalInput").ap())
    out = nc.dram_tensor("out_0", (B, C, H, W), F32, kind="ExternalOutput").ap()
    build(nc, ins, [out])
    r = run(nc, [arrays], core_ids=[0])
    return r.results[0]["out_0"]
```
